# Optimizing a Trainium2 kernel written in Bass

```python
import numpy as np
import jax
import jax.numpy as jnp

def _softmax(x, axis=-1):
    return jax.nn.softmax(x, axis=axis)

def _gelu(x):
    return jax.nn.gelu(x, approximate=True)

def _silu(x):
    return jax.nn.silu(x)

def _sigmoid(x):
    return jax.nn.sigmoid(x)

def _layernorm(x, axis=-1, eps=1e-05):
    m = jnp.mean(x, axis=axis, keepdims=True)
    v = jnp.var(x, axis=axis, keepdims=True)
    return (x - m) / jnp.sqrt(v + eps)

def _scatter_add(tgt, idx, src, axis=0):
    return tgt.at[idx].add(src)

def _segment_sum(src, seg, n):
    return jax.ops.segment_sum(src, seg, n)
kernel_name = 'mk_gnn_resnorm_d4_gnn_r8_6b422c'

def setup_inputs(seed: int=0):
    np.random.seed(seed)
    _w = jnp.asarray

    def _rec_inputs():
        import jax
        import jax.numpy as jnp
        _gk = jax.random.key(seed)
        x = -0.0005121 + 1.001 * jax.random.normal(jax.random.fold_in(_gk, 1), (6250, 64), jnp.float32)
        src = jax.random.randint(jax.random.fold_in(_gk, 2), (200000,), 0, 6250, jnp.int32)
        dst = jnp.minimum((6250 * jax.random.uniform(jax.random.fold_in(_gk, 3), (200000,)) ** 2.0).astype(jnp.int32), 49999)
        _o = jnp.argsort(dst, stable=True)
        src = src[_o]
        dst = dst[_o]
        edge_attr_3 = jax.random.uniform(jax.random.fold_in(_gk, 11), (200000, 3), jnp.float32, 0.0, 0.999999)
        edge_attr_32 = 0.000283511 + 1.00007 * jax.random.normal(jax.random.fold_in(_gk, 12), (200000, 32), jnp.float32)
        edge_attr_5 = jax.random.uniform(jax.random.fold_in(_gk, 13), (200000, 5), jnp.float32, 0.0, 1)
        edge_weight = jax.random.uniform(jax.random.fold_in(_gk, 15), (200000,), jnp.float32, 0.0, 0.999998)
        return (x, src, dst, edge_attr_3, edge_attr_32, edge_attr_5, edge_weight)
    x, src, dst, edge_attr_3, edge_attr_32, edge_attr_5, edge_weight = _rec_inputs()

    def _L0_gnn_setup():
        import jax, jax.numpy as jnp
        import numpy as np
        N_NODES = 6250
        N_EDGES = 125000
        C_FEAT = 64
        key = jax.random.key(seed)
        k1, k2, k3 = jax.random.split(key, 3)
        x = jax.random.normal(k1, (N_NODES, C_FEAT), dtype=jnp.float32)
        g = jax.random.randint(k2, (2, N_EDGES), 0, N_NODES, dtype=jnp.int64)
        ew = jax.random.uniform(k3, (N_EDGES,), dtype=jnp.float32)
        return {'x': x, 'g': g, 'ew': ew}
    _L0_gnn_all = _L0_gnn_setup()
    _L0_gnn_in = {k: v for k, v in _L0_gnn_all.items() if k in ()}
    del _L0_gnn_all

    def _L1_gnn_setup():
        import jax, jax.numpy as jnp
        import numpy as np
        EMB = 64
        HEADS = 2
        NUM_BOND = 5
        NEG_SLOPE = 0.2
        key = jax.random.key(seed)
        ks = jax.random.split(key, 9)
        N, E = (6250, 100000)
        x = jax.random.normal(ks[0], (N, EMB), dtype=jnp.float32)
        edge_index = jax.random.randint(ks[1], (2, E), 0, N, dtype=jnp.int64)
        edge_attr = jax.random.uniform(ks[2], (E, NUM_BOND), dtype=jnp.float32)
        W_lin = jax.random.normal(ks[3], (EMB, HEADS * EMB), dtype=jnp.float32) / np.sqrt(EMB)
        b_lin = jnp.zeros((HEADS * EMB,), dtype=jnp.float32)
        W_edge = jax.random.normal(ks[4], (NUM_BOND, HEADS * EMB), dtype=jnp.float32) / np.sqrt(NUM_BOND)
        b_edge = jnp.zeros((HEADS * EMB,), dtype=jnp.float32)
        att = jax.random.normal(ks[5], (1, HEADS, 2 * EMB), dtype=jnp.float32) / np.sqrt(2 * EMB)
        bias = jnp.zeros((EMB,), dtype=jnp.float32)
        return {'x': x, 'edge_index': edge_index, 'edge_attr': edge_attr, 'W_lin': W_lin, 'b_lin': b_lin, 'W_edge': W_edge, 'b_edge': b_edge, 'att': att, 'bias': bias}
    _L1_gnn_all = _L1_gnn_setup()
    _L1_gnn_in = {k: v for k, v in _L1_gnn_all.items() if k in ('W_lin', 'b_lin', 'W_edge', 'b_edge', 'att', 'bias')}
    del _L1_gnn_all

    def _L2_gnn_setup():
        import math
        import jax, jax.numpy as jnp
        import numpy as np
        N_NODES = 6250
        N_EDGES = 75000
        IN_CH = 64
        HEADS = 2
        C = 64
        HC = HEADS * C
        EDGE_DIM = 32

        def _layernorm(x, g, b, eps=1e-05):
            m = jnp.mean(x, axis=-1, keepdims=True)
            v = jnp.mean(jnp.square(x - m), axis=-1, keepdims=True)
            return (x - m) / jnp.sqrt(v + eps) * g + b
        key = jax.random.key(seed)
        ks = jax.random.split(key, 12)
        s = 0.05
        return {'x': jax.random.normal(ks[0], (N_NODES, IN_CH), jnp.float32), 'edge_index': jax.random.randint(ks[1], (2, N_EDGES), 0, N_NODES, dtype=jnp.int64), 'edge_attr': jax.random.normal(ks[2], (N_EDGES, EDGE_DIM), jnp.float32), 'Wq': s * jax.random.normal(ks[3], (IN_CH, HC), jnp.float32), 'bq': jnp.zeros((HC,), jnp.float32), 'Wk': s * jax.random.normal(ks[4], (IN_CH, HC), jnp.float32), 'bk': jnp.zeros((HC,), jnp.float32), 'Wv': s * jax.random.normal(ks[5], (IN_CH, HC), jnp.float32), 'bv': jnp.zeros((HC,), jnp.float32), 'We': s * jax.random.normal(ks[6], (EDGE_DIM, HC), jnp.float32), 'Wp': s * jax.random.normal(ks[7], (HC, IN_CH), jnp.float32), 'bp': jnp.zeros((IN_CH,), jnp.float32), 'ln1_g': jnp.ones((IN_CH,), jnp.float32), 'ln1_b': jnp.zeros((IN_CH,), jnp.float32), 'ln2_g': jnp.ones((IN_CH,), jnp.float32), 'ln2_b': jnp.zeros((IN_CH,), jnp.float32), 'W1': s * jax.random.normal(ks[8], (IN_CH, IN_CH), jnp.float32), 'b1': jnp.zeros((IN_CH,), jnp.float32), 'W2': s * jax.random.normal(ks[9], (IN_CH, IN_CH), jnp.float32), 'b2': jnp.zeros((IN_CH,), jnp.float32)}
    _L2_gnn_all = _L2_gnn_setup()
    _L2_gnn_in = {k: v for k, v in _L2_gnn_all.items() if k in ('Wq', 'bq', 'Wk', 'bk', 'Wv', 'bv', 'We', 'Wp', 'bp', 'ln1_g', 'ln1_b', 'ln2_g', 'ln2_b', 'W1', 'b1', 'W2', 'b2')}
    del _L2_gnn_all

    def _L3_gnn_setup():
        import jax, jax.numpy as jnp
        import numpy as np
        N, E = (6250, 100000)
        C_IN, C_OUT, DIM, K = (64, 64, 3, 2)
        EPS = 1e-05

        def _spline_basis(edge_attr):
            D = edge_attr.shape[1]
            v = edge_attr * (K - 1)
            k0 = jnp.floor(v)
            frac = v - k0
            k0 = k0.astype(jnp.int32)
            bits = np.stack(np.unravel_index(np.arange(2 ** D), (2,) * D), axis=-1).astype(np.int32)
            bits_f = jnp.asarray(bits, dtype=edge_attr.dtype)
            w = jnp.where(bits_f[None] > 0, frac[:, None, :], 1.0 - frac[:, None, :])
            weights = jnp.prod(w, axis=-1)
            idx_d = jnp.clip(k0[:, None, :] + bits[None], 0, K - 1)
            radix = jnp.asarray(K ** np.arange(D), dtype=jnp.int32)
            idx = jnp.sum(idx_d * radix, axis=-1)
            return (weights, idx)
        key = jax.random.key(seed)
        k1, k2, k3, k4, k5 = jax.random.split(key, 5)
        x = jax.random.normal(k1, (N, C_IN), dtype=jnp.float32)
        edge_index = jax.random.randint(k2, (2, E), 0, N, dtype=jnp.int32)
        edge_attr = jax.random.uniform(k3, (E, DIM), dtype=jnp.float32)
        W = jax.random.normal(k4, (K ** DIM, C_IN, C_OUT), dtype=jnp.float32) * 0.05
        root = jax.random.normal(k5, (C_IN, C_OUT), dtype=jnp.float32) * 0.05
        gamma = jnp.ones((C_OUT,), dtype=jnp.float32)
        beta = jnp.zeros((C_OUT,), dtype=jnp.float32)
        return {'x': x, 'edge_attr': edge_attr, 'W': W, 'root': root, 'gamma': gamma, 'beta': beta, 'edge_index': edge_index}
    _L3_gnn_all = _L3_gnn_setup()
    _L3_gnn_in = {k: v for k, v in _L3_gnn_all.items() if k in ('W', 'root', 'gamma', 'beta')}
    del _L3_gnn_all
    return {'x': x, 'src': src, 'dst': dst, 'edge_attr_3': edge_attr_3, 'edge_attr_32': edge_attr_32, 'edge_attr_5': edge_attr_5, 'edge_weight': edge_weight, 'L1_gnn_W_lin': _L1_gnn_in['W_lin'], 'L1_gnn_b_lin': _L1_gnn_in['b_lin'], 'L1_gnn_W_edge': _L1_gnn_in['W_edge'], 'L1_gnn_b_edge': _L1_gnn_in['b_edge'], 'L1_gnn_att': _L1_gnn_in['att'], 'L1_gnn_bias': _L1_gnn_in['bias'], 'L2_gnn_Wq': _L2_gnn_in['Wq'], 'L2_gnn_bq': _L2_gnn_in['bq'], 'L2_gnn_Wk': _L2_gnn_in['Wk'], 'L2_gnn_bk': _L2_gnn_in['bk'], 'L2_gnn_Wv': _L2_gnn_in['Wv'], 'L2_gnn_bv': _L2_gnn_in['bv'], 'L2_gnn_We': _L2_gnn_in['We'], 'L2_gnn_Wp': _L2_gnn_in['Wp'], 'L2_gnn_bp': _L2_gnn_in['bp'], 'L2_gnn_ln1_g': _L2_gnn_in['ln1_g'], 'L2_gnn_ln1_b': _L2_gnn_in['ln1_b'], 'L2_gnn_ln2_g': _L2_gnn_in['ln2_g'], 'L2_gnn_ln2_b': _L2_gnn_in['ln2_b'], 'L2_gnn_W1': _L2_gnn_in['W1'], 'L2_gnn_b1': _L2_gnn_in['b1'], 'L2_gnn_W2': _L2_gnn_in['W2'], 'L2_gnn_b2': _L2_gnn_in['b2'], 'L3_gnn_W': _L3_gnn_in['W'], 'L3_gnn_root': _L3_gnn_in['root'], 'L3_gnn_gamma': _L3_gnn_in['gamma'], 'L3_gnn_beta': _L3_gnn_in['beta']}

def reference(x, src, dst, edge_attr_3, edge_attr_32, edge_attr_5, edge_weight, L1_gnn_W_lin, L1_gnn_b_lin, L1_gnn_W_edge, L1_gnn_b_edge, L1_gnn_att, L1_gnn_bias, L2_gnn_Wq, L2_gnn_bq, L2_gnn_Wk, L2_gnn_bk, L2_gnn_Wv, L2_gnn_bv, L2_gnn_We, L2_gnn_Wp, L2_gnn_bp, L2_gnn_ln1_g, L2_gnn_ln1_b, L2_gnn_ln2_g, L2_gnn_ln2_b, L2_gnn_W1, L2_gnn_b1, L2_gnn_W2, L2_gnn_b2, L3_gnn_W, L3_gnn_root, L3_gnn_gamma, L3_gnn_beta):
    import jax
    import jax.numpy as jnp

    def _L0_gnn_ref(x, g, ew):
        import jax, jax.numpy as jnp
        import numpy as np
        N_NODES = 6250
        N_EDGES = 125000
        C_FEAT = 64
        i, j = (g[0], g[1])
        weighted_info = x[i] * ew[:, None]
        aggr_out = jax.ops.segment_sum(weighted_info, j, num_segments=x.shape[0])
        return aggr_out

    def _L1_gnn_ref(x, edge_index, edge_attr, W_lin, b_lin, W_edge, b_edge, att, bias):
        import jax, jax.numpy as jnp
        import numpy as np
        EMB = 64
        HEADS = 2
        NUM_BOND = 5
        NEG_SLOPE = 0.2
        N = x.shape[0]
        h = (x @ W_lin + b_lin).reshape(N, HEADS, EMB)
        ee = (edge_attr @ W_edge + b_edge).reshape(-1, HEADS, EMB)
        src = edge_index[0]
        dst = edge_index[1]
        x_i = h[src]
        x_j = h[dst] + ee
        att_i, att_j = (att[..., :EMB], att[..., EMB:])
        alpha = (x_i * att_i).sum(-1) + (x_j * att_j).sum(-1)
        alpha = jnp.where(alpha >= 0, alpha, NEG_SLOPE * alpha)
        amax = jax.ops.segment_max(alpha, src, num_segments=N)
        e = jnp.exp(alpha - amax[src])
        denom = jax.ops.segment_sum(e, src, num_segments=N)
        alpha = e / (denom[src] + 1e-16)
        messages = x_j * alpha[:, :, None]
        out = jax.ops.segment_sum(messages, src, num_segments=N)
        out = out.mean(axis=1) + bias
        return out

    def _L2_gnn_ref(x, edge_index, edge_attr, Wq, bq, Wk, bk, Wv, bv, We, Wp, bp, ln1_g, ln1_b, ln2_g, ln2_b, W1, b1, W2, b2):
        import math
        import jax, jax.numpy as jnp
        import numpy as np
        N_NODES = 6250
        N_EDGES = 75000
        IN_CH = 64
        HEADS = 2
        C = 64
        HC = HEADS * C
        EDGE_DIM = 32

        def _layernorm(x, g, b, eps=1e-05):
            m = jnp.mean(x, axis=-1, keepdims=True)
            v = jnp.mean(jnp.square(x - m), axis=-1, keepdims=True)
            return (x - m) / jnp.sqrt(v + eps) * g + b
        n = x.shape[0]
        residual = x
        h = _layernorm(x, ln1_g, ln1_b)
        q = (h @ Wq + bq).reshape(n, HEADS, C)
        k = (h @ Wk + bk).reshape(n, HEADS, C)
        v = (h @ Wv + bv).reshape(n, HEADS, C)
        src, tgt = (edge_index[0], edge_index[1])
        e = (edge_attr @ We).reshape(-1, HEADS, C)
        qi = q[tgt]
        kj = k[src] + e
        vj = v[src] + e
        alpha = jnp.sum(qi * kj, axis=-1) / math.sqrt(C)
        amax = jax.ops.segment_max(alpha, tgt, num_segments=n)
        ex = jnp.exp(alpha - amax[tgt])
        den = jax.ops.segment_sum(ex, tgt, num_segments=n)
        a = ex / (den[tgt] + 1e-08)
        agg = jax.ops.segment_sum(a[:, :, None] * vj, tgt, num_segments=n)
        out = agg.reshape(n, HC) @ Wp + bp
        out = out + residual
        res2 = out
        o = _layernorm(out, ln2_g, ln2_b)
        o = jax.nn.gelu(o @ W1 + b1, approximate=False) @ W2 + b2
        return o + res2

    def _L3_gnn_ref(x, edge_attr, W, root, gamma, beta, edge_index):
        import jax, jax.numpy as jnp
        import numpy as np
        N, E = (6250, 100000)
        C_IN, C_OUT, DIM, K = (64, 64, 3, 2)
        EPS = 1e-05

        def _spline_basis(edge_attr):
            D = edge_attr.shape[1]
            v = edge_attr * (K - 1)
            k0 = jnp.floor(v)
            frac = v - k0
            k0 = k0.astype(jnp.int32)
            bits = np.stack(np.unravel_index(np.arange(2 ** D), (2,) * D), axis=-1).astype(np.int32)
            bits_f = jnp.asarray(bits, dtype=edge_attr.dtype)
            w = jnp.where(bits_f[None] > 0, frac[:, None, :], 1.0 - frac[:, None, :])
            weights = jnp.prod(w, axis=-1)
            idx_d = jnp.clip(k0[:, None, :] + bits[None], 0, K - 1)
            radix = jnp.asarray(K ** np.arange(D), dtype=jnp.int32)
            idx = jnp.sum(idx_d * radix, axis=-1)
            return (weights, idx)
        src, dst = (edge_index[0], edge_index[1])
        Etot = edge_attr.shape[0]
        S = W.shape[0]
        weights, idx = _spline_basis(edge_attr)
        B = jnp.zeros((Etot, S), dtype=x.dtype).at[jnp.arange(Etot)[:, None], idx].add(weights)
        xj = x[src]
        z = (B[:, :, None] * xj[:, None, :]).reshape(Etot, S * x.shape[1])
        msg = z @ W.reshape(S * x.shape[1], W.shape[2])
        agg = jax.ops.segment_sum(msg, dst, num_segments=x.shape[0])
        cnt = jax.ops.segment_sum(jnp.ones((Etot,), dtype=x.dtype), dst, num_segments=x.shape[0])
        out = agg / jnp.maximum(cnt, 1.0)[:, None] + x @ root
        mean = jnp.mean(out, axis=0)
        var = jnp.var(out, axis=0)
        y = (out - mean) * jax.lax.rsqrt(var + EPS) * gamma + beta
        return jax.nn.elu(y)
    edge_index = jnp.stack([src, dst])
    x = _layernorm(x + _L0_gnn_ref(x, edge_index, edge_weight), axis=-1)
    x = _layernorm(x + _L1_gnn_ref(x, edge_index, edge_attr_5, L1_gnn_W_lin, L1_gnn_b_lin, L1_gnn_W_edge, L1_gnn_b_edge, L1_gnn_att, L1_gnn_bias), axis=-1)
    x = _layernorm(x + _L2_gnn_ref(x, edge_index, edge_attr_32, L2_gnn_Wq, L2_gnn_bq, L2_gnn_Wk, L2_gnn_bk, L2_gnn_Wv, L2_gnn_bv, L2_gnn_We, L2_gnn_Wp, L2_gnn_bp, L2_gnn_ln1_g, L2_gnn_ln1_b, L2_gnn_ln2_g, L2_gnn_ln2_b, L2_gnn_W1, L2_gnn_b1, L2_gnn_W2, L2_gnn_b2), axis=-1)
    x = _layernorm(x + _L3_gnn_ref(x, edge_attr_3, L3_gnn_W, L3_gnn_root, L3_gnn_gamma, L3_gnn_beta, edge_index), axis=-1)
    return x

_drawn_inputs = setup_inputs


def setup_inputs(seed=0):
    import zlib

    import numpy as np

    out = dict(_drawn_inputs(seed))
    spreads = {'L1_gnn_b_lin': (0.0, 0.1),
     'L1_gnn_b_edge': (0.0, 0.1),
     'L1_gnn_bias': (0.0, 0.1),
     'L2_gnn_bq': (0.0, 0.8),
     'L2_gnn_bk': (0.0, 2.0),
     'L2_gnn_bv': (0.0, 0.358),
     'L2_gnn_bp': (0.0, 0.1),
     'L2_gnn_ln1_g': (1.0, 0.6),
     'L2_gnn_ln1_b': (0.0, 0.8),
     'L2_gnn_ln2_g': (1.0, 0.6),
     'L2_gnn_ln2_b': (0.0, 2.0),
     'L2_gnn_b1': (0.0, 0.8),
     'L2_gnn_b2': (0.0, 0.283),
     'L3_gnn_gamma': (1.0, 0.2),
     'L3_gnn_beta': (0.0, 0.1)}
    factors = {'edge_attr_32': 3.23, 'L2_gnn_Wq': 7.883, 'L2_gnn_Wk': 8.0, 'L2_gnn_We': 3.105}
    for name, (base, spread) in spreads.items():
        noise = np.random.default_rng([zlib.crc32(name.encode()), seed]).standard_normal(out[name].shape)
        drawn = base * np.exp(spread * noise) if base else spread * noise
        out[name] = jnp.asarray(drawn.astype(out[name].dtype))
    for name, factor in factors.items():
        out[name] = (out[name] * factor).astype(out[name].dtype)
    return out
```

```python
from contextlib import ExitStack

import numpy as np

import concourse.bass as bass
from concourse import mybir

F32 = mybir.dt.float32
I32 = mybir.dt.int32
BF16 = mybir.dt.bfloat16
ALU = mybir.AluOpType
ACT = mybir.ActivationFunctionType
AX = mybir.AxisListType.X

P = 128
N = 6250
E = 200000
C = 64
NT = -(-N // P)
NP = NT * P
L = 1568
EP = P * L
assert EP >= E and NP > N
H = 2
D5, D32, D3 = 5, 32, 3
FAR = 1.0e30
OFF = 1.0e7
LN_EPS = 1e-5

F1 = C + D5 + 1
R1 = F1 + H
B1 = C + H + 1
F2 = C + D32 + 1
B2 = H * F2 + H
S3 = 2 ** D3
T1 = 28
T2 = 14
SB = 8


UNROLL = 4


class Chunk:

    def __init__(self, g, r):
        self.g, self.r, self.b = g, r, r % 2
        self.h = g * (UNROLL // 2) + r // 2
        self.at = g * UNROLL + r


def chunks(eng, count):
    with eng.Fori(0, count // UNROLL) as g:
        for r in range(UNROLL):
            yield Chunk(g, r)


def chunks_ahead(eng, count, first, second):
    first(Chunk(0, 0))
    with eng.Fori(0, count // UNROLL - 1) as g:
        for r in range(UNROLL):
            first(Chunk(g, r + 1) if r + 1 < UNROLL else Chunk(g + 1, 0))
            second(Chunk(g, r))
    last = count // UNROLL - 1
    for r in range(UNROLL):
        if r + 1 < UNROLL:
            first(Chunk(last, r + 1))
        second(Chunk(last, r))


def wait(eng, sem, value):
    eng.wait_ge(sem, value)
    eng.nop(nofuse=True)


def build(nc, a, out):
    top = ExitStack()

    in_use = []

    def sem(name):
        in_use.append(nc.alloc_semaphore(name=name))
        return in_use[-1]

    def clear_semaphores():
        nc.all_engine_barrier()
        nc.clear_and_free_semaphores(in_use)
        in_use.clear()
        nc.all_engine_barrier()

    def dram(name, shape, dt=F32):
        return nc.dram_tensor(name, shape, dt, kind="Internal").ap()

    first_d = {k: dram(f"first_{k}", (NP + 1, 1)) for k in ("src", "dst")}
    pos_d = dram("pos", (P, L), I32)
    sums0_d = dram("sums0", (EP, C))
    table1_d = dram("table1", (NP, B1))
    tablea_d = dram("tablea", (NP, H + 1))
    spread1_d = dram("spread1", (EP, B1))
    spreada_d = dram("spreada", (EP, H + 1))
    rows1_d = dram("rows1", (EP, R1))
    sums1_d = dram("sums1", (EP, H * F1 + H))
    h2_d = dram("h2", (NP, C))
    table2_d = dram("table2", (NP, B2))
    spread2_d = dram("spread2", (EP, B2))
    sums2_d = dram("sums2", (EP, H * F2 + H))
    table3_d = dram("table3", (NP, S3 * C))
    sums3_d = dram("sums3", (EP, C))

    def run_of(t, w):
        return t.rearrange("(p l) w -> p (l w)", p=P) if w else t.rearrange("(p l) -> p l", p=P)

    with top:
        def keep_tile(name, shape, dt=F32):
            return top.enter_context(nc.sbuf_tensor(name, shape, dt))

        x = keep_tile("x", [P, NT, C])
        identity = keep_tile("identity", [P, P])
        run_end = keep_tile("run_end", [P, 1])
        end_idx = {k: keep_tile(f"end_idx_{k}", [P, NT], I32) for k in ("src", "dst")}
        start_idx = {k: keep_tile(f"start_idx_{k}", [P, NT], I32) for k in ("src", "dst")}
        filled = {k: keep_tile(f"filled_{k}", [P, NT]) for k in ("src", "dst")}
        degree = keep_tile("degree", [P, NT])
        head_key = {k: keep_tile(f"head_key_{k}", [P, 1], I32) for k in ("src", "dst")}
        tail_key = {k: keep_tile(f"tail_key_{k}", [P, 1]) for k in ("src", "dst")}

        ordering(nc, a, sem, dict(locals()))
        layer0(nc, a, sem, dict(locals()))
        layer1(nc, a, sem, dict(locals()))
        clear_semaphores()
        layer2(nc, a, sem, dict(locals()))
        layer3(nc, a, sem, dict(locals()), out)


class Space:

    def __init__(self, nc, stack):
        self.nc, self.stack = nc, stack

    def sb(self, name, shape, dt=F32):
        return self.stack.enter_context(self.nc.sbuf_tensor(name, shape, dt))

    def ps(self, name, shape, dt=F32):
        return self.stack.enter_context(self.nc.psum_tensor(name, shape, dt))


def ordering(nc, a, sem, g):
    with ExitStack() as stack:
        sp_ = Space(nc, stack)
        sb, ps = sp_.sb, sp_.ps
        key = {k: sb(f"key_{k}", [P, L], I32) for k in ("src", "dst")}
        part = sb("part", [P, L], I32)
        low = {k: sb(f"low_{k}", [P, L], BF16) for k in ("src", "dst")}
        high = {k: sb(f"high_{k}", [P, L], BF16) for k in ("src", "dst")}
        iota_i = sb("iota_i", [P, P], I32)
        iota_b = sb("iota_b", [P, P], BF16)
        row_i = sb("row_i", [P, 1], I32)
        row_f = sb("row_f", [P, 1])
        col_f = sb("col_f", [P, P])
        ident_b = sb("ident_b", [P, P], BF16)
        upper_b = sb("upper_b", [P, P], BF16)
        upper = sb("upper", [P, P])
        ones = sb("ones", [P, P])
        zero_b = sb("zero_b", [P, P], BF16)
        hot_low = sb("hot_low", [P, 2, SB, P], BF16)
        hot_high = sb("hot_high", [P, 2, SB, NT], BF16)
        low_t = sb("low_t", [P, 2, SB * P], BF16)
        low_tf = sb("low_tf", [P, 2, SB * P])
        earlier = sb("earlier", [P, SB * P], BF16)
        count = sb("count", [P, NT])
        col_sum = sb("col_sum", [P, NT + 1])
        prefix = sb("prefix", [P, NT + 1])
        first = {k: sb(f"firstt_{k}", [P, NT]) for k in ("src", "dst")}
        after = sb("after", [P, NT])
        tmp = sb("tmp_o", [P, NT])
        tmp2 = sb("tmp2_o", [P, NT])
        before = sb("before", [P, 2, NT])
        picked = sb("picked", [P, SB, NT])
        pos_f = sb("pos_f", [P, L])
        pos_i = sb("pos_i", [P, L], I32)
        ends_row = sb("ends_row", [P, NP])
        scratch_row = sb("scratch_row", [P, NP], BF16)
        key_f = sb("key_f", [P, 1])
        last_f = sb("last_f", [P, 1])
        total = sb("total", [1, 2])
        zeros = sb("zeros", [P, 4096])
        hist = ps("hist", [P, 512])
        turned = ps("turned", [P, SB * P], BF16)
        same = ps("same", [P, SB, P])
        rank = ps("rank", [P, SB, C])

        loaded, made, drawn, hot, counted = (sem(f"o_{n}") for n in ("loaded", "made", "drawn", "hot", "counted"))
        hot_used, summed, hist_free, first_out, ends_in = (sem(f"o_{n}") for n in ("hot_used", "summed", "hist_free", "first_out", "ends_in"))
        ready = sem("o_ready")
        steps = L // SB

        with nc.Block() as block:
            @block.sync
            def _(sp):
                for k in ("src", "dst"):
                    sp.dma_start(key[k][:], g["run_of"](a[k], 0)).then_inc(loaded, 16)

            @block.gpsimd
            def _(pool):
                nc.gpsimd.iota(iota_i[:], [[1, P]], base=0, channel_multiplier=0).then_inc(drawn, 1)
                nc.gpsimd.iota(row_i[:], [[0, 1]], base=0, channel_multiplier=1).then_inc(drawn, 1)

            @block.vector
            def _(v):
                v.wait_ge(drawn, 2)
                v.tensor_copy(iota_b[:], iota_i[:])
                v.tensor_copy(col_f[:], iota_i[:])
                v.tensor_copy(row_f[:], row_i[:])
                v.memset(ones[:], 1.0)
                v.memset(zero_b[:], 0.0)
                v.memset(zeros[:], 0.0)
                v.memset(col_sum[:], 0.0)
                v.memset(total[:], float(EP))
                v.drain()
                v.tensor_scalar(g["identity"][:], col_f[:], row_f[:, 0:1], None, ALU.is_equal)
                v.tensor_scalar(ident_b[:], col_f[:], row_f[:, 0:1], None, ALU.is_equal)
                v.tensor_scalar(upper[:], col_f[:], row_f[:, 0:1], None, ALU.is_gt)
                v.tensor_scalar(upper_b[:], col_f[:], row_f[:, 0:1], None, ALU.is_gt)
                v.tensor_scalar(g["run_end"][:], row_f[:], float(L), float(L), ALU.mult, ALU.add)
                v.wait_ge(loaded, 32)
                for k in ("src", "dst"):
                    v.tensor_scalar(part[:], key[k][:], 127, None, ALU.bitwise_and)
                    v.drain()
                    v.tensor_copy(low[k][:], part[:])
                    v.drain()
                    v.tensor_scalar(part[:], key[k][:], 7, None, ALU.arith_shift_right)
                    v.drain()
                    v.tensor_copy(high[k][:], part[:])
                    v.drain()

        def one_hots(v, k, step, b):
            at = bass.ds(step * SB, SB)
            v.tensor_tensor(hot_low[:, b], iota_b[:].unsqueeze(1).to_broadcast([P, SB, P]),
                            low[k][:, at].unsqueeze(2).to_broadcast([P, SB, P]), ALU.is_equal)
            return v.tensor_tensor(hot_high[:, b], iota_b[:, 0:NT].unsqueeze(1).to_broadcast([P, SB, NT]),
                                   high[k][:, at].unsqueeze(2).to_broadcast([P, SB, NT]), ALU.is_equal)

        for k in ("src", "dst"):
            hot, hot_used = [sem(f"o_hot{k}{b}") for b in range(2)], [sem(f"o_used{k}{b}") for b in range(2)]
            summed, prefixed, tri = sem(f"o_sum{k}"), sem(f"o_pre{k}"), sem(f"o_tri{k}")
            first_out, ends_in, counted = sem(f"o_fo{k}"), sem(f"o_ei{k}"), sem(f"o_c{k}")
            with nc.Block() as block:
                @block.tensor
                def _(pe):
                    nc.tensor.matmul(hist[:, 0:NT], zero_b[:], zero_b[:, 0:NT], start=True, stop=False,
                                     skip_group_check=True)
                    with pe.Fori(0, steps // 2) as h:
                        for b in range(2):
                            wait(pe, hot[b], h + 1)
                            for j in range(SB):
                                last = nc.tensor.matmul(hist[:, 0:NT], hot_low[:, b, j], hot_high[:, b, j],
                                                        start=False, stop=False, skip_group_check=True)
                            last.then_inc(hot_used[b], 1)
                    pe.wait_ge(counted, 1)
                    nc.tensor.matmul(hist[:, 64:64 + NT], ones[:], count[:], start=True, stop=True,
                                     skip_group_check=True)
                    nc.tensor.matmul(hist[:, 128:128 + NT], upper[:], count[:], start=True, stop=True,
                                     skip_group_check=True).then_inc(tri, 1)

                @block.vector
                def _(v):
                    v.sem_inc(hot_used[0], 1)
                    v.sem_inc(hot_used[1], 1)
                    with v.Fori(0, steps // 2) as h:
                        for b in range(2):
                            wait(v, hot_used[b], h + 1)
                            one_hots(v, k, h * 2 + b, b).then_inc(hot[b], 1)
                    v.wait_ge(hot_used[0], steps // 2 + 1)
                    v.wait_ge(hot_used[1], steps // 2 + 1)
                    v.tensor_copy(count[:], hist[:, 0:NT]).then_inc(counted, 1)
                    v.wait_ge(tri, 1)
                    v.tensor_copy(col_sum[:, 1:NT + 1], hist[:, 64:64 + NT])
                    v.drain()
                    v.tensor_tensor_scan(prefix[:], ones[:, 0:NT + 1], col_sum[:], 0.0, ALU.mult, ALU.add)
                    v.drain()
                    v.tensor_tensor(first[k][:], prefix[:, 0:NT], hist[:, 128:128 + NT], ALU.add)
                    if k == "dst":
                        v.tensor_copy(g["degree"][:], count[:])
                    v.tensor_scalar(g["filled"][k][:], count[:], 0.5, None, ALU.is_gt)
                    v.drain()
                    v.tensor_tensor(after[:], first[k][:], count[:], ALU.add).then_inc(summed, 1)
                    v.tensor_scalar(tmp2[:], g["filled"][k][:], -OFF, OFF, ALU.mult, ALU.add)
                    v.drain()
                    v.tensor_scalar(tmp[:], after[:], -1.0, 0.0, ALU.add, ALU.max)
                    v.tensor_tensor(tmp2[:], tmp2[:], first[k][:], ALU.add)
                    v.drain()
                    v.tensor_copy(g["end_idx"][k][:], tmp[:])
                    v.tensor_copy(g["start_idx"][k][:], tmp2[:])
                    v.wait_ge(ends_in, 16)
                    v.tensor_scalar(key_f[:], g["run_end"][:], -float(L), None, ALU.add)
                    v.tensor_scalar(last_f[:], g["run_end"][:], -1.0, None, ALU.add)
                    v.drain()
                    v.tensor_scalar(scratch_row[:], ends_row[:], key_f[:, 0:1], 0.0, ALU.is_le, ALU.add,
                                    accum_out=tmp[:, 0:1])
                    v.drain()
                    v.tensor_scalar(scratch_row[:], ends_row[:], last_f[:, 0:1], 0.0, ALU.is_le, ALU.add,
                                    accum_out=g["tail_key"][k][:])
                    v.drain()
                    v.tensor_copy(g["head_key"][k][:], tmp[:, 0:1])

                @block.sync
                def _(sp):
                    sp.wait_ge(summed, 1)
                    sp.dma_start(g["first_d"][k][0:NP].rearrange("(t p) o -> p (t o)", p=P), first[k][:],
                                 allow_slow_non_contiguous=True).then_inc(first_out, 16)
                    sp.dma_start(g["first_d"][k][NP:NP + 1], total[:, 0:1]).then_inc(first_out, 16)
                    sp.wait_ge(first_out, 32)
                    sp.dma_start(ends_row[:], g["first_d"][k][1:NP + 1].rearrange("n o -> o n").to_broadcast([P, NP])) \
                      .then_inc(ends_in, 16)

        hot = [sem(f"r_hot{b}") for b in range(2)]
        hot_used = [sem(f"r_used{b}") for b in range(2)]
        turned_ready, copied, same_ready, masked = (sem(f"r_{n}") for n in ("turned", "copied", "same", "masked"))
        based, grown, ranked, rank_read, pos_out = (sem(f"r_{n}") for n in ("based", "grown", "ranked", "rank_read", "pos_out"))
        cleared = sem("r_cleared")
        with nc.Block() as block:
            @block.tensor
            def _(pe):
                nc.tensor.matmul(hist[:, 0:NT], zero_b[:], zero_b[:, 0:NT], start=True, stop=False,
                                 skip_group_check=True)
                with pe.Fori(0, steps // 2) as h:
                    for b in range(2):
                        s = h * 2 + b
                        wait(pe, hot[b], h + 1)
                        wait(pe, copied, s + 1)
                        for j in range(SB):
                            last = nc.tensor.transpose(turned[:, j * P:(j + 1) * P], hot_low[:, b, j], ident_b[:])
                        last.then_inc(turned_ready, 1)
                        wait(pe, copied, s + 2)
                        wait(pe, masked, s + 1)
                        for j in range(SB):
                            t = low_t[:, b, j * P:(j + 1) * P]
                            last = nc.tensor.matmul(same[:, j], t, t, start=True, stop=True)
                        last.then_inc(same_ready, 1)
                        wait(pe, masked, s + 2)
                        wait(pe, rank_read, s + 1)
                        for j in range(SB):
                            nc.tensor.matmul(rank[:, j, 0:NT], earlier[:, j * P:(j + 1) * P], hot_high[:, b, j],
                                             start=True, stop=False, skip_group_check=True)
                            wait(pe, based, s * SB + (j + 1))
                            nc.tensor.matmul(hist[:, 0:NT], hot_low[:, b, j], hot_high[:, b, j],
                                             start=False, stop=False, skip_group_check=True).then_inc(grown, 1)
                            last = nc.tensor.matmul(rank[:, j, 0:NT], low_tf[:, b, j * P:(j + 1) * P],
                                                    before[:, j % 2], start=False, stop=True, skip_group_check=True)
                        last.then_inc(ranked, 1)

            @block.scalar
            def _(act):
                act.sem_inc(copied, 1)
                with act.Fori(0, steps // 2) as h:
                    for b in range(2):
                        wait(act, turned_ready, h * 2 + (b + 1))
                        wait(act, ranked, h * 2 + b + 1)
                        nc.scalar.copy(low_t[:, b], turned[:])
                        nc.scalar.copy(low_tf[:, b], turned[:]).then_inc(copied, 1)

            @block.vector
            def _(v):
                v.sem_inc(masked, 1)
                v.sem_inc(rank_read, 1)
                v.sem_inc(ranked, 2)
                v.tensor_copy(before[:, 0], first["src"][:]).then_inc(based, 1)
                one_hots(v, "src", 0, 0).then_inc(hot[0], 1)

                def step(s, b, h, more=True):
                    wait(v, same_ready, s + 1)
                    v.tensor_tensor(earlier[:].rearrange("p (j e) -> p j e", j=SB), same[:],
                                    upper_b[:].unsqueeze(1).to_broadcast([P, SB, P]), ALU.mult).then_inc(masked, 1)
                    if more:
                        wait(v, ranked, s + 2)
                        one_hots(v, "src", s + 1, 1 - b).then_inc(hot[1 - b], 1)
                    for j in range(SB):
                        wait(v, grown, s * SB + (j + 1))
                        v.tensor_tensor(before[:, (j + 1) % 2], first["src"][:], hist[:, 0:NT], ALU.add) \
                         .then_inc(based, 1)
                    wait(v, ranked, s + 3)
                    v.tensor_tensor(picked[:], rank[:, :, 0:NT], hot_high[:, b], ALU.mult).then_inc(rank_read, 1)
                    v.drain()
                    v.tensor_reduce(pos_f[:, bass.ds(s * SB, SB)], picked[:], AX, ALU.add)

                with v.Fori(0, steps // 2 - 1) as h:
                    step(h * 2, 0, h)
                    step(h * 2 + 1, 1, h)
                step(steps - 2, 0, None)
                step(steps - 1, 1, None, more=False)
                v.drain()
                v.tensor_copy(pos_i[:], pos_f[:]).then_inc(ready, 1)

            @block.sync
            def _(sp):
                def clear(t, w):
                    flat = g["run_of"](t, w)
                    width = L * w
                    step = width // -(-width // 4096)
                    while width % step:
                        step -= 1
                    n = 0
                    for c in range(width // step):
                        sp.dma_start(flat[:, c * step:(c + 1) * step], zeros[:, 0:step]).then_inc(cleared, 16)
                        n += 16
                    return n
                n = clear(g["spread1_d"], B1) + clear(g["spreada_d"], H + 1) + clear(g["spread2_d"], B2)
                sp.wait_ge(cleared, n)
                sp.wait_ge(ready, 1)
                sp.dma_start(g["pos_d"], pos_i[:]).then_inc(pos_out, 16)
                sp.wait_ge(pos_out, 16)


def spread_masks(nc, sem, g, k, name, masks, last_only):
    with ExitStack() as stack:
        s = Space(nc, stack)
        first_row = s.sb(f"{name}_first", [P, NP])
        end_row = s.sb(f"{name}_end", [P, NP])
        got, done = sem(f"{name}_got"), sem(f"{name}_done")
        run_past = s.sb(f"{name}_past", [P, 1])
        with nc.Block() as block:
            @block.sync
            def _(sp):
                sp.dma_start(first_row[:], g["first_d"][k][0:NP].rearrange("n o -> o n").to_broadcast([P, NP])).then_inc(got, 16)
                sp.dma_start(end_row[:], g["first_d"][k][1:NP + 1].rearrange("n o -> o n").to_broadcast([P, NP])).then_inc(got, 16)

            @block.vector
            def _(v):
                v.wait_ge(got, 32)
                run_end = g["run_end"][:, 0:1]
                v.tensor_scalar(run_past[:], g["run_end"][:], float(L), None, ALU.add)
                v.tensor_scalar(first_row[:], first_row[:], run_end, None, ALU.is_lt)
                v.drain()
                v.scalar_tensor_tensor(out=masks[:], in0=end_row[:], scalar=run_end, in1=first_row[:],
                                       op0=ALU.is_gt, op1=ALU.mult)
                v.drain()
                if last_only is not None:
                    v.scalar_tensor_tensor(out=last_only[:], in0=end_row[:], scalar=run_past[:, 0:1], in1=masks[:],
                                           op0=ALU.is_le, op1=ALU.mult)


def normalise(nc, v, act, sums, out_, work, stat, sems, turn, gain=None, shift=None):
    centred, rooted = sems
    if v is not None:
        v.tensor_reduce(stat[:, 0], sums, AX, ALU.add)
        v.drain()
        v.tensor_scalar(stat[:, 0], stat[:, 0], 1.0 / C, None, ALU.mult)
        v.drain()
        v.tensor_tensor(sums, sums, stat[:, 0].unsqueeze(2).to_broadcast([P, NT, C]), ALU.subtract)
        v.drain()
        v.tensor_tensor(work, sums, sums, ALU.mult)
        v.drain()
        v.tensor_reduce(stat[:, 1], work, AX, ALU.add)
        v.drain()
        v.tensor_scalar(stat[:, 1], stat[:, 1], 1.0 / C, LN_EPS, ALU.mult, ALU.add).then_inc(centred, 1)
        v.wait_ge(rooted, turn)
        v.reciprocal(stat[:, 1], stat[:, 2])
        v.drain()
        v.tensor_tensor(out_, sums, stat[:, 1].unsqueeze(2).to_broadcast([P, NT, C]), ALU.mult)
        v.drain()
        if gain is not None:
            v.tensor_tensor(out_, out_, gain[:].unsqueeze(1).to_broadcast([P, NT, C]), ALU.mult)
            v.drain()
            v.tensor_tensor(out_, out_, shift[:].unsqueeze(1).to_broadcast([P, NT, C]), ALU.add)
            v.drain()
    if act is not None:
        act.wait_ge(centred, turn)
        nc.scalar.activation(stat[:, 2], stat[:, 1], ACT.Sqrt).then_inc(rooted, 1)


def layer0(nc, a, sem, g):
    T, NC = T1, L // T1
    x = g["x"]
    with ExitStack() as outer:
        tail = Space(nc, outer).sb("l0_tail", [P, C])
        with ExitStack() as stack:
            s = Space(nc, stack)
            idx = s.sb("l0_idx", [P, 2, T], I32)
            rows = s.sb("l0_rows", [P, 2, T, C])
            data = s.sb("l0_data", [P, C, T + 1])
            keep = s.sb("l0_keep", [P, 2, C, T + 1])
            run = s.sb("l0_run", [P, 2, C, T + 1])
            outb = s.sb("l0_out", [P, 2, T, C])
            weight = s.sb("l0_weight", [P, L])
            keys = s.sb("l0_keys", [P, L], I32)
            prev = s.sb("l0_prev", [P, L], I32)
            same = s.sb("l0_same", [P, L])
            two = lambda n: [sem(f"l0_{n}{b}") for b in range(2)]
            idx_in, got, rows_used, keep_ready, scanned, copied, stored = (two(n) for n in (
                "idx_in", "got", "rows_used", "keep_ready", "scanned", "copied", "stored"))
            loaded, flags, x_in = sem("l0_loaded"), sem("l0_flags"), sem("l0_x_in")
            with nc.Block() as block:
                @block.sync
                def _(sp):
                    sp.dma_start(weight[:], g["run_of"](a["edge_weight"], 0)).then_inc(loaded, 16)
                    sp.dma_start(keys[:], g["run_of"](a["dst"], 0)).then_inc(loaded, 16)
                    sp.dma_start(prev[:], g["run_of"](a["dst_before"], 0)).then_inc(loaded, 16)
                    sp.dma_start(x[:], a["x"].rearrange("(t p) c -> p t c", p=P)).then_inc(x_in, 16)
                    src = g["run_of"](a["src"], 0)
                    with sp.Fori(0, NC // 2) as h:
                        for b in range(2):
                            wait(sp, rows_used[b], h + 1)
                            sp.dma_start(idx[:, b], src[:, bass.ds((h * 2 + b) * T, T)]).then_inc(idx_in[b], 16)
                    sp.wait_ge(x_in, 16)

                @block.gpsimd
                def _(pool):
                    with pool.Fori(0, NC // 2) as h:
                        for b in range(2):
                            wait(pool, idx_in[b], (h + 1) * 16)
                            for t in range(T):
                                pool.indirect_dma_start(rows[:, b, t], None, a["x"],
                                                        bass.IndirectOffsetOnAxis(ap=idx[:, b, t:t + 1], axis=0)) \
                                    .then_inc(got[b], 16)

                @block.vector
                def _(v):
                    v.memset(run[:].rearrange("p b f t -> p (b f t)"), 0.0)
                    v.memset(keep[:].rearrange("p b f t -> p (b f t)"), 0.0)
                    v.sem_inc(rows_used[0], 1)
                    v.sem_inc(rows_used[1], 1)
                    v.wait_ge(loaded, 48)
                    v.tensor_tensor(same[:], keys[:], prev[:], ALU.is_equal).then_inc(flags, 1)
                    v.drain()
                    with v.Fori(0, NC // 2) as h:
                        for b in range(2):
                            wait(v, got[b], (h + 1) * (16 * T))
                            at = bass.ds((h * 2 + b) * T, T)
                            v.tensor_tensor(data[:, :, 1:], rows[:, b].rearrange("p t f -> p f t"),
                                            weight[:, at].unsqueeze(1).to_broadcast([P, C, T]), ALU.mult) \
                             .then_inc(rows_used[b], 1)
                            v.tensor_copy(data[:, :, 0:1], run[:, 1 - b, :, T:T + 1])
                            wait(v, keep_ready[b], h + 1)
                            wait(v, copied[b], h + 1)
                            v.drain()
                            v.tensor_tensor_scan(run[:, b].rearrange("p f t -> p (f t)"),
                                                 keep[:, b].rearrange("p f t -> p (f t)"),
                                                 data[:].rearrange("p f t -> p (f t)"), 0.0, ALU.mult, ALU.add) \
                             .then_inc(scanned[b], 1)
                            v.drain()
                    v.tensor_copy(tail[:], run[:, 1, :, T])

                @block.scalar
                def _(act):
                    act.wait_ge(flags, 1)
                    act.sem_inc(copied[0], 1)
                    act.sem_inc(copied[1], 1)
                    act.sem_inc(stored[0], 16)
                    act.sem_inc(stored[1], 16)
                    act.sem_inc(scanned[0], 1)
                    act.sem_inc(scanned[1], 1)
                    with act.Fori(0, NC // 2) as h:
                        for b in range(2):
                            wait(act, scanned[b], h + 1)
                            at = bass.ds((h * 2 + b) * T, T)
                            nc.scalar.copy(keep[:, b, :, 1:], same[:, at].unsqueeze(1).to_broadcast([P, C, T])) \
                              .then_inc(keep_ready[b], 1)
                            wait(act, scanned[b], h + 2)
                            wait(act, stored[b], (h + 1) * 16)
                            nc.scalar.copy(outb[:, b], run[:, b, :, 1:].rearrange("p f t -> p t f")).then_inc(copied[b], 1)
                            wait(act, copied[b], h + 2)
                            act.dma_start(g["run_of"](g["sums0_d"], C)[:, bass.ds((h * 2 + b) * (T * C), T * C)],
                                          outb[:, b].rearrange("p t f -> p (t f)")).then_inc(stored[b], 16)
                    for b in range(2):
                        act.wait_ge(stored[b], 16 * (NC // 2 + 1))

        total = collect_sums(nc, sem, g, outer, "l0", g["sums0_d"], tail)
        with ExitStack() as stack:
            s = Space(nc, stack)
            work, stat = s.sb("l0_work", [P, NT, C]), s.sb("l0_stat", [P, 3, NT])
            sems = sem("l0_centred"), sem("l0_rooted")
            with nc.Block() as block:
                @block.vector
                def _(v):
                    v.tensor_tensor(total[:], total[:], x[:], ALU.add)
                    v.drain()
                    normalise(nc, v, None, total[:], x[:], work[:], stat, sems, 1)

                @block.scalar
                def _(act):
                    normalise(nc, None, act, None, None, None, stat, sems, 1)


def collect_sums(nc, sem, g, outer, name, sums_d, tail):
    s0 = Space(nc, outer)
    total = s0.sb(f"{name}_total", [P, NT, C])
    with ExitStack() as stack:
        s = Space(nc, stack)
        masks = s.sb(f"{name}_masks", [P, NP])
        more = s.ps(f"{name}_more", [P, 2, 8, C])
        spread_masks(nc, sem, g, "dst", name, masks, None)
        got, read, mult = sem(f"{name}_cgot"), sem(f"{name}_cread"), sem(f"{name}_cmult")
        groups = [range(i, min(i + 8, NT)) for i in range(0, NT, 8)]
        with nc.Block() as block:
            @block.gpsimd
            def _(pool):
                for i in range(NT):
                    pool.indirect_dma_start(total[:, i], None, sums_d,
                                            bass.IndirectOffsetOnAxis(ap=g["end_idx"]["dst"][:, i:i + 1], axis=0)).then_inc(got, 16)

            @block.tensor
            def _(pe):
                for n, tiles in enumerate(groups):
                    if n >= 2:
                        pe.wait_ge(read, n - 1)
                    for j, i in enumerate(tiles):
                        last = nc.tensor.matmul(more[:, n % 2, j], masks[:, i * P:(i + 1) * P], tail[:], start=True, stop=True)
                    last.then_inc(mult, 1)

            @block.vector
            def _(v):
                v.wait_ge(got, 16 * NT)
                v.tensor_tensor(total[:], total[:], g["filled"]["dst"][:].unsqueeze(2).to_broadcast([P, NT, C]), ALU.mult)
                v.drain()
                for n, tiles in enumerate(groups):
                    v.wait_ge(mult, n + 1)
                    at = slice(tiles[0], tiles[-1] + 1)
                    v.tensor_tensor(total[:, at], total[:, at], more[:, n % 2, 0:len(tiles)], ALU.add).then_inc(read, 1)
    return total


def layer1(nc, a, sem, g):
    x = g["x"]
    with ExitStack() as outer:
        s0 = Space(nc, outer)
        tail = s0.sb("l1_tail", [P, H * F1 + H])
        head = s0.sb("l1_head", [P, B1])
        head_a = s0.sb("l1_heada", [P, H + 1])
        edge_w = s0.sb("l1_edge_w", [P, H, D5])
        with ExitStack() as stack:
            s = Space(nc, stack)
            att = s.sb("l1_att", [C, 2 * H])
            att_wide = s.sb("l1_att_wide", [C, 2 * H, P])
            proj = s.sb("l1_proj", [C, H, F1 + 1])
            node_w = s.sb("l1_node_w", [P, 2, H, F1 + 1])
            const = s.sb("l1_const", [P, H])
            rows = s.sb("l1_node_rows", [P, NT, B1])
            rows_a = s.sb("l1_node_rows_a", [P, NT, H + 1])
            prod = s.sb("l1_node_prod", [P, NT, C])
            score = s.sb("l1_node_score", [P, 2, H, NT])
            dots = s.ps("l1_dots", [P, 2, H, P])
            loaded, wide, dotted, tabled, saved, fetched = (sem(f"l1_{n}") for n in ("loaded", "wide", "dotted", "tabled", "saved", "fetched"))
            with nc.Block() as block:
                @block.sync
                def _(sp):
                    sp.dma_start(att[:], a["att1"]).then_inc(loaded, 16)
                    sp.dma_start(proj[:], a["proj1"]).then_inc(loaded, 16)
                    sp.wait_ge(tabled, 2)
                    sp.dma_start(g["table1_d"].rearrange("(t p) w -> p t w", p=P), rows[:]).then_inc(saved, 16)
                    sp.dma_start(g["tablea_d"].rearrange("(t p) w -> p t w", p=P), rows_a[:]).then_inc(saved, 16)

                @block.tensor
                def _(pe):
                    pe.wait_ge(loaded, 32)
                    pe.wait_ge(wide, 1)
                    for side in range(2):
                        for h in range(H):
                            last = nc.tensor.matmul(dots[:, side, h, 0:F1 + 1], att_wide[:, side * H + h], proj[:, h],
                                                    start=True, stop=True)
                    last.then_inc(dotted, 1)

                @block.vector
                def _(v):
                    v.wait_ge(loaded, 32)
                    v.tensor_copy(att_wide[:], att[:].unsqueeze(2).to_broadcast([C, 2 * H, P])).then_inc(wide, 1)
                    v.memset(rows[:], 1.0)
                    v.memset(rows_a[:], 1.0)
                    v.wait_ge(dotted, 1)
                    v.tensor_copy(node_w[:], dots[:, :, :, 0:F1 + 1])
                    v.drain()
                    v.tensor_copy(edge_w[:], node_w[:, 1, :, C + 1:C + 1 + D5])
                    v.tensor_tensor(const[:], node_w[:, 1, :, C], node_w[:, 1, :, F1], ALU.add)
                    v.tensor_copy(rows[:, :, 0:C], x[:])
                    v.drain()
                    for side in range(2):
                        for h in range(H):
                            v.tensor_tensor(prod[:], x[:], node_w[:, side, h, 0:C].unsqueeze(1).to_broadcast([P, NT, C]), ALU.mult)
                            v.drain()
                            v.tensor_reduce(score[:, side, h], prod[:], AX, ALU.add)
                            v.drain()
                    for h in range(H):
                        v.tensor_scalar(rows_a[:, :, h], score[:, 0, h], node_w[:, 0, h, C:C + 1], None, ALU.add)
                        v.tensor_scalar(rows[:, :, C + h], score[:, 1, h], const[:, h:h + 1], None, ALU.add)
                    v.drain().then_inc(tabled, 2)

                @block.gpsimd
                def _(pool):
                    pool.wait_ge(tabled, 2)
                    for table, target, k in ((rows, "spread1_d", "dst"), (rows_a, "spreada_d", "src")):
                        for i in range(NT):
                            pool.indirect_dma_start(g[target], bass.IndirectOffsetOnAxis(ap=g["start_idx"][k][:, i:i + 1], axis=0),
                                                    table[:, i], None, bounds_check=EP - 1, oob_is_err=False).then_inc(fetched, 16)
                    pool.wait_ge(saved, 32)
                    pool.indirect_dma_start(head[:], None, g["table1_d"],
                                            bass.IndirectOffsetOnAxis(ap=g["head_key"]["dst"][:], axis=0)).then_inc(fetched, 16)
                    pool.indirect_dma_start(head_a[:], None, g["tablea_d"],
                                            bass.IndirectOffsetOnAxis(ap=g["head_key"]["src"][:], axis=0)).then_inc(fetched, 16)
                    pool.wait_ge(fetched, 16 * (2 * NT + 2))

        T, NC = T1, L // T1
        with ExitStack() as stack:
            s = Space(nc, stack)
            W = C + H
            spread = s.sb("l1_spread", [P, 2, T, B1])
            attr = s.sb("l1_attr", [P, 2, T, D5])
            idx = s.sb("l1_idx", [P, 2, T], I32)
            data = s.sb("l1_data", [P, W, T + 1])
            keep = s.sb("l1_keep", [P, 2, W, T + 1])
            run = s.sb("l1_run", [P, 2, W, T + 1])
            rows = s.sb("l1_rows", [P, 2, T, R1])
            prod = s.sb("l1_prod", [P, T, H, D5])
            dot = s.sb("l1_dot", [P, T, H])
            two = lambda n: [sem(f"l1d_{n}{b}") for b in range(2)]
            loaded, used, keep_ready, scanned, filled, sent, scored, free = (two(n) for n in (
                "loaded", "used", "keep_ready", "scanned", "filled", "sent", "scored", "free"))
            set_up = sem("l1d_set_up")
            with nc.Block() as block:
                @block.sync
                def _(sp):
                    spread_v, attr_v = g["run_of"](g["spread1_d"], B1), g["run_of"](a["attr5"], D5)
                    with sp.Fori(0, NC // 2) as h:
                        for b in range(2):
                            c = h * 2 + b
                            wait(sp, used[b], h + 1)
                            wait(sp, keep_ready[b], h + 1)
                            wait(sp, free[b], h + 1)
                            sp.dma_start(spread[:, b].rearrange("p t w -> p (t w)"), spread_v[:, bass.ds(c * (T * B1), T * B1)]).then_inc(loaded[b], 16)
                            sp.dma_start(attr[:, b].rearrange("p t w -> p (t w)"), attr_v[:, bass.ds(c * (T * D5), T * D5)]).then_inc(loaded[b], 16)
                            sp.dma_start(idx[:, b], g["pos_d"][:, bass.ds(c * T, T)]).then_inc(loaded[b], 16)

                @block.scalar
                def _(act):
                    act.wait_ge(set_up, 1)
                    with act.Fori(0, NC // 2) as h:
                        for b in range(2):
                            wait(act, loaded[b], (h + 1) * 48)
                            wait(act, scanned[b], h + 1)
                            nc.scalar.activation(keep[:, b, :, 1:], spread[:, b, :, B1 - 1].unsqueeze(1).to_broadcast([P, W, T]),
                                                 ACT.Copy, bias=1.0, scale=-1.0).then_inc(keep_ready[b], 1)
                            wait(act, scanned[b], h + 2)
                            wait(act, free[b], h + 1)
                            nc.scalar.copy(rows[:, b, :, 0:C], run[:, b, 0:C, 1:].rearrange("p f t -> p t f"))
                            nc.scalar.copy(rows[:, b, :, C:C + D5], attr[:, b]).then_inc(filled[b], 1)

                @block.vector
                def _(v):
                    v.memset(keep[:], 0.0)
                    v.memset(rows[:], 1.0)
                    v.memset(run[:], 0.0)
                    v.drain()
                    v.tensor_copy(run[:, 1, :, T], head[:, 0:W])
                    for b in range(2):
                        v.sem_inc(used[b], 1)
                        v.sem_inc(keep_ready[b], 1)
                        v.sem_inc(scanned[b], 1)
                        v.sem_inc(free[b], 1)
                        v.sem_inc(filled[b], 1)
                    v.drain().then_inc(set_up, 1)
                    with v.Fori(0, NC // 2) as h:
                        for b in range(2):
                            wait(v, loaded[b], (h + 1) * 48)
                            v.tensor_copy(data[:, :, 1:], spread[:, b, :, 0:W].rearrange("p t f -> p f t"))
                            v.tensor_copy(data[:, :, 0:1], run[:, 1 - b, :, T:T + 1])
                            v.tensor_tensor(prod[:], attr[:, b].unsqueeze(2).to_broadcast([P, T, H, D5]),
                                            edge_w[:].unsqueeze(1).to_broadcast([P, T, H, D5]), ALU.mult)
                            v.drain().then_inc(used[b], 1)
                            v.tensor_reduce(dot[:], prod[:], AX, ALU.add)
                            wait(v, keep_ready[b], h + 2)
                            wait(v, filled[b], h + 1)
                            v.tensor_tensor_scan(run[:, b].rearrange("p f t -> p (f t)"), keep[:, b].rearrange("p f t -> p (f t)"),
                                                 data[:].rearrange("p f t -> p (f t)"), 0.0, ALU.mult, ALU.add).then_inc(scanned[b], 1)
                            wait(v, free[b], h + 1)
                            v.drain()
                            v.tensor_tensor(rows[:, b, :, F1:R1], run[:, b, C:W, 1:].rearrange("p f t -> p t f"), dot[:], ALU.add) \
                             .then_inc(scored[b], 1)

                @block.gpsimd
                def _(pool):
                    def scatter(h, b, first=False):
                        wait(pool, filled[b], h + 2)
                        wait(pool, scored[b], h + 1)
                        for t in range(T):
                            pool.indirect_dma_start(g["rows1_d"], bass.IndirectOffsetOnAxis(ap=idx[:, b, t:t + 1], axis=0),
                                                    rows[:, b, t], None).then_inc(sent[b], 16)
                            if t == T // 2 and not first:
                                wait(pool, sent[1 - b], (h + b) * (16 * T))
                                pool.sem_inc(free[1 - b], 1)
                    scatter(0, 0, True)
                    scatter(0, 1)
                    with pool.Fori(1, NC // 2) as h:
                        for b in range(2):
                            scatter(h, b)
                    for b in range(2):
                        pool.wait_ge(sent[b], 16 * T * (NC // 2))

        with ExitStack() as stack:
            s = Space(nc, stack)
            W = H * F1
            rows = s.sb("l1s_rows", [P, UNROLL, T, R1])
            side = s.sb("l1s_side", [P, UNROLL, T, H + 1])
            hold = s.sb("l1s_hold", [P, 2, H, T + 1])
            hold_data = s.sb("l1s_hold_data", [P, H, T + 1])
            hold_keep = s.sb("l1s_hold_keep", [P, H, T + 1])
            score = s.sb("l1s_score", [P, H, T + 1])
            leak = s.sb("l1s_leak", [P, H, T])
            soft = Softmax(s, "l1s", T, F1)
            outb = s.sb("l1s_out", [P, 2, T, W + H])
            two = lambda n: [sem(f"l1s_{n}{b}") for b in range(2)]
            loaded, used = ([sem(f"l1s_{n}{r}") for r in range(UNROLL)] for n in ("loaded", "used"))
            soft.semaphores(two)
            set_up = sem("l1s_set_up")
            with nc.Block() as block:
                @block.sync
                def _(sp):
                    rows_v, side_v = g["run_of"](g["rows1_d"], R1), g["run_of"](g["spreada_d"], H + 1)
                    for c in chunks(sp, NC):
                        wait(sp, used[c.r], c.g + 1)
                        sp.dma_start(rows[:, c.r].rearrange("p t w -> p (t w)"), rows_v[:, bass.ds(c.at * (T * R1), T * R1)]).then_inc(loaded[c.r], 16)
                        sp.dma_start(side[:, c.r].rearrange("p t w -> p (t w)"), side_v[:, bass.ds(c.at * (T * (H + 1)), T * (H + 1))]).then_inc(loaded[c.r], 16)

                @block.scalar
                def _(act):
                    act.wait_ge(set_up, 1)
                    soft.scalar_program(nc, act, NC, outb, g["run_of"](g["sums1_d"], W + H))

                @block.vector
                def _(v):
                    v.memset(hold[:], 0.0)
                    v.memset(hold_keep[:], 0.0)
                    v.drain()
                    v.tensor_copy(hold[:, 1, :, T], head_a[:, 0:H])
                    soft.start(v)
                    for r in range(UNROLL):
                        v.sem_inc(used[r], 1)
                    v.drain().then_inc(set_up, 1)

                    def scores(c):
                        b, r = c.b, c.r
                        wait(v, loaded[r], (c.g + 1) * 32)
                        start = side[:, r, :, H].unsqueeze(1).to_broadcast([P, H, T])
                        v.tensor_scalar(hold_keep[:, :, 1:], start, -1.0, 1.0, ALU.mult, ALU.add)
                        v.tensor_copy(hold_data[:, :, 1:], side[:, r, :, 0:H].rearrange("p t h -> p h t"))
                        v.tensor_copy(hold_data[:, :, 0:1], hold[:, 1 - b, :, T:T + 1])
                        v.drain()
                        v.tensor_tensor_scan(hold[:, b].rearrange("p h t -> p (h t)"), hold_keep[:].rearrange("p h t -> p (h t)"),
                                             hold_data[:].rearrange("p h t -> p (h t)"), 0.0, ALU.mult, ALU.add)
                        v.drain()
                        v.tensor_tensor(leak[:], hold[:, b, :, 1:], rows[:, r, :, F1:R1].rearrange("p t h -> p h t"), ALU.add)
                        v.drain()
                        v.scalar_tensor_tensor(out=score[:, :, 1:], in0=leak[:], scalar=0.2, in1=leak[:], op0=ALU.mult, op1=ALU.max)
                        soft.running_max(v, c, score, start)

                    def sums(c):
                        soft.sums(v, c, rows[:, c.r, :, 0:F1].rearrange("p t f -> p f t")).then_inc(used[c.r], 1)
                        soft.scan(v, c)

                    soft.vector_program(v, NC, scores, sums)
                    soft.keep_tail(v, tail)

        summed = collect_softmax(nc, sem, g, outer, "l1", "src", g["sums1_d"], tail, F1)
        with ExitStack() as stack:
            s = Space(nc, stack)
            out_w = s.sb("l1_out_w", [F1, H, C])
            bias = s.sb("l1_bias", [P, C])
            recip = s.sb("l1_recip", [P, NT, H])
            turned_s = s.sb("l1_turned", [F1, 2, H, P])
            work, stat = s.sb("l1_work", [P, NT, C]), s.sb("l1_stat", [P, 3, NT])
            acc = s.sb("l1_acc", [P, NT, C])
            turned = s.ps("l1_turned_ps", [P, 2, 512])
            made = s.ps("l1_made", [P, 2, 512])
            loaded, added, scaled, turned_ready, copied, made_ready, read = (sem(f"l1n_{n}") for n in (
                "loaded", "added", "scaled", "turned", "copied", "made", "read"))
            sems = sem("l1_centred"), sem("l1_rooted")
            with nc.Block() as block:
                @block.gpsimd
                def _(pool):
                    pool.dma_start(out_w[:], a["out1"]).then_inc(loaded, 16)
                    pool.dma_start(bias[:], a["bias1"].to_broadcast([P, C])).then_inc(added, 16)
                    pool.wait_ge(loaded, 16)
                    pool.dma_start(out_w[F1 - 1:F1], a["out1_bias"], accum_op=ALU.add).then_inc(added, 16)
                    pool.wait_ge(added, 32)

                @block.vector
                def _(v):
                    den = summed[:, :, 0:H * F1].rearrange("p t (h f) -> p t h f", h=H)[:, :, :, F1 - 1]
                    v.tensor_scalar(recip[:], den, 1e-16, float(H), ALU.add, ALU.mult)
                    v.drain()
                    v.reciprocal(recip[:], recip[:])
                    v.drain()
                    for h in range(H):
                        part = summed[:, :, h * F1:(h + 1) * F1]
                        v.tensor_tensor(part, part, recip[:, :, h].unsqueeze(2).to_broadcast([P, NT, F1]), ALU.mult)
                    v.drain().then_inc(scaled, 1)
                    v.wait_ge(added, 32)
                    v.tensor_tensor(acc[:], x[:], bias[:].unsqueeze(1).to_broadcast([P, NT, C]), ALU.add)
                    for i in range(NT):
                        v.wait_ge(made_ready, i + 1)
                        v.drain()
                        v.tensor_tensor(acc[:, i], acc[:, i], made[:, i % 2, 0:C], ALU.add).then_inc(read, 1)
                    v.drain()
                    normalise(nc, v, None, acc[:], x[:], work[:], stat, sems, 1)

                @block.scalar
                def _(act):
                    for i in range(NT):
                        act.wait_ge(turned_ready, i + 1)
                        if i >= 2:
                            act.wait_ge(made_ready, i - 1)
                        nc.scalar.copy(turned_s[:, i % 2].rearrange("f h e -> f (h e)"), turned[0:F1, i % 2, 0:H * P]).then_inc(copied, 1)
                    normalise(nc, None, act, None, None, None, stat, sems, 1)

                @block.tensor
                def _(pe):
                    pe.wait_ge(scaled, 1)
                    pe.wait_ge(added, 32)

                    def turn(i):
                        if i >= 2:
                            pe.wait_ge(copied, i - 1)
                        for h in range(H):
                            last = nc.tensor.transpose(turned[0:F1, i % 2, h * P:(h + 1) * P], summed[:, i, h * F1:(h + 1) * F1],
                                                       g["identity"][:])
                        last.then_inc(turned_ready, 1)
                    turn(0)
                    for i in range(NT):
                        if i + 1 < NT:
                            turn(i + 1)
                        pe.wait_ge(copied, i + 1)
                        if i >= 2:
                            pe.wait_ge(read, i - 1)
                        for h in range(H):
                            last = nc.tensor.matmul(made[:, i % 2, 0:C], turned_s[:, i % 2, h], out_w[:, h],
                                                    start=(h == 0), stop=(h == H - 1))
                        last.then_inc(made_ready, 1)


class Softmax:

    def __init__(self, s, name, T, F):
        self.T, self.F = T, F
        self.fresh = s.sb(f"{name}_fresh", [P, H, T + 1])
        self.top = s.sb(f"{name}_top", [P, 2, H, T + 1])
        self.arg = s.sb(f"{name}_arg", [P, 2, 2, H, T])
        self.exp = s.sb(f"{name}_exp", [P, 2, 2, H, T])
        self.scale = s.sb(f"{name}_scale", [P, 2, H, F, T + 1])
        self.data = s.sb(f"{name}_data", [P, H, F, T + 1])
        self.run = s.sb(f"{name}_run", [P, 2, H, F, T + 1])

    def semaphores(self, two):
        self.args_ready, self.exp_ready, self.scale_ready, self.scanned, self.copied, self.stored = (
            two(n) for n in ("args", "exp", "scale", "scanned", "copied", "stored"))

    def start(self, v):
        v.memset(self.fresh[:], -FAR)
        v.memset(self.top[:], -FAR)
        v.memset(self.scale[:], 0.0)
        v.memset(self.run[:], 0.0)
        for b in range(2):
            v.sem_inc(self.scanned[b], 1)
            v.sem_inc(self.copied[b], 1)
            v.sem_inc(self.exp_ready[b], 1)
            v.sem_inc(self.stored[b], 16)

    def running_max(self, v, c, score, start):
        T, h, b = self.T, c.h, c.b
        v.tensor_scalar(self.fresh[:, :, 1:], start, -FAR, None, ALU.mult)
        v.tensor_copy(score[:, :, 0:1], self.top[:, 1 - b, :, T:T + 1])
        wait(v, self.copied[b], h + 1)
        wait(v, self.exp_ready[b], h + 1)
        v.drain()
        v.tensor_tensor_scan(self.top[:, b].rearrange("p h t -> p (h t)"), self.fresh[:].rearrange("p h t -> p (h t)"),
                             score[:].rearrange("p h t -> p (h t)"), -FAR, ALU.add, ALU.max)
        v.drain()
        v.tensor_tensor(self.arg[:, b, 0], self.top[:, b, :, 0:T], self.fresh[:, :, 1:], ALU.add)
        v.tensor_tensor(self.arg[:, b, 1], score[:, :, 1:], self.top[:, b, :, 1:], ALU.subtract)
        v.drain()
        v.tensor_tensor(self.arg[:, b, 0], self.arg[:, b, 0], self.top[:, b, :, 1:], ALU.subtract).then_inc(self.args_ready[b], 1)

    def sums(self, v, c, rows):
        T, h, b = self.T, c.h, c.b
        wait(v, self.exp_ready[b], h + 2)
        for head in range(H):
            v.tensor_tensor(self.data[:, head, :, 1:], rows,
                            self.exp[:, b, 1, head].unsqueeze(1).to_broadcast([P, self.F, T]), ALU.mult)
        return v.drain()

    def scan(self, v, c):
        T, h, b = self.T, c.h, c.b
        v.tensor_copy(self.data[:, :, :, 0:1], self.run[:, 1 - b, :, :, T:T + 1])
        wait(v, self.scale_ready[b], h + 1)
        wait(v, self.copied[b], h + 1)
        v.drain()
        v.tensor_tensor_scan(self.run[:, b].rearrange("p h f t -> p (h f t)"), self.scale[:, b].rearrange("p h f t -> p (h f t)"),
                             self.data[:].rearrange("p h f t -> p (h f t)"), 0.0, ALU.mult, ALU.add).then_inc(self.scanned[b], 1)
        v.drain()

    def vector_program(self, v, count, scores, sums):
        chunks_ahead(v, count, scores, sums)

    def keep_tail(self, v, tail):
        T, W = self.T, H * self.F
        v.tensor_copy(tail[:, 0:W], self.run[:, 1].rearrange("p h f t -> p (h f) t")[:, :, T])
        v.tensor_copy(tail[:, W:W + H], self.top[:, 1, :, T])

    def scalar_program(self, nc, act, count, outb, sums_v, before=lambda c: None):
        T, W = self.T, H * self.F

        def exponentials(c):
            before(c)
            h, b = c.h, c.b
            wait(act, self.args_ready[b], h + 1)
            nc.scalar.activation(self.exp[:, b], self.arg[:, b], ACT.Exp).then_inc(self.exp_ready[b], 1)
            wait(act, self.exp_ready[b], h + 2)
            wait(act, self.scanned[b], h + 1)
            for head in range(H):
                last = nc.scalar.copy(self.scale[:, b, head, :, 1:], self.exp[:, b, 0, head].unsqueeze(1).to_broadcast([P, self.F, T]))
            last.then_inc(self.scale_ready[b], 1)

        def store(c):
            h, b = c.h, c.b
            wait(act, self.scanned[b], h + 2)
            wait(act, self.stored[b], (h + 1) * 16)
            nc.scalar.copy(outb[:, b, :, 0:W], self.run[:, b].rearrange("p h f t -> p (h f) t")[:, :, 1:].rearrange("p w t -> p t w"))
            nc.scalar.copy(outb[:, b, :, W:W + H], self.top[:, b, :, 1:].rearrange("p h t -> p t h")).then_inc(self.copied[b], 1)
            wait(act, self.copied[b], h + 2)
            wide = T * outb.shape[-1]
            act.dma_start(sums_v[:, bass.ds(c.at * wide, wide)], outb[:, b].rearrange("p t w -> p (t w)")).then_inc(self.stored[b], 16)

        chunks_ahead(act, count, exponentials, store)
        for b in range(2):
            act.wait_ge(self.stored[b], 16 * (count // 2 + 1))


def collect_softmax(nc, sem, g, outer, name, k, sums_d, tail, F):
    W = H * F
    total = Space(nc, outer).sb(f"{name}_total", [P, NT, W + H])
    with ExitStack() as stack:
        s = Space(nc, stack)
        masks = s.sb(f"{name}_masks", [P, NP])
        last_only = s.sb(f"{name}_last_only", [P, NP])
        spread_masks(nc, sem, g, k, name, masks, last_only)
        ones = s.sb(f"{name}_ones", [P, P])
        diag = s.sb(f"{name}_diag", [P, H + 1, P])
        other = s.sb(f"{name}_other", [P, P])
        pair = s.sb(f"{name}_pair", [P, H, P])
        top = s.sb(f"{name}_gtop", [P, H + 1])
        factor = s.sb(f"{name}_factor", [P, H])
        scaled = s.sb(f"{name}_scaled", [P, W])
        crossing = s.sb(f"{name}_crossing", [P, NT, H + 1])
        best = s.sb(f"{name}_best", [P, NT, H])
        args = s.sb(f"{name}_args", [P, 2, NT, H])
        exps = s.sb(f"{name}_exps", [P, 2, NT, H])
        wide = s.ps(f"{name}_wide", [P, 512])
        found = s.ps(f"{name}_found", [P, 512])
        more = s.ps(f"{name}_more", [P, 2, 512])
        got, read, mult, diag_ready, spread, arg_ready, exp_ready, top_ready, found_ready, tail_ready = (
            sem(f"{name}_s{n}") for n in ("got", "read", "mult", "diag", "spread", "arg", "exp", "top", "found", "tail"))
        with nc.Block() as block:
            @block.gpsimd
            def _(pool):
                for i in range(NT):
                    pool.indirect_dma_start(total[:, i], None, sums_d,
                                            bass.IndirectOffsetOnAxis(ap=g["end_idx"][k][:, i:i + 1], axis=0)).then_inc(got, 16)

            @block.tensor
            def _(pe):
                pe.wait_ge(diag_ready, 1)
                nc.tensor.matmul(wide[:, 0:(H + 1) * P], ones[:], diag[:].rearrange("p a q -> p (a q)"), start=True, stop=True).then_inc(spread, 1)
                pe.wait_ge(top_ready, 1)
                for i in range(NT):
                    last = nc.tensor.matmul(found[:, i * (H + 1):(i + 1) * (H + 1)], last_only[:, i * P:(i + 1) * P], top[:],
                                            start=True, stop=True)
                last.then_inc(found_ready, 1)
                pe.wait_ge(tail_ready, 1)
                for i in range(NT):
                    if i >= 2:
                        pe.wait_ge(read, i - 1)
                    nc.tensor.matmul(more[:, i % 2, 0:W], masks[:, i * P:(i + 1) * P], scaled[:], start=True, stop=True).then_inc(mult, 1)

            @block.scalar
            def _(act):
                act.wait_ge(arg_ready, 1)
                nc.scalar.activation(factor[:], factor[:], ACT.Exp).then_inc(exp_ready, 1)
                act.wait_ge(arg_ready, 2)
                nc.scalar.activation(exps[:], args[:], ACT.Exp).then_inc(exp_ready, 1)

            @block.vector
            def _(v):
                v.memset(ones[:], 1.0)
                v.memset(top[:], 1.0)
                ident = g["identity"]
                for j in range(H):
                    v.tensor_scalar(diag[:, j], ident[:], tail[:, W + j:W + j + 1], None, ALU.mult)
                v.tensor_scalar(diag[:, H], ident[:], g["tail_key"][k][:, 0:1], None, ALU.mult)
                v.drain().then_inc(diag_ready, 1)
                v.wait_ge(spread, 1)
                v.tensor_scalar(other[:], wide[:, H * P:(H + 1) * P], g["tail_key"][k][:, 0:1], None, ALU.is_equal)
                v.drain()
                v.tensor_scalar(other[:], other[:], FAR, -FAR, ALU.mult, ALU.add)
                v.drain()
                v.tensor_tensor(pair[:], wide[:, 0:H * P].rearrange("p (h q) -> p h q", h=H),
                                other[:].unsqueeze(1).to_broadcast([P, H, P]), ALU.add)
                v.drain()
                v.tensor_reduce(top[:, 0:H], pair[:], AX, ALU.max)
                v.drain().then_inc(top_ready, 1)
                v.tensor_tensor(factor[:], tail[:, W:W + H], top[:, 0:H], ALU.subtract)
                v.drain().then_inc(arg_ready, 1)
                v.wait_ge(exp_ready, 1)
                for h in range(H):
                    v.tensor_scalar(scaled[:, h * F:(h + 1) * F], tail[:, h * F:(h + 1) * F], factor[:, h:h + 1], None, ALU.mult)
                v.drain().then_inc(tail_ready, 1)
                v.wait_ge(found_ready, 1)
                v.tensor_copy(crossing[:].rearrange("p t a -> p (t a)"), found[:, 0:NT * (H + 1)])
                v.drain()
                v.tensor_scalar(crossing[:, :, H], crossing[:, :, H], FAR, -FAR, ALU.mult, ALU.add)
                v.drain()
                v.tensor_tensor(crossing[:, :, 0:H], crossing[:, :, 0:H], crossing[:, :, H].unsqueeze(2).to_broadcast([P, NT, H]), ALU.add)
                v.wait_ge(got, 16 * NT)
                v.drain()
                v.tensor_tensor(best[:], crossing[:, :, 0:H], total[:, :, W:W + H], ALU.max)
                v.drain()
                v.tensor_tensor(args[:, 0], total[:, :, W:W + H], best[:], ALU.subtract)
                v.tensor_tensor(args[:, 1], crossing[:, :, 0:H], best[:], ALU.subtract)
                v.drain().then_inc(arg_ready, 1)
                v.wait_ge(exp_ready, 2)
                v.tensor_tensor(exps[:, 0], exps[:, 0], g["filled"][k][:].unsqueeze(2).to_broadcast([P, NT, H]), ALU.mult)
                v.drain()
                for h in range(H):
                    part = total[:, :, h * F:(h + 1) * F]
                    v.tensor_tensor(part, part, exps[:, 0, :, h].unsqueeze(2).to_broadcast([P, NT, F]), ALU.mult)
                v.drain()
                for i in range(NT):
                    v.wait_ge(mult, i + 1)
                    for h in range(H):
                        last = v.scalar_tensor_tensor(out=total[:, i, h * F:(h + 1) * F], in0=more[:, i % 2, h * F:(h + 1) * F],
                                                      scalar=exps[:, 1, i, h:h + 1], in1=total[:, i, h * F:(h + 1) * F],
                                                      op0=ALU.mult, op1=ALU.add)
                    last.then_inc(read, 1)
    return total


class Pipeline:

    def __init__(self, sem, name, stages):
        self.stages = stages
        self.made = [sem(f"{name}_made{k}") for k in range(stages)]
        self.brought = [sem(f"{name}_brought{k}") for k in range(stages)]

    def tensor(self, pe, work):
        for step in range(NT + self.stages - 1):
            for k in reversed(range(self.stages)):
                i = step - k
                if not 0 <= i < NT:
                    continue
                if k:
                    pe.wait_ge(self.brought[k - 1], i + 1)
                if i >= 2:
                    pe.wait_ge(self.brought[k], i - 1)
                work[k](i).then_inc(self.made[k], 1)

    def scalar(self, act, work):
        last = self.stages - 1
        for step in range(NT + last - 1):
            for k in reversed(range(last)):
                i = step - k
                if not 0 <= i < NT:
                    continue
                act.wait_ge(self.made[k], i + 1)
                if i >= 2:
                    act.wait_ge(self.made[k + 1], i - 1)
                work[k](i).then_inc(self.brought[k], 1)

    def vector(self, v, work):
        for i in range(NT):
            v.wait_ge(self.made[-1], i + 1)
            work(i).then_inc(self.brought[-1], 1)


def layer2(nc, a, sem, g):
    x = g["x"]
    ident = g["identity"]
    with ExitStack() as outer:
        s0 = Space(nc, outer)
        tail = s0.sb("l2_tail", [P, H * F2 + H])
        head = s0.sb("l2_head", [P, B2])
        with ExitStack() as stack:
            s = Space(nc, stack)
            hidden = s.sb("l2_hidden", [P, NT, C])
            work, stat = s.sb("l2_work", [P, NT, C]), s.sb("l2_stat", [P, 3, NT])
            gain, shift = s.sb("l2_gain", [P, C]), s.sb("l2_shift", [P, C])
            wq, bq, keys = s.sb("l2_wq", [C, H * C]), s.sb("l2_bq", [H * C, 1]), s.sb("l2_keys", [H * C, H * F2])
            bq8 = s.sb("l2_bq8", [H * C, 1])
            rows = s.sb("l2_node_rows", [P, NT, B2])
            hid_t, query_t = s.sb("l2_hid_t", [C, 2, P]), s.sb("l2_query_t", [H * C, 2, P])
            ps_a, ps_b, ps_c = s.ps("l2_psa", [P, 2, 512]), s.ps("l2_psb", [P, 2, 512]), s.ps("l2_psc", [P, 2, 512])
            loaded, ready, saved, spread, fetched, scaled, tabled = (sem(f"l2a_{n}") for n in (
                "loaded", "ready", "saved", "spread", "fetched", "scaled", "tabled"))
            sems = sem("l2a_centred"), sem("l2a_rooted")
            pipe = Pipeline(sem, "l2a", 3)
            inv = float(C) ** -0.5
            with nc.Block() as block:
                @block.sync
                def _(sp):
                    sp.dma_start(gain[:], a["ln1_g"].to_broadcast([P, C])).then_inc(loaded, 16)
                    sp.dma_start(shift[:], a["ln1_b"].to_broadcast([P, C])).then_inc(loaded, 16)
                    sp.dma_start(wq[:], a["wq"]).then_inc(loaded, 16)
                    sp.dma_start(bq[:], a["bq"]).then_inc(loaded, 16)
                    sp.dma_start(keys[:], a["keys2"]).then_inc(loaded, 16)
                    sp.wait_ge(ready, 1)
                    sp.dma_start(g["h2_d"].rearrange("(t p) w -> p t w", p=P), hidden[:]).then_inc(saved, 16)
                    sp.wait_ge(tabled, 1)
                    sp.dma_start(g["table2_d"].rearrange("(t p) w -> p t w", p=P), rows[:]).then_inc(saved, 16)
                    sp.wait_ge(saved, 32)

                @block.vector
                def _(v):
                    v.wait_ge(loaded, 80)
                    v.memset(rows[:, :, H * F2:B2], 1.0)
                    v.tensor_scalar(bq8[:], bq[:], inv, None, ALU.mult)
                    v.tensor_copy(work[:], x[:])
                    v.drain().then_inc(scaled, 1)
                    normalise(nc, v, None, work[:], hidden[:], hidden[:], stat, sems, 1, gain, shift)
                    v.drain().then_inc(ready, 1)
                    pipe.vector(v, lambda i: v.tensor_copy(rows[:, i, 0:H * F2], ps_c[:, i % 2, 0:H * F2]))
                    v.drain().then_inc(tabled, 1)

                @block.scalar
                def _(act):
                    normalise(nc, None, act, None, None, None, stat, sems, 1)
                    act.wait_ge(scaled, 1)
                    pipe.scalar(act, [
                        lambda i: nc.scalar.copy(hid_t[:, i % 2], ps_a[0:C, i % 2, 0:P]),
                        lambda i: nc.scalar.activation(query_t[:, i % 2], ps_b[:, i % 2, 0:P], ACT.Identity, bias=bq8[:, 0:1], scale=inv)])

                @block.tensor
                def _(pe):
                    pe.wait_ge(ready, 1)
                    pipe.tensor(pe, [
                        lambda i: nc.tensor.transpose(ps_a[0:C, i % 2, 0:P], hidden[:, i], ident[:]),
                        lambda i: nc.tensor.matmul(ps_b[:, i % 2, 0:P], wq[:], hid_t[:, i % 2], start=True, stop=True),
                        lambda i: nc.tensor.matmul(ps_c[:, i % 2, 0:H * F2], query_t[:, i % 2], keys[:], start=True, stop=True)])

                @block.gpsimd
                def _(pool):
                    pool.wait_ge(tabled, 1)
                    for i in range(NT):
                        pool.indirect_dma_start(g["spread2_d"], bass.IndirectOffsetOnAxis(ap=g["start_idx"]["dst"][:, i:i + 1], axis=0),
                                                rows[:, i], None, bounds_check=EP - 1, oob_is_err=False).then_inc(spread, 16)
                    pool.wait_ge(saved, 32)
                    pool.indirect_dma_start(head[:], None, g["table2_d"],
                                            bass.IndirectOffsetOnAxis(ap=g["head_key"]["dst"][:], axis=0)).then_inc(fetched, 16)
                    pool.wait_ge(spread, 16 * NT)
                    pool.wait_ge(fetched, 16)

        T, NC, W = T2, L // T2, H * F2
        with ExitStack() as stack:
            s = Space(nc, stack)
            spread = s.sb("l2_spread", [P, 2, T, B2])
            rows = s.sb("l2_rows", [P, UNROLL, T, F2])
            idx = s.sb("l2_idx", [P, UNROLL, T], I32)
            hold_data = s.sb("l2_hold_data", [P, H, F2, T + 1])
            hold_keep = s.sb("l2_hold_keep", [P, 2, W, T + 1])
            hold = s.sb("l2_hold", [P, H, F2, T + 1])
            prod = s.sb("l2_prod", [P, H, F2, T])
            score = s.sb("l2_score", [P, H, T + 1])
            soft = Softmax(s, "l2s", T, F2)
            outb = s.sb("l2_out", [P, 2, T, W + H])
            two = lambda n: [sem(f"l2_{n}{b}") for b in range(2)]
            four = lambda n: [sem(f"l2_{n}{b}") for b in range(UNROLL)]
            spread_in, spread_used, keep_ready = two("spread_in"), two("spread_used"), two("keep_ready")
            loaded, idx_in, got, used = four("loaded"), four("idx_in"), four("got"), four("used")
            soft.semaphores(two)
            set_up = sem("l2_set_up")
            with nc.Block() as block:
                @block.sync
                def _(sp):
                    spread_v, attr_v, src_v = g["run_of"](g["spread2_d"], B2), a["attr32"].rearrange("(p l) w -> p l w", p=P), g["run_of"](a["src"], 0)
                    for c in chunks(sp, NC):
                        wait(sp, used[c.r], c.g + 1)
                        sp.dma_start(idx[:, c.r], src_v[:, bass.ds(c.at * T, T)]).then_inc(idx_in[c.r], 16)
                        sp.dma_start(rows[:, c.r, :, C:C + D32], attr_v[:, bass.ds(c.at * T, T)]).then_inc(loaded[c.r], 16)
                        wait(sp, spread_used[c.b], c.h + 1)
                        sp.dma_start(spread[:, c.b].rearrange("p t w -> p (t w)"), spread_v[:, bass.ds(c.at * (T * B2), T * B2)]).then_inc(spread_in[c.b], 16)

                @block.gpsimd
                def _(pool):
                    for c in chunks(pool, NC):
                        wait(pool, idx_in[c.r], (c.g + 1) * 16)
                        for t in range(T):
                            pool.indirect_dma_start(rows[:, c.r, t, 0:C], None, g["h2_d"],
                                                    bass.IndirectOffsetOnAxis(ap=idx[:, c.r, t:t + 1], axis=0)).then_inc(got[c.r], 16)

                @block.scalar
                def _(act):
                    act.wait_ge(set_up, 1)

                    def keep(c):
                        wait(act, spread_in[c.b], (c.h + 1) * 16)
                        nc.scalar.activation(hold_keep[:, c.b, :, 1:], spread[:, c.b, :, W].unsqueeze(1).to_broadcast([P, W, T]),
                                             ACT.Copy, bias=1.0, scale=-1.0).then_inc(keep_ready[c.b], 1)
                    soft.scalar_program(nc, act, NC, outb, g["run_of"](g["sums2_d"], W + H), keep)

                @block.vector
                def _(v):
                    v.memset(hold_keep[:], 0.0)
                    v.memset(rows[:, :, :, F2 - 1:F2], 1.0)
                    v.tensor_copy(hold[:].rearrange("p h f t -> p (h f) t")[:, :, T], head[:, 0:W])
                    soft.start(v)
                    for b in range(2):
                        v.sem_inc(spread_used[b], 1)
                    for r in range(UNROLL):
                        v.sem_inc(used[r], 1)
                    v.drain().then_inc(set_up, 1)

                    def scores(c):
                        b = c.b
                        start = spread[:, b, :, W].unsqueeze(1).to_broadcast([P, H, T])
                        wait(v, spread_in[b], (c.h + 1) * 16)
                        v.tensor_copy(hold_data[:].rearrange("p h f t -> p (h f) t")[:, :, 1:], spread[:, b, :, 0:W].rearrange("p t w -> p w t"))
                        v.tensor_copy(hold_data[:, :, :, 0:1], hold[:, :, :, T:T + 1])
                        wait(v, keep_ready[b], c.h + 1)
                        v.drain()
                        v.tensor_tensor_scan(hold[:].rearrange("p h f t -> p (h f t)"), hold_keep[:, b].rearrange("p w t -> p (w t)"),
                                             hold_data[:].rearrange("p h f t -> p (h f t)"), 0.0, ALU.mult, ALU.add)
                        wait(v, loaded[c.r], (c.g + 1) * 16)
                        wait(v, got[c.r], (c.g + 1) * (16 * T))
                        v.drain()
                        for h in range(H):
                            v.tensor_tensor(prod[:, h], hold[:, h, :, 1:], rows[:, c.r].rearrange("p t f -> p f t"), ALU.mult)
                        v.drain()
                        v.tensor_reduce(score[:, :, 1:], prod[:].rearrange("p h f t -> p h t f"), AX, ALU.add)
                        soft.running_max(v, c, score, start)
                        v.drain().then_inc(spread_used[b], 1)

                    def sums(c):
                        soft.sums(v, c, rows[:, c.r].rearrange("p t f -> p f t")).then_inc(used[c.r], 1)
                        soft.scan(v, c)

                    soft.vector_program(v, NC, scores, sums)
                    soft.keep_tail(v, tail)

        summed = collect_softmax(nc, sem, g, outer, "l2", "dst", g["sums2_d"], tail, F2)
        with ExitStack() as stack:
            s = Space(nc, stack)
            vals, wp = s.sb("l2_vals", [F2, H, C]), s.sb("l2_wp", [C, H, C])
            w1, w2, b1 = s.sb("l2_w1", [C, C]), s.sb("l2_w2", [C, C]), s.sb("l2_b1", [C, 1])
            bp, b2 = s.sb("l2_bp", [P, C]), s.sb("l2_b2", [P, C])
            gain, shift = s.sb("l2_gain2", [P, C]), s.sb("l2_shift2", [P, C])
            recip = s.sb("l2_recip", [P, NT, H])
            res, acc, hidden = s.sb("l2_res", [P, NT, C]), s.sb("l2_acc", [P, NT, C]), s.sb("l2_hidden2", [P, NT, C])
            stat = s.sb("l2_stat2", [P, 3, NT])
            sum_t, mean_t = s.sb("l2_sum_t", [F2, 2, H, P]), s.sb("l2_mean_t", [C, 2, H, P])
            ps_a, ps_b, ps_c = s.ps("l2_psd", [P, 2, 512]), s.ps("l2_pse", [P, 2, 512]), s.ps("l2_psf", [P, 2, 512])
            loaded, scaled, ready = (sem(f"l2c_{n}") for n in ("loaded", "scaled", "ready"))
            sems = sem("l2c_centred"), sem("l2c_rooted")
            pipe, mlp = Pipeline(sem, "l2c", 3), Pipeline(sem, "l2m", 3)
            loads = [(vals, a["values2"]), (wp, a["wp"]), (w1, a["w1"]), (w2, a["w2"]), (b1, a["b1"])] + [
                (t, a[k].to_broadcast([P, C])) for t, k in ((bp, "bp"), (b2, "b2"), (gain, "ln2_g"), (shift, "ln2_b"))]
            with nc.Block() as block:
                @block.sync
                def _(sp):
                    for t, of in loads:
                        sp.dma_start(t[:], of).then_inc(loaded, 16)

                @block.vector
                def _(v):
                    den = summed[:, :, 0:H * F2].rearrange("p t (h f) -> p t h f", h=H)[:, :, :, F2 - 1]
                    v.tensor_scalar(recip[:], den, 1e-8, None, ALU.add)
                    v.drain()
                    v.reciprocal(recip[:], recip[:])
                    v.drain()
                    for h in range(H):
                        part = summed[:, :, h * F2:(h + 1) * F2]
                        v.tensor_tensor(part, part, recip[:, :, h].unsqueeze(2).to_broadcast([P, NT, F2]), ALU.mult)
                    v.drain().then_inc(scaled, 1)
                    v.wait_ge(loaded, 16 * len(loads))
                    v.tensor_tensor(res[:], x[:], bp[:].unsqueeze(1).to_broadcast([P, NT, C]), ALU.add)
                    v.drain()
                    pipe.vector(v, lambda i: v.tensor_tensor(res[:, i], res[:, i], ps_c[:, i % 2, 0:C], ALU.add))
                    v.drain()
                    v.tensor_copy(acc[:], res[:])
                    v.drain()
                    normalise(nc, v, None, acc[:], hidden[:], hidden[:], stat, sems, 1, gain, shift)
                    v.tensor_tensor(acc[:], x[:], res[:], ALU.add)
                    v.drain()
                    v.tensor_tensor(acc[:], acc[:], b2[:].unsqueeze(1).to_broadcast([P, NT, C]), ALU.add)
                    v.drain().then_inc(ready, 1)
                    mlp.vector(v, lambda i: v.tensor_tensor(acc[:, i], acc[:, i], ps_c[:, i % 2, C:2 * C], ALU.add))
                    v.drain()
                    normalise(nc, v, None, acc[:], x[:], res[:], stat, sems, 2)

                @block.scalar
                def _(act):
                    act.wait_ge(loaded, 16 * len(loads))
                    pipe.scalar(act, [
                        lambda i: nc.scalar.copy(sum_t[:, i % 2].rearrange("f h e -> f (h e)"), ps_a[0:F2, i % 2, 0:H * P]),
                        lambda i: nc.scalar.copy(mean_t[:, i % 2].rearrange("f h e -> f (h e)"), ps_b[0:C, i % 2, 0:H * P])])
                    normalise(nc, None, act, None, None, None, stat, sems, 1)
                    mlp.scalar(act, [
                        lambda i: nc.scalar.copy(mean_t[:, i % 2, 0], ps_a[0:C, i % 2, 256:256 + P]),
                        lambda i: nc.scalar.activation(mean_t[:, i % 2, 1], ps_b[0:C, i % 2, 256:256 + P], ACT.Gelu, bias=b1[:, 0:1])])
                    normalise(nc, None, act, None, None, None, stat, sems, 2)

                @block.tensor
                def _(pe):
                    def turn(i):
                        for h in range(H):
                            last = nc.tensor.transpose(ps_a[0:F2, i % 2, h * P:(h + 1) * P], summed[:, i, h * F2:(h + 1) * F2], ident[:])
                        return last

                    def means(i):
                        for h in range(H):
                            last = nc.tensor.matmul(ps_b[0:C, i % 2, h * P:(h + 1) * P], vals[:, h], sum_t[:, i % 2, h], start=True, stop=True)
                        return last

                    def project(i):
                        for h in range(H):
                            last = nc.tensor.matmul(ps_c[:, i % 2, 0:C], mean_t[:, i % 2, h], wp[:, h], start=(h == 0), stop=(h == H - 1))
                        return last
                    pe.wait_ge(loaded, 16 * len(loads))
                    pe.wait_ge(scaled, 1)
                    pipe.tensor(pe, [turn, means, project])
                    pe.wait_ge(ready, 1)
                    mlp.tensor(pe, [
                        lambda i: nc.tensor.transpose(ps_a[0:C, i % 2, 256:256 + P], hidden[:, i], ident[:]),
                        lambda i: nc.tensor.matmul(ps_b[0:C, i % 2, 256:256 + P], w1[:], mean_t[:, i % 2, 0], start=True, stop=True),
                        lambda i: nc.tensor.matmul(ps_c[:, i % 2, C:2 * C], mean_t[:, i % 2, 1], w2[:], start=True, stop=True)])


def layer3(nc, a, sem, g, out):
    x = g["x"]
    ident = g["identity"]
    T, NC = T2, L // T2
    with ExitStack() as outer:
        s0 = Space(nc, outer)
        tail = s0.sb("l3_tail", [P, C])
        rooted_x = s0.sb("l3_rooted_x", [P, NT, C])
        with ExitStack() as stack:
            s = Space(nc, stack)
            spline, root = s.sb("l3_spline", [C, S3 * C]), s.sb("l3_root", [C, C])
            x_t = s.sb("l3_x_t", [C, 2, P])
            row = s.sb("l3_row", [P, 2, S3 * C])
            ps_a, ps_b, ps_c = s.ps("l3_psa", [P, 2, 512]), s.ps("l3_psb", [P, 2, 512]), s.ps("l3_psc", [P, 2, 512])
            loaded, made, brought, tabled, copied, read = (sem(f"l3a_{n}") for n in ("loaded", "made", "brought", "tabled", "copied", "read"))
            stored = [sem(f"l3a_stored{b}") for b in range(2)]
            with nc.Block() as block:
                @block.sync
                def _(sp):
                    sp.dma_start(spline[:], a["spline"]).then_inc(loaded, 16)
                    sp.dma_start(root[:], a["root"]).then_inc(loaded, 16)
                    for i in range(NT):
                        sp.wait_ge(copied, i + 1)
                        sp.dma_start(g["table3_d"][i * P:(i + 1) * P], row[:, i % 2]).then_inc(stored[i % 2], 16)
                    sp.wait_ge(stored[0], 16 * ((NT + 1) // 2))
                    sp.wait_ge(stored[1], 16 * (NT // 2))

                @block.tensor
                def _(pe):
                    pe.wait_ge(loaded, 32)

                    def turn(i):
                        if i >= 2:
                            pe.wait_ge(brought, i - 1)
                        nc.tensor.transpose(ps_a[0:C, i % 2, 0:P], x[:, i], ident[:]).then_inc(made, 1)
                    turn(0)
                    for i in range(NT):
                        if i + 1 < NT:
                            turn(i + 1)
                        pe.wait_ge(brought, i + 1)
                        if i >= 2:
                            pe.wait_ge(copied, i - 1)
                            pe.wait_ge(read, i - 1)
                        nc.tensor.matmul(ps_b[:, i % 2], x_t[:, i % 2], spline[:], start=True, stop=True)
                        nc.tensor.matmul(ps_c[:, i % 2, 0:C], x_t[:, i % 2], root[:], start=True, stop=True).then_inc(tabled, 1)

                @block.scalar
                def _(act):
                    for i in range(NT):
                        act.wait_ge(made, i + 1)
                        if i >= 2:
                            act.wait_ge(tabled, i - 1)
                        nc.scalar.copy(x_t[:, i % 2], ps_a[0:C, i % 2, 0:P]).then_inc(brought, 1)
                        if i >= 1:
                            act.wait_ge(tabled, i)
                            nc.scalar.copy(rooted_x[:, i - 1], ps_c[:, (i - 1) % 2, 0:C]).then_inc(read, 1)
                    act.wait_ge(tabled, NT)
                    nc.scalar.copy(rooted_x[:, NT - 1], ps_c[:, (NT - 1) % 2, 0:C]).then_inc(read, 1)

                @block.vector
                def _(v):
                    for i in range(NT):
                        v.wait_ge(tabled, i + 1)
                        if i >= 2:
                            v.wait_ge(stored[i % 2], 16 * (i // 2))
                        v.tensor_copy(row[:, i % 2], ps_b[:, i % 2]).then_inc(copied, 1)

        with ExitStack() as stack:
            s = Space(nc, stack)
            idx = s.sb("l3_idx", [P, 2, T], I32)
            rows = s.sb("l3_rows", [P, 2, T, S3 * C])
            data = s.sb("l3_data", [P, C, T + 1])
            keep = s.sb("l3_keep", [P, 2, C, T + 1])
            run = s.sb("l3_run", [P, 2, C, T + 1])
            outb = s.sb("l3_out", [P, 2, T, C])
            frac = s.sb("l3_frac", [P, L * D3])
            bits = s.sb("l3_bits", [P, T, D3, 2])
            pairs = s.sb("l3_pairs", [P, T, 2, 2])
            basis = s.sb("l3_basis", [P, T, S3])
            keys, prev, same = s.sb("l3_keys", [P, L], I32), s.sb("l3_prev", [P, L], I32), s.sb("l3_same", [P, L])
            two = lambda n: [sem(f"l3_{n}{b}") for b in range(2)]
            idx_in, got, rows_used, keep_ready, scanned, copied, stored = (two(n) for n in (
                "idx_in", "got", "rows_used", "keep_ready", "scanned", "copied", "stored"))
            loaded, flags = sem("l3_loaded"), sem("l3_flags")
            with nc.Block() as block:
                @block.sync
                def _(sp):
                    sp.dma_start(frac[:], g["run_of"](a["attr3"], D3)).then_inc(loaded, 16)
                    sp.dma_start(keys[:], g["run_of"](a["dst"], 0)).then_inc(loaded, 16)
                    sp.dma_start(prev[:], g["run_of"](a["dst_before"], 0)).then_inc(loaded, 16)
                    src = g["run_of"](a["src"], 0)
                    with sp.Fori(0, NC // 2) as h:
                        for b in range(2):
                            wait(sp, rows_used[b], h + 1)
                            sp.dma_start(idx[:, b], src[:, bass.ds((h * 2 + b) * T, T)]).then_inc(idx_in[b], 16)

                @block.gpsimd
                def _(pool):
                    with pool.Fori(0, NC // 2) as h:
                        for b in range(2):
                            wait(pool, idx_in[b], (h + 1) * 16)
                            for t in range(T):
                                pool.indirect_dma_start(rows[:, b, t], None, g["table3_d"],
                                                        bass.IndirectOffsetOnAxis(ap=idx[:, b, t:t + 1], axis=0)) \
                                    .then_inc(got[b], 16)

                @block.vector
                def _(v):
                    v.memset(run[:], 0.0)
                    v.memset(keep[:], 0.0)
                    v.sem_inc(rows_used[0], 1)
                    v.sem_inc(rows_used[1], 1)
                    v.wait_ge(loaded, 48)
                    v.tensor_tensor(same[:], keys[:], prev[:], ALU.is_equal)
                    v.tensor_scalar(frac[:], frac[:], 0.0, 1.0, ALU.max, ALU.min)
                    v.drain().then_inc(flags, 1)
                    with v.Fori(0, NC // 2) as h:
                        for b in range(2):
                            c = h * 2 + b
                            up = frac[:, bass.ds(c * (T * D3), T * D3)].rearrange("p (t d) -> p t d", d=D3)
                            v.tensor_scalar(bits[:, :, :, 0], up, -1.0, 1.0, ALU.mult, ALU.add)
                            v.tensor_copy(bits[:, :, :, 1], up)
                            v.drain()
                            v.tensor_tensor(pairs[:], bits[:, :, 1].unsqueeze(3).to_broadcast([P, T, 2, 2]),
                                            bits[:, :, 0].unsqueeze(2).to_broadcast([P, T, 2, 2]), ALU.mult)
                            v.drain()
                            v.tensor_tensor(basis[:].rearrange("p t (k j) -> p t k j", k=2),
                                            bits[:, :, 2].unsqueeze(3).to_broadcast([P, T, 2, 4]),
                                            pairs[:].rearrange("p t k j -> p t (k j)").unsqueeze(2).to_broadcast([P, T, 2, 4]), ALU.mult)
                            wait(v, got[b], (h + 1) * (16 * T))
                            v.drain()
                            r4 = rows[:, b].rearrange("p t (s f) -> p (t s) f", s=S3)
                            v.tensor_tensor(r4, r4, basis[:].rearrange("p t s -> p (t s)").unsqueeze(2).to_broadcast([P, T * S3, C]), ALU.mult)
                            v.drain()
                            v.tensor_reduce(data[:, :, 1:].rearrange("p f t -> p t f"), rows[:, b].rearrange("p t (s f) -> p t f s", s=S3),
                                            AX, ALU.add).then_inc(rows_used[b], 1)
                            v.tensor_copy(data[:, :, 0:1], run[:, 1 - b, :, T:T + 1])
                            wait(v, keep_ready[b], h + 1)
                            wait(v, copied[b], h + 1)
                            v.drain()
                            v.tensor_tensor_scan(run[:, b].rearrange("p f t -> p (f t)"),
                                                 keep[:, b].rearrange("p f t -> p (f t)"),
                                                 data[:].rearrange("p f t -> p (f t)"), 0.0, ALU.mult, ALU.add) \
                             .then_inc(scanned[b], 1)
                            v.drain()
                    v.tensor_copy(tail[:], run[:, 1, :, T])

                @block.scalar
                def _(act):
                    act.wait_ge(flags, 1)
                    for b in range(2):
                        act.sem_inc(copied[b], 1)
                        act.sem_inc(stored[b], 16)
                        act.sem_inc(scanned[b], 1)
                    with act.Fori(0, NC // 2) as h:
                        for b in range(2):
                            wait(act, scanned[b], h + 1)
                            at = bass.ds((h * 2 + b) * T, T)
                            nc.scalar.copy(keep[:, b, :, 1:], same[:, at].unsqueeze(1).to_broadcast([P, C, T])) \
                              .then_inc(keep_ready[b], 1)
                            wait(act, scanned[b], h + 2)
                            wait(act, stored[b], (h + 1) * 16)
                            nc.scalar.copy(outb[:, b], run[:, b, :, 1:].rearrange("p f t -> p t f")).then_inc(copied[b], 1)
                            wait(act, copied[b], h + 2)
                            act.dma_start(g["run_of"](g["sums3_d"], C)[:, bass.ds((h * 2 + b) * (T * C), T * C)],
                                          outb[:, b].rearrange("p t f -> p (t f)")).then_inc(stored[b], 16)
                    for b in range(2):
                        act.wait_ge(stored[b], 16 * (NC // 2 + 1))

        total = collect_sums(nc, sem, g, outer, "l3", g["sums3_d"], tail)
        with ExitStack() as stack:
            s = Space(nc, stack)
            valid = s.sb("l3_valid", [P, NT])
            part = s.sb("l3_part", [P, C])
            moment = s.sb("l3_moment", [P, 2, C])
            deviation = s.sb("l3_deviation", [P, C])
            gamma, beta = s.sb("l3_gamma", [P, C]), s.sb("l3_beta", [P, C])
            ones = s.sb("l3_ones", [P, P])
            recip = s.sb("l3_recip", [P, NT])
            work, work2, stat = s.sb("l3_work", [P, NT, C]), s.sb("l3_work2", [P, NT, C]), s.sb("l3_stat", [P, 3, NT])
            summed = s.ps("l3_summed", [P, 2, 512])
            loaded, parted, added, ready, rooted_, low, high, done, finished = (sem(f"l3c_{n}") for n in (
                "loaded", "parted", "added", "ready", "rooted", "low", "high", "done", "finished"))
            sems = sem("l3c_centred"), sem("l3c_rooted_")
            with nc.Block() as block:
                @block.sync
                def _(sp):
                    sp.dma_start(gamma[:], a["gamma"].to_broadcast([P, C])).then_inc(loaded, 16)
                    sp.dma_start(beta[:], a["beta"].to_broadcast([P, C])).then_inc(loaded, 16)
                    sp.wait_ge(finished, 1)
                    sp.dma_start(out[0:NP - P].rearrange("(t p) c -> p t c", p=P), x[:, 0:NT - 1]).then_inc(done, 16)
                    sp.dma_start(out[NP - P:N], x[0:N - (NP - P), NT - 1]).then_inc(done, 16)
                    sp.wait_ge(done, 32)

                @block.tensor
                def _(pe):
                    for n in range(2):
                        pe.wait_ge(parted, n + 1)
                        nc.tensor.matmul(summed[:, n, 0:C], ones[:], part[:], start=True, stop=True).then_inc(added, 1)

                @block.vector
                def _(v):
                    over_tiles = lambda t: t[:].unsqueeze(1).to_broadcast([P, NT, C])
                    over_features = lambda t: t.unsqueeze(2).to_broadcast([P, NT, C])
                    v.memset(ones[:], 1.0)
                    v.memset(valid[:], 1.0)
                    v.tensor_scalar(recip[:], g["degree"][:], 1.0, None, ALU.max)
                    v.drain()
                    v.tensor_scalar(valid[:, NT - 1:NT], g["run_end"][:], float((N - (NP - P)) * L), None, ALU.is_le)
                    v.reciprocal(recip[:], recip[:])
                    v.drain()
                    v.tensor_tensor(total[:], total[:], over_features(recip[:]), ALU.mult)
                    v.drain()
                    v.tensor_tensor(total[:], total[:], rooted_x[:], ALU.add)
                    v.drain()
                    for n in range(2):
                        if n:
                            v.tensor_tensor(work[:], total[:], total[:], ALU.mult)
                            v.drain()
                        v.tensor_tensor(work[:], work[:] if n else total[:], over_features(valid[:]), ALU.mult)
                        v.drain()
                        v.tensor_reduce(part[:], work[:].rearrange("p t c -> p c t"), AX, ALU.add)
                        v.drain().then_inc(parted, 1)
                        v.wait_ge(added, n + 1)
                        v.tensor_scalar(moment[:, n], summed[:, n, 0:C], 1.0 / N, LN_EPS * n, ALU.mult, ALU.add)
                        v.drain()
                        if n == 0:
                            v.tensor_tensor(total[:], total[:], moment[:, 0].unsqueeze(1).to_broadcast([P, NT, C]), ALU.subtract)
                            v.drain()
                    v.drain().then_inc(ready, 1)
                    v.wait_ge(rooted_, 1)
                    v.reciprocal(deviation[:], deviation[:])
                    v.wait_ge(loaded, 32)
                    v.drain()
                    v.tensor_tensor(deviation[:], deviation[:], gamma[:], ALU.mult)
                    v.drain()
                    v.tensor_tensor(total[:], total[:], over_tiles(deviation), ALU.mult)
                    v.drain()
                    v.tensor_tensor(total[:], total[:], over_tiles(beta), ALU.add)
                    v.drain()
                    v.tensor_scalar(work[:], total[:], 0.0, None, ALU.min)
                    v.drain().then_inc(low, 1)
                    v.tensor_scalar(total[:], total[:], 0.0, -1.0, ALU.max, ALU.add)
                    v.drain()
                    v.tensor_tensor(total[:], total[:], x[:], ALU.add)
                    v.wait_ge(high, 1)
                    v.drain()
                    v.tensor_tensor(total[:], total[:], work2[:], ALU.add)
                    v.drain()
                    normalise(nc, v, None, total[:], x[:], work[:], stat, sems, 1)
                    v.drain().then_inc(finished, 1)

                @block.scalar
                def _(act):
                    act.wait_ge(ready, 1)
                    nc.scalar.activation(deviation[:], moment[:, 1], ACT.Sqrt).then_inc(rooted_, 1)
                    act.wait_ge(low, 1)
                    nc.scalar.activation(work2[:], work[:], ACT.Exp).then_inc(high, 1)
                    normalise(nc, None, act, None, None, None, stat, sems, 1)


def laid_out(inputs):
    n = {k: np.asarray(v) for k, v in inputs.items()}

    def padded(t, rows, fill=0):
        t = np.asarray(t)
        more = np.full((rows - t.shape[0],) + t.shape[1:], fill, t.dtype)
        return np.ascontiguousarray(np.concatenate([t, more]))

    arrays = {"x": padded(n["x"], NP), "edge_weight": padded(n["edge_weight"], EP)}
    for k in ("src", "dst"):
        arrays[k] = padded(n[k], EP, N)
    arrays["dst_before"] = np.concatenate([np.full(1, -1, n["dst"].dtype), arrays["dst"][:-1]])
    arrays["attr3"] = padded(n["edge_attr_3"], EP)
    arrays["attr5"] = padded(n["edge_attr_5"], EP)
    arrays["attr32"] = padded(n["edge_attr_32"], EP)
    lin, edge = n["L1_gnn_W_lin"].reshape(C, H, C), n["L1_gnn_W_edge"].reshape(D5, H, C)
    b_lin, b_edge = n["L1_gnn_b_lin"].reshape(1, H, C), n["L1_gnn_b_edge"].reshape(1, H, C)
    arrays["att1"] = n["L1_gnn_att"].reshape(H, 2, C).transpose(2, 1, 0).reshape(C, 2 * H)
    arrays["proj1"] = np.concatenate([lin, b_lin, edge, b_edge]).transpose(2, 1, 0)
    arrays["out1"] = np.concatenate([lin, edge, b_lin])
    arrays["out1_bias"] = b_edge
    arrays["bias1"] = n["L1_gnn_bias"].reshape(1, C)
    wk, wv, we = (n[f"L2_gnn_{k}"].reshape(-1, H, C) for k in ("Wk", "Wv", "We"))
    bk, bv = n["L2_gnn_bk"].reshape(1, H, C), n["L2_gnn_bv"].reshape(1, H, C)
    arrays["wq"] = n["L2_gnn_Wq"]
    arrays["bq"] = n["L2_gnn_bq"].reshape(H * C, 1)
    keys = np.zeros((H, C, H, F2), n["L2_gnn_Wk"].dtype)
    for h in range(H):
        keys[h, :, h] = np.concatenate([wk, we, bk])[:, h].T
    arrays["keys2"] = keys.reshape(H * C, H * F2)
    arrays["values2"] = np.concatenate([wv, we, bv])
    arrays["wp"] = n["L2_gnn_Wp"].reshape(H, C, C).transpose(1, 0, 2)
    for k in ("ln1_g", "ln1_b", "ln2_g", "ln2_b", "bp", "b2"):
        arrays[k] = n[f"L2_gnn_{k}"].reshape(1, C)
    arrays["w1"], arrays["w2"] = n["L2_gnn_W1"], n["L2_gnn_W2"]
    arrays["b1"] = n["L2_gnn_b1"].reshape(C, 1)
    arrays["spline"] = n["L3_gnn_W"].transpose(1, 0, 2).reshape(C, S3 * C)
    arrays["root"] = n["L3_gnn_root"]
    arrays["gamma"], arrays["beta"] = n["L3_gnn_gamma"].reshape(1, C), n["L3_gnn_beta"].reshape(1, C)
    return {f"in_{k}": np.ascontiguousarray(v) for k, v in arrays.items()}


def kernel(**inputs):
    import concourse.bacc as bacc
    from concourse.bass_utils import run_bass_kernel_spmd

    arrays = laid_out(inputs)
    nc = bacc.Bacc("TRN2", target_bir_lowering=False, num_devices=1)
    a = {k[3:]: nc.dram_tensor(k, v.shape, mybir.dt.from_np(v.dtype), kind="ExternalInput").ap()
         for k, v in arrays.items()}
    out = nc.dram_tensor("out_0_dram", (N, C), F32, kind="ExternalOutput").ap()
    build(nc, a, out)
    r = run_bass_kernel_spmd(nc, [arrays], core_ids=[0])
    return r.results[0]["out_0_dram"]
```

```python
from contextlib import ExitStack

import numpy as np

import concourse.bass as bass
from concourse import mybir

F32 = mybir.dt.float32
I32 = mybir.dt.int32
BF16 = mybir.dt.bfloat16
ALU = mybir.AluOpType
ACT = mybir.ActivationFunctionType
AX = mybir.AxisListType.X

P = 128
N = 6250
E = 200000
C = 64
NT = -(-N // P)
NP = NT * P
L = 1568
EP = P * L
assert EP >= E and NP > N
H = 2
D5, D32, D3 = 5, 32, 3
FAR = 1.0e30
OFF = 1.0e7
LN_EPS = 1e-5

F1 = C + D5 + 1
R1 = F1 + H
B1 = C + H + 1
F2 = C + D32 + 1
B2 = H * F2 + H
S3 = 2 ** D3
T1 = 28
T2 = 14
SB = 7


UNROLL = 4


class Chunk:

    def __init__(self, g, r):
        self.g, self.r, self.b = g, r, r % 2
        self.h = g * (UNROLL // 2) + r // 2
        self.at = g * UNROLL + r


def chunks(eng, count):
    with eng.Fori(0, count // UNROLL) as g:
        for r in range(UNROLL):
            yield Chunk(g, r)


def chunks_ahead(eng, count, first, second):
    first(Chunk(0, 0))
    with eng.Fori(0, count // UNROLL - 1) as g:
        for r in range(UNROLL):
            first(Chunk(g, r + 1) if r + 1 < UNROLL else Chunk(g + 1, 0))
            second(Chunk(g, r))
    last = count // UNROLL - 1
    for r in range(UNROLL):
        if r + 1 < UNROLL:
            first(Chunk(last, r + 1))
        second(Chunk(last, r))


def wait(eng, sem, value):
    eng.wait_ge(sem, value)
    eng.nop(nofuse=True)


def build(nc, a, out):
    top = ExitStack()

    in_use = []

    def sem(name):
        in_use.append(nc.alloc_semaphore(name=name))
        return in_use[-1]

    def clear_semaphores():
        nc.all_engine_barrier()
        nc.clear_and_free_semaphores(in_use)
        in_use.clear()
        nc.all_engine_barrier()

    def dram(name, shape, dt=F32):
        return nc.dram_tensor(name, shape, dt, kind="Internal").ap()

    first_d = {k: dram(f"first_{k}", (NP + 1, 1)) for k in ("src", "dst")}
    pos_d = dram("pos", (P, L), I32)
    sums0_d = dram("sums0", (EP, C))
    table1_d = dram("table1", (NP, B1))
    tablea_d = dram("tablea", (NP, H + 1))
    spread1_d = dram("spread1", (EP, B1))
    spreada_d = dram("spreada", (EP, H + 1))
    rows1_d = dram("rows1", (EP, R1))
    sums1_d = dram("sums1", (EP, H * F1 + H))
    h2_d = dram("h2", (NP, C))
    table2_d = dram("table2", (NP, B2))
    spread2_d = dram("spread2", (EP, B2))
    sums2_d = dram("sums2", (EP, H * F2 + H))
    table3_d = dram("table3", (NP, S3 * C))
    sums3_d = dram("sums3", (EP, C))

    e = {k: dram(f"sorted_{k}", (EP, w), dt) for k, w, dt in ARRAYS + (("dst_before", 1, I32),)}

    def run_of(t, w):
        return t.rearrange("(p l) w -> p (l w)", p=P)

    with top:
        def keep_tile(name, shape, dt=F32):
            return top.enter_context(nc.sbuf_tensor(name, shape, dt))

        x = keep_tile("x", [P, NT, C])
        identity = keep_tile("identity", [P, P])
        run_end = keep_tile("run_end", [P, 1])
        end_idx = {k: keep_tile(f"end_idx_{k}", [P, NT], I32) for k in ("src", "dst")}
        start_idx = {k: keep_tile(f"start_idx_{k}", [P, NT], I32) for k in ("src", "dst")}
        filled = {k: keep_tile(f"filled_{k}", [P, NT]) for k in ("src", "dst")}
        degree = keep_tile("degree", [P, NT])
        head_key = {k: keep_tile(f"head_key_{k}", [P, 1], I32) for k in ("src", "dst")}
        tail_key = {k: keep_tile(f"tail_key_{k}", [P, 1]) for k in ("src", "dst")}

        first = {k: keep_tile(f"first_pos_{k}", [P, NT]) for k in ("src", "dst")}
        zeros = keep_tile("zeros", [P, 2048])
        iota_b, ident_b, upper_b = (keep_tile(n, [P, P], BF16) for n in ("iota_b", "ident_b", "upper_b"))
        late = sem("late")
        ordering(nc, a, sem, dict(locals()))
        layer0(nc, a, sem, dict(locals()))
        layer1(nc, a, sem, dict(locals()))
        clear_semaphores()
        layer2(nc, a, sem, dict(locals()))
        layer3(nc, a, sem, dict(locals()), out)


def clear_part(g, sp, cleared, target, w, turn, turns):
    width = L * w // turns
    assert width * turns == L * w
    step = max(d for d in range(1, 2049) if width % d == 0)
    for c in range(width // step):
        sp.dma_start(g["run_of"](g[target], w)[:, bass.ds(turn * width + c * step, step)], g["zeros"][:, 0:step]).then_inc(cleared, 16)
    return width // step


class Space:

    def __init__(self, nc, stack):
        self.nc, self.stack = nc, stack

    def sb(self, name, shape, dt=F32):
        return self.stack.enter_context(self.nc.sbuf_tensor(name, shape, dt))

    def ps(self, name, shape, dt=F32):
        return self.stack.enter_context(self.nc.psum_tensor(name, shape, dt))


def index_tables(v, g, k, s, count, ones, hist, ends_in, summed, tri):
    col_sum, prefix, first, after, tmp, tmp2, ends_row, scratch_row, key_f, last_f = s
    v.wait_ge(tri, 1)
    v.tensor_copy(col_sum[:, 1:NT + 1], hist[:, 64:64 + NT])
    v.drain()
    v.tensor_tensor_scan(prefix[:], ones[:, 0:NT + 1], col_sum[:], 0.0, ALU.mult, ALU.add)
    v.drain()
    v.tensor_tensor(first[:], prefix[:, 0:NT], hist[:, 128:128 + NT], ALU.add)
    if k == "dst":
        v.tensor_copy(g["degree"][:], count[:])
    v.tensor_scalar(g["filled"][k][:], count[:], 0.5, None, ALU.is_gt)
    v.drain()
    v.tensor_tensor(after[:], first[:], count[:], ALU.add).then_inc(summed, 1)
    v.tensor_scalar(tmp2[:], g["filled"][k][:], -OFF, OFF, ALU.mult, ALU.add)
    v.drain()
    v.tensor_scalar(tmp[:], after[:], -1.0, 0.0, ALU.add, ALU.max)
    v.tensor_tensor(tmp2[:], tmp2[:], first[:], ALU.add)
    v.drain()
    v.tensor_copy(g["end_idx"][k][:], tmp[:])
    v.tensor_copy(g["start_idx"][k][:], tmp2[:])
    v.tensor_scalar(key_f[:], g["run_end"][:], -float(L), None, ALU.add)
    v.tensor_scalar(last_f[:], g["run_end"][:], -1.0, None, ALU.add)
    v.wait_ge(ends_in, 16)
    v.drain()
    v.tensor_scalar(scratch_row[:], ends_row[:], key_f[:, 0:1], 0.0, ALU.is_le, ALU.add, accum_out=tmp[:, 0:1])
    v.drain()
    v.tensor_scalar(scratch_row[:], ends_row[:], last_f[:, 0:1], 0.0, ALU.is_le, ALU.add, accum_out=g["tail_key"][k][:])
    v.drain()
    v.tensor_copy(g["head_key"][k][:], tmp[:, 0:1])


def split_keys(v, key, part, low, high):
    v.tensor_scalar(part[:], key[:], P - 1, None, ALU.bitwise_and)
    v.drain()
    v.tensor_copy(low[:, 0:L], part[:])
    v.drain()
    v.tensor_scalar(part[:], key[:], 7, None, ALU.arith_shift_right)
    v.drain()
    v.tensor_copy(high[:, 0:L], part[:])
    v.drain()


def one_hots(v, hot_low, hot_high, iota_b, low, high, step):
    at = bass.ds(step * SB, SB)
    v.tensor_tensor(hot_low, iota_b[:].unsqueeze(1).to_broadcast([P, SB, P]),
                    low[:, at].unsqueeze(2).to_broadcast([P, SB, P]), ALU.is_equal)
    return v.tensor_tensor(hot_high, iota_b[:, 0:NT].unsqueeze(1).to_broadcast([P, SB, NT]),
                           high[:, at].unsqueeze(2).to_broadcast([P, SB, NT]), ALU.is_equal)


HOT = 4
TURN = 8


class Ranking:

    def __init__(self, s, sem, name, consts):
        self.iota_b, self.ident_b, self.upper_b = consts
        self.low, self.high = s.sb(f"{name}_low", [P, L + 2 * SB], BF16), s.sb(f"{name}_high", [P, L + 2 * SB], BF16)
        self.key, self.part = s.sb(f"{name}_key", [P, L], I32), s.sb(f"{name}_part", [P, L], I32)
        self.hot_low = s.sb(f"{name}_hot_low", [P, HOT, SB, P], BF16)
        self.hot_high = s.sb(f"{name}_hot_high", [P, HOT, SB, NT], BF16)
        self.low_t = s.sb(f"{name}_low_t", [P, 2, SB * P], BF16)
        self.low_tf = s.sb(f"{name}_low_tf", [P, 2, SB * P])
        self.earlier = s.sb(f"{name}_earlier", [P, 2, SB, P], BF16)
        self.added = s.sb(f"{name}_added", [P, NT, SB + 1])
        self.goes_on = s.sb(f"{name}_goes_on", [P, NT, SB + 1])
        self.before = s.sb(f"{name}_before", [P, 2, NT, SB + 1])
        self.picked = s.sb(f"{name}_picked", [P, SB, NT])
        self.pos_f = s.sb(f"{name}_pos_f", [P, L + SB])
        self.pos_i = s.sb(f"{name}_pos_i", [P, L], I32)
        self.turned = s.ps(f"{name}_turned", [P, 2, 1024], BF16)
        self.same = s.ps(f"{name}_same", [P, 8, P])
        self.rank = s.ps(f"{name}_rank", [P, 2, 8, C])
        self.count = s.ps(f"{name}_count", [P, 2, 512])
        self.hot = [sem(f"{name}_hot{r}") for r in range(HOT)]
        self.turned_ready, self.copied, self.same_ready, self.masked, self.counted, self.based, self.ranked, self.read, self.ready = (
            sem(f"{name}_{n}") for n in ("turned_ready", "copied", "same_ready", "masked", "counted", "based", "ranked", "read", "ready"))

    @staticmethod
    def at(h, r):
        return h * TURN + r

    def tensor_start(self, nc, pe):
        self.tensor_ahead(nc, pe, 0, 0)

    def tensor_ahead(self, nc, pe, h, r):
        q = r % HOT
        wait(pe, self.hot[q], h * (TURN // HOT) + (r // HOT + 1))
        for j in range(SB):
            last = nc.tensor.matmul(self.count[:, r % 2, j * NT:(j + 1) * NT], self.hot_low[:, q, j], self.hot_high[:, q, j], start=True, stop=True)
        last.then_inc(self.counted, 1)
        for j in range(SB):
            last = nc.tensor.transpose(self.turned[:, r % 2, j * P:(j + 1) * P], self.hot_low[:, q, j], self.ident_b[:])
        last.then_inc(self.turned_ready, 1)

    def tensor_step(self, nc, pe, h, r):
        s, b = self.at(h, r), r % 2
        wait(pe, self.copied, s + 1)
        for j in range(SB):
            t = self.low_t[:, b, j * P:(j + 1) * P]
            last = nc.tensor.matmul(self.same[:, j], t, t, start=True, stop=True)
        last.then_inc(self.same_ready, 1)
        self.tensor_ahead(nc, pe, *((h, r + 1) if r + 1 < TURN else (h + 1, 0)))
        wait(pe, self.masked, s + 1)
        wait(pe, self.based, s + 1)
        wait(pe, self.read, s + 1)
        for j in range(SB):
            nc.tensor.matmul(self.rank[:, b, j, 0:NT], self.earlier[:, b, j], self.hot_high[:, r % HOT, j], start=True, stop=False)
            last = nc.tensor.matmul(self.rank[:, b, j, 0:NT], self.low_tf[:, b, j * P:(j + 1) * P], self.before[:, b, :, j], start=False, stop=True)
        last.then_inc(self.ranked, 1)

    def scalar_step(self, nc, act, h, r):
        s, b = self.at(h, r), r % 2
        wait(act, self.turned_ready, s + 1)
        wait(act, self.ranked, s + 1)
        nc.scalar.copy(self.low_t[:, b], self.turned[:, b, 0:SB * P])
        nc.scalar.copy(self.low_tf[:, b], self.turned[:, b, 0:SB * P]).then_inc(self.copied, 1)

    def vector_start(self, v, first, keys_in, filled):
        v.memset(self.low[:, L:], 0.0)
        v.memset(self.high[:, L:], 0.0)
        v.memset(self.goes_on[:], 1.0)
        v.memset(self.rank[:], 0.0)
        v.memset(self.hot_high[:], 0.0)
        v.sem_inc(self.ranked, 2)
        v.sem_inc(self.read, 1)
        v.wait_ge(keys_in, filled)
        split_keys(v, self.key, self.part, self.low, self.high)
        v.memset(self.goes_on[:, :, 0], 0.0)
        v.tensor_copy(self.before[:, 1, :, SB], first[:])
        v.drain()
        for r in range(2):
            one_hots(v, self.hot_low[:, r], self.hot_high[:, r], self.iota_b, self.low, self.high, r).then_inc(self.hot[r], 1)
        self.bases(v, 0, 0)

    def bases(self, v, h, r):
        b = r % 2
        wait(v, self.counted, self.at(h, r) + 1)
        v.tensor_copy(self.added[:, :, 1:], self.count[:, b, 0:SB * NT].rearrange("p (j n) -> p n j", j=SB))
        v.tensor_copy(self.added[:, :, 0], self.before[:, 1 - b, :, SB])
        v.drain()
        v.tensor_tensor_scan(self.before[:, b].rearrange("p n j -> p (n j)"), self.goes_on[:].rearrange("p n j -> p (n j)"),
                             self.added[:].rearrange("p n j -> p (n j)"), 0.0, ALU.mult, ALU.add).then_inc(self.based, 1)

    def pick(self, v, s, r):
        b = (r - 1) % 2
        wait(v, self.ranked, s + 2)
        v.tensor_tensor(self.picked[:], self.rank[:, b, 0:SB, 0:NT], self.hot_high[:, (r - 1) % HOT], ALU.mult).then_inc(self.read, 1)
        v.drain()
        v.tensor_reduce(self.pos_f[:, bass.ds(s * SB, SB)], self.picked[:], AX, ALU.add)

    def vector_step(self, v, h, r):
        s, b, q = self.at(h, r), r % 2, (r + 2) % HOT
        wait(v, self.same_ready, s + 1)
        v.tensor_tensor(self.earlier[:, b], self.same[:, 0:SB], self.upper_b[:].unsqueeze(1).to_broadcast([P, SB, P]), ALU.mult).then_inc(self.masked, 1)
        self.pick(v, s, r)
        self.bases(v, *((h, r + 1) if r + 1 < TURN else (h + 1, 0)))
        one_hots(v, self.hot_low[:, q], self.hot_high[:, q], self.iota_b, self.low, self.high, s + 2).then_inc(self.hot[q], 1)
        v.drain()

    def vector_end(self, v):
        self.pick(v, L // SB, 0)
        v.drain()
        v.tensor_copy(self.pos_i[:], self.pos_f[:, SB:])
        v.drain().then_inc(self.ready, 1)


ARRAYS = (("src", 1, I32), ("dst", 1, I32), ("edge_weight", 1, F32), ("attr3", D3, F32), ("attr5", D5, F32), ("attr32", D32, F32))


def ordering(nc, a, sem, g):
    with ExitStack() as stack:
        s = Space(nc, stack)
        sb, ps = s.sb, s.ps
        flag = sb("flag", [P, 1], I32)
        iota_i, row_i = sb("iota_i", [P, P], I32), sb("row_i", [P, 1], I32)
        row_f, col_f = sb("row_f", [P, 1]), sb("col_f", [P, P])
        upper, ones = sb("upper", [P, P]), sb("ones", [P, P])
        zero_b = sb("zero_b", [P, P], BF16)
        total = sb("total", [1, 2])
        minus = sb("minus", [1, 2], I32)
        iota_b, ident_b, upper_b = g["iota_b"], g["ident_b"], g["upper_b"]
        with ExitStack() as inner:
            s = Space(nc, inner)
            sb, ps = s.sb, s.ps
            key = {k: sb(f"key_{k}", [P, L], I32) for k in ("src", "dst")}
            before_key = sb("before_key", [P, L], I32)
            falls, fell = sb("falls", [P, L], BF16), sb("fell", [P, 1])
            part = sb("part", [P, L], I32)
            low = {k: sb(f"low_{k}", [P, L], BF16) for k in ("src", "dst")}
            high = {k: sb(f"high_{k}", [P, L], BF16) for k in ("src", "dst")}
            hot_low = sb("hot_low", [P, 2, SB, P], BF16)
            hot_high = sb("hot_high", [P, 2, SB, NT], BF16)
            count = {k: sb(f"count_{k}", [P, NT]) for k in ("src", "dst")}
            small = [sb("col_sum", [P, NT + 1]), sb("prefix", [P, NT + 1]), None, sb("after", [P, NT]), sb("tmp_o", [P, NT]), sb("tmp2_o", [P, NT]),
                     None, sb("scratch_row", [P, NP], BF16), sb("key_f", [P, 1]), sb("last_f", [P, 1])]
            ends_row = {k: sb(f"ends_row_{k}", [P, NP]) for k in ("src", "dst")}
            hist = {k: ps(f"hist_{k}", [P, 512]) for k in ("src", "dst")}
            fall_ps = ps("fall_ps", [P, 512])
            drawn, checked, fallen = (sem(f"o_{n}") for n in ("drawn", "checked", "fallen"))
            loaded = {k: sem(f"o_loaded_{k}") for k in ("src", "dst")}
            hot, hot_used = [sem(f"o_hot{b}") for b in range(2)], [sem(f"o_used{b}") for b in range(2)]
            summed, tri, first_out, ends_in, counted = ({k: sem(f"o_{n}{k}") for k in ("src", "dst")} for n in ("sum", "tri", "fo", "ei", "c"))
            turns = L // SB // 2
            with nc.Block() as block:
                @block.sync
                def _(sp):
                    for k in ("src", "dst"):
                        sp.dma_start(key[k][:], g["run_of"](a[k], 1)).then_inc(loaded[k], 16)
                    sp.dma_start(before_key[:], g["run_of"](a["dst_before"], 1)).then_inc(loaded["dst"], 16)
                    for k in ("src", "dst"):
                        sp.wait_ge(summed[k], 1)
                        first_d = g["first_d"][k]
                        sp.dma_start(first_d[0:NP].rearrange("(t p) o -> p (t o)", p=P), g["first"][k][:],
                                     allow_slow_non_contiguous=True).then_inc(first_out[k], 16)
                        sp.dma_start(first_d[NP:NP + 1], total[:, 0:1]).then_inc(first_out[k], 16)
                        sp.wait_ge(first_out[k], 32)
                        sp.dma_start(ends_row[k][:], first_d[1:NP + 1].rearrange("n o -> o n").to_broadcast([P, NP])).then_inc(ends_in[k], 16)

                @block.gpsimd
                def _(pool):
                    nc.gpsimd.iota(iota_i[:], [[1, P]], base=0, channel_multiplier=0).then_inc(drawn, 1)
                    nc.gpsimd.iota(row_i[:], [[0, 1]], base=0, channel_multiplier=1).then_inc(drawn, 1)

                @block.tensor
                def _(pe):
                    for n, k in enumerate(("src", "dst")):
                        wait(pe, hot[0], turns * n + 1)
                        nc.tensor.matmul(hist[k][:, 0:NT], zero_b[:], zero_b[:, 0:NT], start=True, stop=False, skip_group_check=True)
                        with pe.Fori(0, turns) as h:
                            for b in range(2):
                                wait(pe, hot[b], h + (turns * n + 1))
                                for j in range(SB):
                                    last = nc.tensor.matmul(hist[k][:, 0:NT], hot_low[:, b, j], hot_high[:, b, j],
                                                            start=False, stop=False, skip_group_check=True)
                                last.then_inc(hot_used[b], 1)
                        pe.wait_ge(counted[k], 1)
                        nc.tensor.matmul(hist[k][:, 64:64 + NT], ones[:], count[k][:], start=True, stop=True, skip_group_check=True)
                        nc.tensor.matmul(hist[k][:, 128:128 + NT], upper[:], count[k][:], start=True, stop=True,
                                         skip_group_check=True).then_inc(tri[k], 1)
                    pe.wait_ge(checked, 1)
                    nc.tensor.matmul(fall_ps[:, 0:1], ones[:], fell[:], start=True, stop=True).then_inc(fallen, 1)

                @block.vector
                def _(v):
                    v.wait_ge(drawn, 2)
                    v.tensor_copy(iota_b[:], iota_i[:])
                    v.tensor_copy(col_f[:], iota_i[:])
                    v.tensor_copy(row_f[:], row_i[:])
                    v.memset(ones[:], 1.0)
                    v.memset(zero_b[:], 0.0)
                    v.memset(g["zeros"][:], 0.0)
                    v.memset(small[0][:], 0.0)
                    v.memset(total[:], float(EP))
                    v.memset(minus[:], -1)
                    v.drain()
                    v.tensor_scalar(g["identity"][:], col_f[:], row_f[:, 0:1], None, ALU.is_equal)
                    v.tensor_scalar(ident_b[:], col_f[:], row_f[:, 0:1], None, ALU.is_equal)
                    v.tensor_scalar(upper[:], col_f[:], row_f[:, 0:1], None, ALU.is_gt)
                    v.tensor_scalar(upper_b[:], col_f[:], row_f[:, 0:1], None, ALU.is_gt)
                    v.tensor_scalar(g["run_end"][:], row_f[:], float(L), float(L), ALU.mult, ALU.add)
                    for n, k in enumerate(("src", "dst")):
                        v.wait_ge(loaded[k], 16 if k == "src" else 32)
                        split_keys(v, key[k], part, low[k], high[k])
                        if k == "src":
                            for b in range(2):
                                v.sem_inc(hot_used[b], 1)
                        with v.Fori(0, turns) as h:
                            for b in range(2):
                                wait(v, hot_used[b], h + (turns * n + 1))
                                one_hots(v, hot_low[:, b], hot_high[:, b], iota_b, low[k], high[k], h * 2 + b).then_inc(hot[b], 1)
                        for b in range(2):
                            v.wait_ge(hot_used[b], turns * (n + 1) + 1)
                        v.tensor_copy(count[k][:], hist[k][:, 0:NT])
                        v.drain().then_inc(counted[k], 1)
                        small[2], small[6] = g["first"][k], ends_row[k]
                        index_tables(v, g, k, small, count[k], ones, hist[k], ends_in[k], summed[k], tri[k])
                    v.tensor_tensor(falls[:], key["dst"][:], before_key[:], ALU.is_lt)
                    v.drain()
                    v.tensor_reduce(fell[:], falls[:], AX, ALU.max)
                    v.drain().then_inc(checked, 1)
                    v.wait_ge(fallen, 1)
                    v.tensor_scalar(fell[:], fall_ps[:, 0:1], 1.0, None, ALU.min)
                    v.drain()
                    v.tensor_copy(flag[:], fell[:])

        with ExitStack() as inner:
            s = Space(nc, inner)
            ranking = Ranking(s, sem, "d", (iota_b, ident_b, upper_b))
            T, NC = T1, L // T1
            idx = s.sb("d_idx", [P, T], I32)
            rows = {k: s.sb(f"d_{k}", [P, T, w], dt) for k, w, dt in ARRAYS}
            keys_in, pos_out, chunk_in, chunk_free, soon, shifted = (sem(f"d_{n}") for n in (
                "keys_in", "pos_out", "chunk_in", "chunk_free", "soon", "shifted"))
            sent = {k: sem(f"d_sent_{k}") for k, _, _ in ARRAYS}
            late = g["late"]
            turns = L // SB // TURN
            with nc.Block() as block:
                def branch(eng, sort, keep=None):
                    unsorted = eng.value_load(flag[0:1, 0:1], min_val=0, max_val=1)
                    with eng.If(unsorted > 0):
                        sort()
                    with eng.Else():
                        if keep:
                            keep()
                        else:
                            eng.nop()

                @block.sync
                def _(sp):
                    def sort():
                        sp.dma_start(ranking.key[:], g["run_of"](a["dst"], 1)).then_inc(keys_in, 16)
                        sp.wait_ge(ranking.ready, 1)
                        sp.dma_start(g["pos_d"], ranking.pos_i[:]).then_inc(pos_out, 16)
                        sp.wait_ge(pos_out, 16)
                        with sp.Fori(0, NC) as c:
                            wait(sp, chunk_free, c + 1)
                            sp.dma_start(idx[:], g["pos_d"][:, bass.ds(c * T, T)]).then_inc(chunk_in, 16)
                            for k, w, _ in ARRAYS:
                                sp.dma_start(rows[k][:].rearrange("p t w -> p (t w)"), g["run_of"](a[k], w)[:, bass.ds(c * (T * w), T * w)]).then_inc(chunk_in, 16)
                        sp.wait_ge(chunk_free, NC + 1)
                        sp.dma_start(g["e"]["dst_before"][1:EP], g["e"]["dst"][0:EP - 1]).then_inc(shifted, 16)
                        sp.dma_start(g["e"]["dst_before"][0:1], minus[:, 0:1]).then_inc(shifted, 16)
                        sp.wait_ge(shifted, 32)
                        sp.sem_inc(late, 48)

                    def keep():
                        for k, w in (("src", 1), ("dst", 1), ("dst_before", 1), ("edge_weight", 1)):
                            sp.dma_start(g["run_of"](g["e"][k], w), g["run_of"](a[k], w)).then_inc(soon, 16)
                        sp.wait_ge(soon, 64)
                    branch(sp, sort, keep)

                @block.tensor
                def _(pe):
                    def sort():
                        ranking.tensor_start(nc, pe)
                        with pe.Fori(0, turns) as h:
                            for r in range(TURN):
                                ranking.tensor_step(nc, pe, h, r)
                    branch(pe, sort)

                @block.scalar
                def _(act):
                    def sort():
                        with act.Fori(0, turns) as h:
                            for r in range(TURN):
                                ranking.scalar_step(nc, act, h, r)

                    def keep():
                        for k, w in (("attr5", D5), ("attr32", D32), ("attr3", D3)):
                            act.dma_start(g["run_of"](g["e"][k], w), g["run_of"](a[k], w)).then_inc(late, 16)
                    branch(act, sort, keep)

                @block.vector
                def _(v):
                    def sort():
                        ranking.vector_start(v, g["first"]["dst"], keys_in, 16)
                        with v.Fori(0, turns) as h:
                            for r in range(TURN):
                                ranking.vector_step(v, h, r)
                        ranking.vector_end(v)
                    branch(v, sort)

                @block.gpsimd
                def _(pool):
                    def sort():
                        pool.sem_inc(chunk_free, 1)
                        with pool.Fori(0, NC) as c:
                            wait(pool, chunk_in, (c + 1) * (16 * (1 + len(ARRAYS))))
                            for k, w, _ in ARRAYS:
                                for t in range(T):
                                    pool.indirect_dma_start(g["e"][k], bass.IndirectOffsetOnAxis(ap=idx[:, t:t + 1], axis=0),
                                                            rows[k][:, t], None).then_inc(sent[k], 16)
                            for k, _, _ in ARRAYS:
                                wait(pool, sent[k], (c + 1) * (16 * T))
                            pool.sem_inc(chunk_free, 1)
                    branch(pool, sort)


def spread_masks(nc, sem, g, k, name, masks, last_only):
    with ExitStack() as stack:
        s = Space(nc, stack)
        first_row = s.sb(f"{name}_first", [P, NP])
        end_row = s.sb(f"{name}_end", [P, NP])
        got, done = sem(f"{name}_got"), sem(f"{name}_done")
        run_past = s.sb(f"{name}_past", [P, 1])
        with nc.Block() as block:
            @block.sync
            def _(sp):
                sp.dma_start(first_row[:], g["first_d"][k][0:NP].rearrange("n o -> o n").to_broadcast([P, NP])).then_inc(got, 16)
                sp.dma_start(end_row[:], g["first_d"][k][1:NP + 1].rearrange("n o -> o n").to_broadcast([P, NP])).then_inc(got, 16)

            @block.vector
            def _(v):
                v.wait_ge(got, 32)
                run_end = g["run_end"][:, 0:1]
                v.tensor_scalar(run_past[:], g["run_end"][:], float(L), None, ALU.add)
                v.tensor_scalar(first_row[:], first_row[:], run_end, None, ALU.is_lt)
                v.drain()
                v.scalar_tensor_tensor(out=masks[:], in0=end_row[:], scalar=run_end, in1=first_row[:],
                                       op0=ALU.is_gt, op1=ALU.mult)
                v.drain()
                if last_only is not None:
                    v.scalar_tensor_tensor(out=last_only[:], in0=end_row[:], scalar=run_past[:, 0:1], in1=masks[:],
                                           op0=ALU.is_le, op1=ALU.mult)


def normalise(nc, v, act, sums, out_, work, stat, sems, turn, gain=None, shift=None):
    centred, rooted = sems
    if v is not None:
        v.tensor_reduce(stat[:, 0], sums, AX, ALU.add)
        v.drain()
        v.tensor_scalar(stat[:, 0], stat[:, 0], 1.0 / C, None, ALU.mult)
        v.drain()
        v.tensor_tensor(sums, sums, stat[:, 0].unsqueeze(2).to_broadcast([P, NT, C]), ALU.subtract)
        v.drain()
        v.tensor_tensor(work, sums, sums, ALU.mult)
        v.drain()
        v.tensor_reduce(stat[:, 1], work, AX, ALU.add)
        v.drain()
        v.tensor_scalar(stat[:, 1], stat[:, 1], 1.0 / C, LN_EPS, ALU.mult, ALU.add).then_inc(centred, 1)
        v.wait_ge(rooted, turn)
        v.reciprocal(stat[:, 1], stat[:, 2])
        v.drain()
        v.tensor_tensor(out_, sums, stat[:, 1].unsqueeze(2).to_broadcast([P, NT, C]), ALU.mult)
        v.drain()
        if gain is not None:
            v.tensor_tensor(out_, out_, gain[:].unsqueeze(1).to_broadcast([P, NT, C]), ALU.mult)
            v.drain()
            v.tensor_tensor(out_, out_, shift[:].unsqueeze(1).to_broadcast([P, NT, C]), ALU.add)
            v.drain()
    if act is not None:
        act.wait_ge(centred, turn)
        nc.scalar.activation(stat[:, 2], stat[:, 1], ACT.Sqrt).then_inc(rooted, 1)


def layer0(nc, a, sem, g):
    T, NC = T1, L // T1
    x, e = g["x"], g["e"]
    turns = L // SB // TURN
    assert turns == NC // 2
    with ExitStack() as outer:
        tail = Space(nc, outer).sb("l0_tail", [P, C])
        with ExitStack() as stack:
            s = Space(nc, stack)
            ranking = Ranking(s, sem, "r", (g["iota_b"], g["ident_b"], g["upper_b"]))
            idx = s.sb("l0_idx", [P, 2, T], I32)
            rows = s.sb("l0_rows", [P, 2, T, C])
            data = s.sb("l0_data", [P, C, T + 1])
            keep = s.sb("l0_keep", [P, 2, C, T + 1])
            run = s.sb("l0_run", [P, 2, C, T + 1])
            outb = s.sb("l0_out", [P, 2, T, C])
            weight = s.sb("l0_weight", [P, L])
            keys = s.sb("l0_keys", [P, L], I32)
            prev = s.sb("l0_prev", [P, L], I32)
            same = s.sb("l0_same", [P, L])
            two = lambda n: [sem(f"l0_{n}{b}") for b in range(2)]
            idx_in, got, rows_used, keep_ready, scanned, copied, stored = (two(n) for n in (
                "idx_in", "got", "rows_used", "keep_ready", "scanned", "copied", "stored"))
            loaded, flags, x_in, keys_in, cleared, pos_out = (sem(f"l0_{n}") for n in ("loaded", "flags", "x_in", "keys_in", "cleared", "pos_out"))
            with nc.Block() as block:
                @block.sync
                def _(sp):
                    sp.dma_start(ranking.key[:], g["run_of"](e["src"], 1)).then_inc(keys_in, 16)
                    sp.dma_start(weight[:], g["run_of"](e["edge_weight"], 1)).then_inc(loaded, 16)
                    sp.dma_start(keys[:], g["run_of"](e["dst"], 1)).then_inc(loaded, 16)
                    sp.dma_start(prev[:], g["run_of"](e["dst_before"], 1)).then_inc(loaded, 16)
                    sp.dma_start(x[:], a["x"].rearrange("(t p) c -> p t c", p=P)).then_inc(x_in, 16)
                    src = g["run_of"](e["src"], 1)
                    with sp.Fori(0, NC // 2) as h:
                        for b in range(2):
                            wait(sp, rows_used[b], h + 1)
                            sp.dma_start(idx[:, b], src[:, bass.ds((h * 2 + b) * T, T)]).then_inc(idx_in[b], 16)
                        parts = clear_part(g, sp, cleared, "spread1_d", B1, h, NC // 2)
                        parts += clear_part(g, sp, cleared, "spreada_d", H + 1, h, NC // 2)
                    sp.wait_ge(x_in, 16)
                    sp.wait_ge(cleared, 16 * parts * (NC // 2))
                    sp.wait_ge(g["late"], 48)
                    sp.wait_ge(ranking.ready, 1)
                    sp.dma_start(g["pos_d"], ranking.pos_i[:]).then_inc(pos_out, 16)
                    sp.wait_ge(pos_out, 16)

                @block.gpsimd
                def _(pool):
                    with pool.Fori(0, NC // 2) as h:
                        for b in range(2):
                            wait(pool, idx_in[b], (h + 1) * 16)
                            for t in range(T):
                                pool.indirect_dma_start(rows[:, b, t], None, a["x"],
                                                        bass.IndirectOffsetOnAxis(ap=idx[:, b, t:t + 1], axis=0)) \
                                    .then_inc(got[b], 16)

                @block.tensor
                def _(pe):
                    ranking.tensor_start(nc, pe)
                    with pe.Fori(0, turns) as h:
                        for r in range(TURN):
                            ranking.tensor_step(nc, pe, h, r)

                @block.vector
                def _(v):
                    v.memset(run[:], 0.0)
                    v.memset(keep[:], 0.0)
                    v.sem_inc(rows_used[0], 1)
                    v.sem_inc(rows_used[1], 1)
                    v.wait_ge(loaded, 48)
                    v.tensor_tensor(same[:], keys[:], prev[:], ALU.is_equal)
                    v.drain().then_inc(flags, 1)
                    ranking.vector_start(v, g["first"]["src"], keys_in, 16)

                    def sum_rows(h, b):
                        wait(v, got[b], (h + 1) * (16 * T))
                        at = bass.ds((h * 2 + b) * T, T)
                        v.tensor_tensor(data[:, :, 1:], rows[:, b].rearrange("p t f -> p f t"),
                                        weight[:, at].unsqueeze(1).to_broadcast([P, C, T]), ALU.mult) \
                         .then_inc(rows_used[b], 1)
                        v.tensor_copy(data[:, :, 0:1], run[:, 1 - b, :, T:T + 1])
                        wait(v, keep_ready[b], h + 1)
                        wait(v, copied[b], h + 1)
                        v.drain()
                        v.tensor_tensor_scan(run[:, b].rearrange("p f t -> p (f t)"),
                                             keep[:, b].rearrange("p f t -> p (f t)"),
                                             data[:].rearrange("p f t -> p (f t)"), 0.0, ALU.mult, ALU.add) \
                         .then_inc(scanned[b], 1)
                        v.drain()

                    with v.Fori(0, turns) as h:
                        for b in range(2):
                            for r in range(b * TURN // 2, (b + 1) * TURN // 2):
                                ranking.vector_step(v, h, r)
                            sum_rows(h, b)
                    ranking.vector_end(v)
                    v.tensor_copy(tail[:], run[:, 1, :, T])

                @block.scalar
                def _(act):
                    act.wait_ge(flags, 1)
                    for b in range(2):
                        act.sem_inc(copied[b], 1)
                        act.sem_inc(stored[b], 16)
                        act.sem_inc(scanned[b], 1)

                    def keeps(h, b):
                        wait(act, scanned[b], h + 1)
                        at = bass.ds((h * 2 + b) * T, T)
                        nc.scalar.copy(keep[:, b, :, 1:], same[:, at].unsqueeze(1).to_broadcast([P, C, T])) \
                          .then_inc(keep_ready[b], 1)

                    def store(h, b):
                        wait(act, scanned[b], h + 2)
                        wait(act, stored[b], (h + 1) * 16)
                        nc.scalar.copy(outb[:, b], run[:, b, :, 1:].rearrange("p f t -> p t f")).then_inc(copied[b], 1)
                        wait(act, copied[b], h + 2)
                        act.dma_start(g["run_of"](g["sums0_d"], C)[:, bass.ds((h * 2 + b) * (T * C), T * C)],
                                      outb[:, b].rearrange("p t f -> p (t f)")).then_inc(stored[b], 16)

                    ranking.scalar_step(nc, act, 0, 0)
                    with act.Fori(0, turns) as h:
                        for b in range(2):
                            keeps(h, b)
                            for r in range(b * TURN // 2 + 1, (b + 1) * TURN // 2 + 1):
                                ranking.scalar_step(nc, act, *((h, r) if r < TURN else (h + 1, 0)))
                            store(h, b)
                    for b in range(2):
                        act.wait_ge(stored[b], 16 * (NC // 2 + 1))

        total = collect_sums(nc, sem, g, outer, "l0", g["sums0_d"], tail)
        with ExitStack() as stack:
            s = Space(nc, stack)
            work, stat = s.sb("l0_work", [P, NT, C]), s.sb("l0_stat", [P, 3, NT])
            sems = sem("l0_centred"), sem("l0_rooted")
            with nc.Block() as block:
                @block.vector
                def _(v):
                    v.tensor_tensor(total[:], total[:], x[:], ALU.add)
                    v.drain()
                    normalise(nc, v, None, total[:], x[:], work[:], stat, sems, 1)

                @block.scalar
                def _(act):
                    normalise(nc, None, act, None, None, None, stat, sems, 1)


def collect_sums(nc, sem, g, outer, name, sums_d, tail):
    s0 = Space(nc, outer)
    total = s0.sb(f"{name}_total", [P, NT, C])
    with ExitStack() as stack:
        s = Space(nc, stack)
        masks = s.sb(f"{name}_masks", [P, NP])
        more = s.ps(f"{name}_more", [P, 2, 8, C])
        spread_masks(nc, sem, g, "dst", name, masks, None)
        got, read, mult = sem(f"{name}_cgot"), sem(f"{name}_cread"), sem(f"{name}_cmult")
        groups = [range(i, min(i + 8, NT)) for i in range(0, NT, 8)]
        with nc.Block() as block:
            @block.gpsimd
            def _(pool):
                for i in range(NT):
                    pool.indirect_dma_start(total[:, i], None, sums_d,
                                            bass.IndirectOffsetOnAxis(ap=g["end_idx"]["dst"][:, i:i + 1], axis=0)).then_inc(got, 16)

            @block.tensor
            def _(pe):
                for n, tiles in enumerate(groups):
                    if n >= 2:
                        pe.wait_ge(read, n - 1)
                    for j, i in enumerate(tiles):
                        last = nc.tensor.matmul(more[:, n % 2, j], masks[:, i * P:(i + 1) * P], tail[:], start=True, stop=True)
                    last.then_inc(mult, 1)

            @block.vector
            def _(v):
                v.wait_ge(got, 16 * NT)
                v.tensor_tensor(total[:], total[:], g["filled"]["dst"][:].unsqueeze(2).to_broadcast([P, NT, C]), ALU.mult)
                v.drain()
                for n, tiles in enumerate(groups):
                    v.wait_ge(mult, n + 1)
                    at = slice(tiles[0], tiles[-1] + 1)
                    v.tensor_tensor(total[:, at], total[:, at], more[:, n % 2, 0:len(tiles)], ALU.add).then_inc(read, 1)
    return total


def layer1(nc, a, sem, g):
    x = g["x"]
    with ExitStack() as outer:
        s0 = Space(nc, outer)
        tail = s0.sb("l1_tail", [P, H * F1 + H])
        head = s0.sb("l1_head", [P, B1])
        head_a = s0.sb("l1_heada", [P, H + 1])
        edge_w = s0.sb("l1_edge_w", [P, H, D5])
        with ExitStack() as stack:
            s = Space(nc, stack)
            att = s.sb("l1_att", [C, 2 * H])
            att_wide = s.sb("l1_att_wide", [C, 2 * H, P])
            proj = s.sb("l1_proj", [C, H, F1 + 1])
            node_w = s.sb("l1_node_w", [P, 2, H, F1 + 1])
            const = s.sb("l1_const", [P, H])
            rows = s.sb("l1_node_rows", [P, NT, B1])
            rows_a = s.sb("l1_node_rows_a", [P, NT, H + 1])
            prod = s.sb("l1_node_prod", [P, NT, C])
            score = s.sb("l1_node_score", [P, 2, H, NT])
            dots = s.ps("l1_dots", [P, 2, H, P])
            loaded, wide, dotted, tabled, saved, fetched = (sem(f"l1_{n}") for n in ("loaded", "wide", "dotted", "tabled", "saved", "fetched"))
            with nc.Block() as block:
                @block.sync
                def _(sp):
                    sp.dma_start(att[:], a["att1"]).then_inc(loaded, 16)
                    sp.dma_start(proj[:], a["proj1"]).then_inc(loaded, 16)
                    sp.wait_ge(tabled, 2)
                    sp.dma_start(g["table1_d"].rearrange("(t p) w -> p t w", p=P), rows[:]).then_inc(saved, 16)
                    sp.dma_start(g["tablea_d"].rearrange("(t p) w -> p t w", p=P), rows_a[:]).then_inc(saved, 16)

                @block.tensor
                def _(pe):
                    pe.wait_ge(loaded, 32)
                    pe.wait_ge(wide, 1)
                    for side in range(2):
                        for h in range(H):
                            last = nc.tensor.matmul(dots[:, side, h, 0:F1 + 1], att_wide[:, side * H + h], proj[:, h],
                                                    start=True, stop=True)
                    last.then_inc(dotted, 1)

                @block.vector
                def _(v):
                    v.wait_ge(loaded, 32)
                    v.tensor_copy(att_wide[:], att[:].unsqueeze(2).to_broadcast([C, 2 * H, P])).then_inc(wide, 1)
                    v.memset(rows[:], 1.0)
                    v.memset(rows_a[:], 1.0)
                    v.wait_ge(dotted, 1)
                    v.tensor_copy(node_w[:], dots[:, :, :, 0:F1 + 1])
                    v.drain()
                    v.tensor_copy(edge_w[:], node_w[:, 1, :, C + 1:C + 1 + D5])
                    v.tensor_tensor(const[:], node_w[:, 1, :, C], node_w[:, 1, :, F1], ALU.add)
                    v.tensor_copy(rows[:, :, 0:C], x[:])
                    v.drain()
                    for side in range(2):
                        for h in range(H):
                            v.tensor_tensor(prod[:], x[:], node_w[:, side, h, 0:C].unsqueeze(1).to_broadcast([P, NT, C]), ALU.mult)
                            v.drain()
                            v.tensor_reduce(score[:, side, h], prod[:], AX, ALU.add)
                            v.drain()
                    for h in range(H):
                        v.tensor_scalar(rows_a[:, :, h], score[:, 0, h], node_w[:, 0, h, C:C + 1], None, ALU.add)
                        v.tensor_scalar(rows[:, :, C + h], score[:, 1, h], const[:, h:h + 1], None, ALU.add)
                    v.drain().then_inc(tabled, 2)

                @block.gpsimd
                def _(pool):
                    pool.wait_ge(tabled, 2)
                    for table, target, k in ((rows, "spread1_d", "dst"), (rows_a, "spreada_d", "src")):
                        for i in range(NT):
                            pool.indirect_dma_start(g[target], bass.IndirectOffsetOnAxis(ap=g["start_idx"][k][:, i:i + 1], axis=0),
                                                    table[:, i], None, bounds_check=EP - 1, oob_is_err=False).then_inc(fetched, 16)
                    pool.wait_ge(saved, 32)
                    pool.indirect_dma_start(head[:], None, g["table1_d"],
                                            bass.IndirectOffsetOnAxis(ap=g["head_key"]["dst"][:], axis=0)).then_inc(fetched, 16)
                    pool.indirect_dma_start(head_a[:], None, g["tablea_d"],
                                            bass.IndirectOffsetOnAxis(ap=g["head_key"]["src"][:], axis=0)).then_inc(fetched, 16)
                    pool.wait_ge(fetched, 16 * (2 * NT + 2))

        T, NC = T1, L // T1
        with ExitStack() as stack:
            s = Space(nc, stack)
            W = C + H
            spread = s.sb("l1_spread", [P, 2, T, B1])
            attr = s.sb("l1_attr", [P, 2, T, D5])
            idx = s.sb("l1_idx", [P, 2, T], I32)
            data = s.sb("l1_data", [P, W, T + 1])
            keep = s.sb("l1_keep", [P, 2, W, T + 1])
            run = s.sb("l1_run", [P, 2, W, T + 1])
            rows = s.sb("l1_rows", [P, 2, T, R1])
            prod = s.sb("l1_prod", [P, T, H, D5])
            dot = s.sb("l1_dot", [P, T, H])
            two = lambda n: [sem(f"l1d_{n}{b}") for b in range(2)]
            loaded, used, keep_ready, scanned, filled, sent, scored, free = (two(n) for n in (
                "loaded", "used", "keep_ready", "scanned", "filled", "sent", "scored", "free"))
            set_up, cleared = sem("l1d_set_up"), sem("l1d_cleared")
            with nc.Block() as block:
                @block.sync
                def _(sp):
                    spread_v, attr_v = g["run_of"](g["spread1_d"], B1), g["run_of"](g["e"]["attr5"], D5)
                    with sp.Fori(0, NC // 2) as h:
                        for b in range(2):
                            c = h * 2 + b
                            wait(sp, used[b], h + 1)
                            wait(sp, keep_ready[b], h + 1)
                            wait(sp, free[b], h + 1)
                            sp.dma_start(spread[:, b].rearrange("p t w -> p (t w)"), spread_v[:, bass.ds(c * (T * B1), T * B1)]).then_inc(loaded[b], 16)
                            sp.dma_start(attr[:, b].rearrange("p t w -> p (t w)"), attr_v[:, bass.ds(c * (T * D5), T * D5)]).then_inc(loaded[b], 16)
                            sp.dma_start(idx[:, b], g["pos_d"][:, bass.ds(c * T, T)]).then_inc(loaded[b], 16)
                        parts = clear_part(g, sp, cleared, "spread2_d", B2, h, NC // 2)
                    sp.wait_ge(cleared, 16 * parts * (NC // 2))

                @block.scalar
                def _(act):
                    act.wait_ge(set_up, 1)
                    with act.Fori(0, NC // 2) as h:
                        for b in range(2):
                            wait(act, loaded[b], (h + 1) * 48)
                            wait(act, scanned[b], h + 1)
                            nc.scalar.activation(keep[:, b, :, 1:], spread[:, b, :, B1 - 1].unsqueeze(1).to_broadcast([P, W, T]),
                                                 ACT.Copy, bias=1.0, scale=-1.0).then_inc(keep_ready[b], 1)
                            wait(act, scanned[b], h + 2)
                            wait(act, free[b], h + 1)
                            nc.scalar.copy(rows[:, b, :, 0:C], run[:, b, 0:C, 1:].rearrange("p f t -> p t f"))
                            nc.scalar.copy(rows[:, b, :, C:C + D5], attr[:, b]).then_inc(filled[b], 1)

                @block.vector
                def _(v):
                    v.memset(keep[:], 0.0)
                    v.memset(rows[:], 1.0)
                    v.memset(run[:], 0.0)
                    v.drain()
                    v.tensor_copy(run[:, 1, :, T], head[:, 0:W])
                    for b in range(2):
                        v.sem_inc(used[b], 1)
                        v.sem_inc(keep_ready[b], 1)
                        v.sem_inc(scanned[b], 1)
                        v.sem_inc(free[b], 1)
                        v.sem_inc(filled[b], 1)
                    v.drain().then_inc(set_up, 1)
                    with v.Fori(0, NC // 2) as h:
                        for b in range(2):
                            wait(v, loaded[b], (h + 1) * 48)
                            v.tensor_copy(data[:, :, 1:], spread[:, b, :, 0:W].rearrange("p t f -> p f t"))
                            v.tensor_copy(data[:, :, 0:1], run[:, 1 - b, :, T:T + 1])
                            v.tensor_tensor(prod[:], attr[:, b].unsqueeze(2).to_broadcast([P, T, H, D5]),
                                            edge_w[:].unsqueeze(1).to_broadcast([P, T, H, D5]), ALU.mult)
                            v.drain().then_inc(used[b], 1)
                            v.tensor_reduce(dot[:], prod[:], AX, ALU.add)
                            wait(v, keep_ready[b], h + 2)
                            wait(v, filled[b], h + 1)
                            v.tensor_tensor_scan(run[:, b].rearrange("p f t -> p (f t)"), keep[:, b].rearrange("p f t -> p (f t)"),
                                                 data[:].rearrange("p f t -> p (f t)"), 0.0, ALU.mult, ALU.add).then_inc(scanned[b], 1)
                            wait(v, free[b], h + 1)
                            v.drain()
                            v.tensor_tensor(rows[:, b, :, F1:R1], run[:, b, C:W, 1:].rearrange("p f t -> p t f"), dot[:], ALU.add) \
                             .then_inc(scored[b], 1)

                @block.gpsimd
                def _(pool):
                    def scatter(h, b, first=False):
                        wait(pool, filled[b], h + 2)
                        wait(pool, scored[b], h + 1)
                        for t in range(T):
                            pool.indirect_dma_start(g["rows1_d"], bass.IndirectOffsetOnAxis(ap=idx[:, b, t:t + 1], axis=0),
                                                    rows[:, b, t], None).then_inc(sent[b], 16)
                            if t == T // 2 and not first:
                                wait(pool, sent[1 - b], (h + b) * (16 * T))
                                pool.sem_inc(free[1 - b], 1)
                    scatter(0, 0, True)
                    scatter(0, 1)
                    with pool.Fori(1, NC // 2) as h:
                        for b in range(2):
                            scatter(h, b)
                    for b in range(2):
                        pool.wait_ge(sent[b], 16 * T * (NC // 2))

        with ExitStack() as stack:
            s = Space(nc, stack)
            W = H * F1
            rows = s.sb("l1s_rows", [P, UNROLL, T, R1])
            side = s.sb("l1s_side", [P, UNROLL, T, H + 1])
            hold = s.sb("l1s_hold", [P, 2, H, T + 1])
            hold_data = s.sb("l1s_hold_data", [P, H, T + 1])
            hold_keep = s.sb("l1s_hold_keep", [P, H, T + 1])
            score = s.sb("l1s_score", [P, H, T + 1])
            leak = s.sb("l1s_leak", [P, H, T])
            soft = Softmax(s, "l1s", T, F1)
            outb = s.sb("l1s_out", [P, 2, T, W + H])
            two = lambda n: [sem(f"l1s_{n}{b}") for b in range(2)]
            loaded, used = ([sem(f"l1s_{n}{r}") for r in range(UNROLL)] for n in ("loaded", "used"))
            soft.semaphores(two)
            set_up = sem("l1s_set_up")
            with nc.Block() as block:
                @block.sync
                def _(sp):
                    rows_v, side_v = g["run_of"](g["rows1_d"], R1), g["run_of"](g["spreada_d"], H + 1)
                    for c in chunks(sp, NC):
                        wait(sp, used[c.r], c.g + 1)
                        sp.dma_start(rows[:, c.r].rearrange("p t w -> p (t w)"), rows_v[:, bass.ds(c.at * (T * R1), T * R1)]).then_inc(loaded[c.r], 16)
                        sp.dma_start(side[:, c.r].rearrange("p t w -> p (t w)"), side_v[:, bass.ds(c.at * (T * (H + 1)), T * (H + 1))]).then_inc(loaded[c.r], 16)

                @block.scalar
                def _(act):
                    act.wait_ge(set_up, 1)
                    soft.scalar_program(nc, act, NC, outb, g["run_of"](g["sums1_d"], W + H))

                @block.vector
                def _(v):
                    v.memset(hold[:], 0.0)
                    v.memset(hold_keep[:], 0.0)
                    v.drain()
                    v.tensor_copy(hold[:, 1, :, T], head_a[:, 0:H])
                    soft.start(v)
                    for r in range(UNROLL):
                        v.sem_inc(used[r], 1)
                    v.drain().then_inc(set_up, 1)

                    def scores(c):
                        b, r = c.b, c.r
                        wait(v, loaded[r], (c.g + 1) * 32)
                        start = side[:, r, :, H].unsqueeze(1).to_broadcast([P, H, T])
                        v.tensor_scalar(hold_keep[:, :, 1:], start, -1.0, 1.0, ALU.mult, ALU.add)
                        v.tensor_copy(hold_data[:, :, 1:], side[:, r, :, 0:H].rearrange("p t h -> p h t"))
                        v.tensor_copy(hold_data[:, :, 0:1], hold[:, 1 - b, :, T:T + 1])
                        v.drain()
                        v.tensor_tensor_scan(hold[:, b].rearrange("p h t -> p (h t)"), hold_keep[:].rearrange("p h t -> p (h t)"),
                                             hold_data[:].rearrange("p h t -> p (h t)"), 0.0, ALU.mult, ALU.add)
                        v.drain()
                        v.tensor_tensor(leak[:], hold[:, b, :, 1:], rows[:, r, :, F1:R1].rearrange("p t h -> p h t"), ALU.add)
                        v.drain()
                        v.scalar_tensor_tensor(out=score[:, :, 1:], in0=leak[:], scalar=0.2, in1=leak[:], op0=ALU.mult, op1=ALU.max)
                        soft.running_max(v, c, score, start)

                    def sums(c):
                        soft.sums(v, c, rows[:, c.r, :, 0:F1].rearrange("p t f -> p f t")).then_inc(used[c.r], 1)
                        soft.scan(v, c)

                    soft.vector_program(v, NC, scores, sums)
                    soft.keep_tail(v, tail)

        summed = collect_softmax(nc, sem, g, outer, "l1", "src", g["sums1_d"], tail, F1)
        with ExitStack() as stack:
            s = Space(nc, stack)
            out_w = s.sb("l1_out_w", [F1, H, C])
            bias = s.sb("l1_bias", [P, C])
            recip = s.sb("l1_recip", [P, NT, H])
            turned_s = s.sb("l1_turned", [F1, 2, H, P])
            work, stat = s.sb("l1_work", [P, NT, C]), s.sb("l1_stat", [P, 3, NT])
            acc = s.sb("l1_acc", [P, NT, C])
            turned = s.ps("l1_turned_ps", [P, 2, 512])
            made = s.ps("l1_made", [P, 2, 512])
            loaded, added, scaled, turned_ready, copied, made_ready, read = (sem(f"l1n_{n}") for n in (
                "loaded", "added", "scaled", "turned", "copied", "made", "read"))
            sems = sem("l1_centred"), sem("l1_rooted")
            with nc.Block() as block:
                @block.gpsimd
                def _(pool):
                    pool.dma_start(out_w[:], a["out1"]).then_inc(loaded, 16)
                    pool.dma_start(bias[:], a["bias1"].to_broadcast([P, C])).then_inc(added, 16)
                    pool.wait_ge(loaded, 16)
                    pool.dma_start(out_w[F1 - 1:F1], a["out1_bias"], accum_op=ALU.add).then_inc(added, 16)
                    pool.wait_ge(added, 32)

                @block.vector
                def _(v):
                    den = summed[:, :, 0:H * F1].rearrange("p t (h f) -> p t h f", h=H)[:, :, :, F1 - 1]
                    v.tensor_scalar(recip[:], den, 1e-16, float(H), ALU.add, ALU.mult)
                    v.drain()
                    v.reciprocal(recip[:], recip[:])
                    v.drain()
                    for h in range(H):
                        part = summed[:, :, h * F1:(h + 1) * F1]
                        v.tensor_tensor(part, part, recip[:, :, h].unsqueeze(2).to_broadcast([P, NT, F1]), ALU.mult)
                    v.drain().then_inc(scaled, 1)
                    v.wait_ge(added, 32)
                    v.tensor_tensor(acc[:], x[:], bias[:].unsqueeze(1).to_broadcast([P, NT, C]), ALU.add)
                    for i in range(NT):
                        v.wait_ge(made_ready, i + 1)
                        v.drain()
                        v.tensor_tensor(acc[:, i], acc[:, i], made[:, i % 2, 0:C], ALU.add).then_inc(read, 1)
                    v.drain()
                    normalise(nc, v, None, acc[:], x[:], work[:], stat, sems, 1)

                @block.scalar
                def _(act):
                    for i in range(NT):
                        act.wait_ge(turned_ready, i + 1)
                        if i >= 2:
                            act.wait_ge(made_ready, i - 1)
                        nc.scalar.copy(turned_s[:, i % 2].rearrange("f h e -> f (h e)"), turned[0:F1, i % 2, 0:H * P]).then_inc(copied, 1)
                    normalise(nc, None, act, None, None, None, stat, sems, 1)

                @block.tensor
                def _(pe):
                    pe.wait_ge(scaled, 1)
                    pe.wait_ge(added, 32)

                    def turn(i):
                        if i >= 2:
                            pe.wait_ge(copied, i - 1)
                        for h in range(H):
                            last = nc.tensor.transpose(turned[0:F1, i % 2, h * P:(h + 1) * P], summed[:, i, h * F1:(h + 1) * F1],
                                                       g["identity"][:])
                        last.then_inc(turned_ready, 1)
                    turn(0)
                    for i in range(NT):
                        if i + 1 < NT:
                            turn(i + 1)
                        pe.wait_ge(copied, i + 1)
                        if i >= 2:
                            pe.wait_ge(read, i - 1)
                        for h in range(H):
                            last = nc.tensor.matmul(made[:, i % 2, 0:C], turned_s[:, i % 2, h], out_w[:, h],
                                                    start=(h == 0), stop=(h == H - 1))
                        last.then_inc(made_ready, 1)


class Softmax:

    def __init__(self, s, name, T, F):
        self.T, self.F = T, F
        self.fresh = s.sb(f"{name}_fresh", [P, H, T + 1])
        self.top = s.sb(f"{name}_top", [P, 2, H, T + 1])
        self.arg = s.sb(f"{name}_arg", [P, 2, 2, H, T])
        self.exp = s.sb(f"{name}_exp", [P, 2, 2, H, T])
        self.scale = s.sb(f"{name}_scale", [P, 2, H, F, T + 1])
        self.data = s.sb(f"{name}_data", [P, H, F, T + 1])
        self.run = s.sb(f"{name}_run", [P, 2, H, F, T + 1])

    def semaphores(self, two):
        self.args_ready, self.exp_ready, self.scale_ready, self.scanned, self.copied, self.stored = (
            two(n) for n in ("args", "exp", "scale", "scanned", "copied", "stored"))

    def start(self, v):
        v.memset(self.fresh[:], -FAR)
        v.memset(self.top[:], -FAR)
        v.memset(self.scale[:], 0.0)
        v.memset(self.run[:], 0.0)
        for b in range(2):
            v.sem_inc(self.scanned[b], 1)
            v.sem_inc(self.copied[b], 1)
            v.sem_inc(self.exp_ready[b], 1)
            v.sem_inc(self.stored[b], 16)

    def running_max(self, v, c, score, start):
        T, h, b = self.T, c.h, c.b
        v.tensor_scalar(self.fresh[:, :, 1:], start, -FAR, None, ALU.mult)
        v.tensor_copy(score[:, :, 0:1], self.top[:, 1 - b, :, T:T + 1])
        wait(v, self.copied[b], h + 1)
        wait(v, self.exp_ready[b], h + 1)
        v.drain()
        v.tensor_tensor_scan(self.top[:, b].rearrange("p h t -> p (h t)"), self.fresh[:].rearrange("p h t -> p (h t)"),
                             score[:].rearrange("p h t -> p (h t)"), -FAR, ALU.add, ALU.max)
        v.drain()
        v.tensor_tensor(self.arg[:, b, 0], self.top[:, b, :, 0:T], self.fresh[:, :, 1:], ALU.add)
        v.tensor_tensor(self.arg[:, b, 1], score[:, :, 1:], self.top[:, b, :, 1:], ALU.subtract)
        v.drain()
        v.tensor_tensor(self.arg[:, b, 0], self.arg[:, b, 0], self.top[:, b, :, 1:], ALU.subtract).then_inc(self.args_ready[b], 1)

    def sums(self, v, c, rows):
        T, h, b = self.T, c.h, c.b
        wait(v, self.exp_ready[b], h + 2)
        for head in range(H):
            v.tensor_tensor(self.data[:, head, :, 1:], rows,
                            self.exp[:, b, 1, head].unsqueeze(1).to_broadcast([P, self.F, T]), ALU.mult)
        return v.drain()

    def scan(self, v, c):
        T, h, b = self.T, c.h, c.b
        v.tensor_copy(self.data[:, :, :, 0:1], self.run[:, 1 - b, :, :, T:T + 1])
        wait(v, self.scale_ready[b], h + 1)
        wait(v, self.copied[b], h + 1)
        v.drain()
        v.tensor_tensor_scan(self.run[:, b].rearrange("p h f t -> p (h f t)"), self.scale[:, b].rearrange("p h f t -> p (h f t)"),
                             self.data[:].rearrange("p h f t -> p (h f t)"), 0.0, ALU.mult, ALU.add).then_inc(self.scanned[b], 1)
        v.drain()

    def vector_program(self, v, count, scores, sums):
        chunks_ahead(v, count, scores, sums)

    def keep_tail(self, v, tail):
        T, W = self.T, H * self.F
        v.tensor_copy(tail[:, 0:W], self.run[:, 1].rearrange("p h f t -> p (h f) t")[:, :, T])
        v.tensor_copy(tail[:, W:W + H], self.top[:, 1, :, T])

    def scalar_program(self, nc, act, count, outb, sums_v, before=lambda c: None):
        T, W = self.T, H * self.F

        def exponentials(c):
            before(c)
            h, b = c.h, c.b
            wait(act, self.args_ready[b], h + 1)
            nc.scalar.activation(self.exp[:, b], self.arg[:, b], ACT.Exp).then_inc(self.exp_ready[b], 1)
            wait(act, self.exp_ready[b], h + 2)
            wait(act, self.scanned[b], h + 1)
            for head in range(H):
                last = nc.scalar.copy(self.scale[:, b, head, :, 1:], self.exp[:, b, 0, head].unsqueeze(1).to_broadcast([P, self.F, T]))
            last.then_inc(self.scale_ready[b], 1)

        def store(c):
            h, b = c.h, c.b
            wait(act, self.scanned[b], h + 2)
            wait(act, self.stored[b], (h + 1) * 16)
            nc.scalar.copy(outb[:, b, :, 0:W], self.run[:, b].rearrange("p h f t -> p (h f) t")[:, :, 1:].rearrange("p w t -> p t w"))
            nc.scalar.copy(outb[:, b, :, W:W + H], self.top[:, b, :, 1:].rearrange("p h t -> p t h")).then_inc(self.copied[b], 1)
            wait(act, self.copied[b], h + 2)
            wide = T * outb.shape[-1]
            act.dma_start(sums_v[:, bass.ds(c.at * wide, wide)], outb[:, b].rearrange("p t w -> p (t w)")).then_inc(self.stored[b], 16)

        chunks_ahead(act, count, exponentials, store)
        for b in range(2):
            act.wait_ge(self.stored[b], 16 * (count // 2 + 1))


def collect_softmax(nc, sem, g, outer, name, k, sums_d, tail, F):
    W = H * F
    total = Space(nc, outer).sb(f"{name}_total", [P, NT, W + H])
    with ExitStack() as stack:
        s = Space(nc, stack)
        masks = s.sb(f"{name}_masks", [P, NP])
        last_only = s.sb(f"{name}_last_only", [P, NP])
        spread_masks(nc, sem, g, k, name, masks, last_only)
        ones = s.sb(f"{name}_ones", [P, P])
        diag = s.sb(f"{name}_diag", [P, H + 1, P])
        other = s.sb(f"{name}_other", [P, P])
        pair = s.sb(f"{name}_pair", [P, H, P])
        top = s.sb(f"{name}_gtop", [P, H + 1])
        factor = s.sb(f"{name}_factor", [P, H])
        scaled = s.sb(f"{name}_scaled", [P, W])
        crossing = s.sb(f"{name}_crossing", [P, NT, H + 1])
        best = s.sb(f"{name}_best", [P, NT, H])
        args = s.sb(f"{name}_args", [P, 2, NT, H])
        exps = s.sb(f"{name}_exps", [P, 2, NT, H])
        wide = s.ps(f"{name}_wide", [P, 512])
        found = s.ps(f"{name}_found", [P, 512])
        more = s.ps(f"{name}_more", [P, 2, 512])
        got, read, mult, diag_ready, spread, arg_ready, exp_ready, top_ready, found_ready, tail_ready = (
            sem(f"{name}_s{n}") for n in ("got", "read", "mult", "diag", "spread", "arg", "exp", "top", "found", "tail"))
        with nc.Block() as block:
            @block.gpsimd
            def _(pool):
                for i in range(NT):
                    pool.indirect_dma_start(total[:, i], None, sums_d,
                                            bass.IndirectOffsetOnAxis(ap=g["end_idx"][k][:, i:i + 1], axis=0)).then_inc(got, 16)

            @block.tensor
            def _(pe):
                pe.wait_ge(diag_ready, 1)
                nc.tensor.matmul(wide[:, 0:(H + 1) * P], ones[:], diag[:].rearrange("p a q -> p (a q)"), start=True, stop=True).then_inc(spread, 1)
                pe.wait_ge(top_ready, 1)
                for i in range(NT):
                    last = nc.tensor.matmul(found[:, i * (H + 1):(i + 1) * (H + 1)], last_only[:, i * P:(i + 1) * P], top[:],
                                            start=True, stop=True)
                last.then_inc(found_ready, 1)
                pe.wait_ge(tail_ready, 1)
                for i in range(NT):
                    if i >= 2:
                        pe.wait_ge(read, i - 1)
                    nc.tensor.matmul(more[:, i % 2, 0:W], masks[:, i * P:(i + 1) * P], scaled[:], start=True, stop=True).then_inc(mult, 1)

            @block.scalar
            def _(act):
                act.wait_ge(arg_ready, 1)
                nc.scalar.activation(factor[:], factor[:], ACT.Exp).then_inc(exp_ready, 1)
                act.wait_ge(arg_ready, 2)
                nc.scalar.activation(exps[:], args[:], ACT.Exp).then_inc(exp_ready, 1)

            @block.vector
            def _(v):
                v.memset(ones[:], 1.0)
                v.memset(top[:], 1.0)
                ident = g["identity"]
                for j in range(H):
                    v.tensor_scalar(diag[:, j], ident[:], tail[:, W + j:W + j + 1], None, ALU.mult)
                v.tensor_scalar(diag[:, H], ident[:], g["tail_key"][k][:, 0:1], None, ALU.mult)
                v.drain().then_inc(diag_ready, 1)
                v.wait_ge(spread, 1)
                v.tensor_scalar(other[:], wide[:, H * P:(H + 1) * P], g["tail_key"][k][:, 0:1], None, ALU.is_equal)
                v.drain()
                v.tensor_scalar(other[:], other[:], FAR, -FAR, ALU.mult, ALU.add)
                v.drain()
                v.tensor_tensor(pair[:], wide[:, 0:H * P].rearrange("p (h q) -> p h q", h=H),
                                other[:].unsqueeze(1).to_broadcast([P, H, P]), ALU.add)
                v.drain()
                v.tensor_reduce(top[:, 0:H], pair[:], AX, ALU.max)
                v.drain().then_inc(top_ready, 1)
                v.tensor_tensor(factor[:], tail[:, W:W + H], top[:, 0:H], ALU.subtract)
                v.drain().then_inc(arg_ready, 1)
                v.wait_ge(exp_ready, 1)
                for h in range(H):
                    v.tensor_scalar(scaled[:, h * F:(h + 1) * F], tail[:, h * F:(h + 1) * F], factor[:, h:h + 1], None, ALU.mult)
                v.drain().then_inc(tail_ready, 1)
                v.wait_ge(found_ready, 1)
                v.tensor_copy(crossing[:].rearrange("p t a -> p (t a)"), found[:, 0:NT * (H + 1)])
                v.drain()
                v.tensor_scalar(crossing[:, :, H], crossing[:, :, H], FAR, -FAR, ALU.mult, ALU.add)
                v.drain()
                v.tensor_tensor(crossing[:, :, 0:H], crossing[:, :, 0:H], crossing[:, :, H].unsqueeze(2).to_broadcast([P, NT, H]), ALU.add)
                v.wait_ge(got, 16 * NT)
                v.drain()
                v.tensor_tensor(best[:], crossing[:, :, 0:H], total[:, :, W:W + H], ALU.max)
                v.drain()
                v.tensor_tensor(args[:, 0], total[:, :, W:W + H], best[:], ALU.subtract)
                v.tensor_tensor(args[:, 1], crossing[:, :, 0:H], best[:], ALU.subtract)
                v.drain().then_inc(arg_ready, 1)
                v.wait_ge(exp_ready, 2)
                v.tensor_tensor(exps[:, 0], exps[:, 0], g["filled"][k][:].unsqueeze(2).to_broadcast([P, NT, H]), ALU.mult)
                v.drain()
                for h in range(H):
                    part = total[:, :, h * F:(h + 1) * F]
                    v.tensor_tensor(part, part, exps[:, 0, :, h].unsqueeze(2).to_broadcast([P, NT, F]), ALU.mult)
                v.drain()
                for i in range(NT):
                    v.wait_ge(mult, i + 1)
                    for h in range(H):
                        last = v.scalar_tensor_tensor(out=total[:, i, h * F:(h + 1) * F], in0=more[:, i % 2, h * F:(h + 1) * F],
                                                      scalar=exps[:, 1, i, h:h + 1], in1=total[:, i, h * F:(h + 1) * F],
                                                      op0=ALU.mult, op1=ALU.add)
                    last.then_inc(read, 1)
    return total


class Pipeline:

    def __init__(self, sem, name, stages):
        self.stages = stages
        self.made = [sem(f"{name}_made{k}") for k in range(stages)]
        self.brought = [sem(f"{name}_brought{k}") for k in range(stages)]

    def tensor(self, pe, work):
        for step in range(NT + self.stages - 1):
            for k in reversed(range(self.stages)):
                i = step - k
                if not 0 <= i < NT:
                    continue
                if k:
                    pe.wait_ge(self.brought[k - 1], i + 1)
                if i >= 2:
                    pe.wait_ge(self.brought[k], i - 1)
                work[k](i).then_inc(self.made[k], 1)

    def scalar(self, act, work):
        last = self.stages - 1
        for step in range(NT + last - 1):
            for k in reversed(range(last)):
                i = step - k
                if not 0 <= i < NT:
                    continue
                act.wait_ge(self.made[k], i + 1)
                if i >= 2:
                    act.wait_ge(self.made[k + 1], i - 1)
                work[k](i).then_inc(self.brought[k], 1)

    def vector(self, v, work):
        for i in range(NT):
            v.wait_ge(self.made[-1], i + 1)
            work(i).then_inc(self.brought[-1], 1)


def layer2(nc, a, sem, g):
    x = g["x"]
    ident = g["identity"]
    with ExitStack() as outer:
        s0 = Space(nc, outer)
        tail = s0.sb("l2_tail", [P, H * F2 + H])
        head = s0.sb("l2_head", [P, B2])
        with ExitStack() as stack:
            s = Space(nc, stack)
            hidden = s.sb("l2_hidden", [P, NT, C])
            work, stat = s.sb("l2_work", [P, NT, C]), s.sb("l2_stat", [P, 3, NT])
            gain, shift = s.sb("l2_gain", [P, C]), s.sb("l2_shift", [P, C])
            wq, bq, keys = s.sb("l2_wq", [C, H * C]), s.sb("l2_bq", [H * C, 1]), s.sb("l2_keys", [H * C, H * F2])
            bq8 = s.sb("l2_bq8", [H * C, 1])
            rows = s.sb("l2_node_rows", [P, NT, B2])
            hid_t, query_t = s.sb("l2_hid_t", [C, 2, P]), s.sb("l2_query_t", [H * C, 2, P])
            ps_a, ps_b, ps_c = s.ps("l2_psa", [P, 2, 512]), s.ps("l2_psb", [P, 2, 512]), s.ps("l2_psc", [P, 2, 512])
            loaded, ready, saved, spread, fetched, scaled, tabled = (sem(f"l2a_{n}") for n in (
                "loaded", "ready", "saved", "spread", "fetched", "scaled", "tabled"))
            sems = sem("l2a_centred"), sem("l2a_rooted")
            pipe = Pipeline(sem, "l2a", 3)
            inv = float(C) ** -0.5
            with nc.Block() as block:
                @block.sync
                def _(sp):
                    sp.dma_start(gain[:], a["ln1_g"].to_broadcast([P, C])).then_inc(loaded, 16)
                    sp.dma_start(shift[:], a["ln1_b"].to_broadcast([P, C])).then_inc(loaded, 16)
                    sp.dma_start(wq[:], a["wq"]).then_inc(loaded, 16)
                    sp.dma_start(bq[:], a["bq"]).then_inc(loaded, 16)
                    sp.dma_start(keys[:], a["keys2"]).then_inc(loaded, 16)
                    sp.wait_ge(ready, 1)
                    sp.dma_start(g["h2_d"].rearrange("(t p) w -> p t w", p=P), hidden[:]).then_inc(saved, 16)
                    sp.wait_ge(tabled, 1)
                    sp.dma_start(g["table2_d"].rearrange("(t p) w -> p t w", p=P), rows[:]).then_inc(saved, 16)
                    sp.wait_ge(saved, 32)

                @block.vector
                def _(v):
                    v.wait_ge(loaded, 80)
                    v.memset(rows[:, :, H * F2:B2], 1.0)
                    v.tensor_scalar(bq8[:], bq[:], inv, None, ALU.mult)
                    v.tensor_copy(work[:], x[:])
                    v.drain().then_inc(scaled, 1)
                    normalise(nc, v, None, work[:], hidden[:], hidden[:], stat, sems, 1, gain, shift)
                    v.drain().then_inc(ready, 1)
                    pipe.vector(v, lambda i: v.tensor_copy(rows[:, i, 0:H * F2], ps_c[:, i % 2, 0:H * F2]))
                    v.drain().then_inc(tabled, 1)

                @block.scalar
                def _(act):
                    normalise(nc, None, act, None, None, None, stat, sems, 1)
                    act.wait_ge(scaled, 1)
                    pipe.scalar(act, [
                        lambda i: nc.scalar.copy(hid_t[:, i % 2], ps_a[0:C, i % 2, 0:P]),
                        lambda i: nc.scalar.activation(query_t[:, i % 2], ps_b[:, i % 2, 0:P], ACT.Identity, bias=bq8[:, 0:1], scale=inv)])

                @block.tensor
                def _(pe):
                    pe.wait_ge(ready, 1)
                    pipe.tensor(pe, [
                        lambda i: nc.tensor.transpose(ps_a[0:C, i % 2, 0:P], hidden[:, i], ident[:]),
                        lambda i: nc.tensor.matmul(ps_b[:, i % 2, 0:P], wq[:], hid_t[:, i % 2], start=True, stop=True),
                        lambda i: nc.tensor.matmul(ps_c[:, i % 2, 0:H * F2], query_t[:, i % 2], keys[:], start=True, stop=True)])

                @block.gpsimd
                def _(pool):
                    pool.wait_ge(tabled, 1)
                    for i in range(NT):
                        pool.indirect_dma_start(g["spread2_d"], bass.IndirectOffsetOnAxis(ap=g["start_idx"]["dst"][:, i:i + 1], axis=0),
                                                rows[:, i], None, bounds_check=EP - 1, oob_is_err=False).then_inc(spread, 16)
                    pool.wait_ge(saved, 32)
                    pool.indirect_dma_start(head[:], None, g["table2_d"],
                                            bass.IndirectOffsetOnAxis(ap=g["head_key"]["dst"][:], axis=0)).then_inc(fetched, 16)
                    pool.wait_ge(spread, 16 * NT)
                    pool.wait_ge(fetched, 16)

        T, NC, W = T2, L // T2, H * F2
        with ExitStack() as stack:
            s = Space(nc, stack)
            spread = s.sb("l2_spread", [P, 2, T, B2])
            rows = s.sb("l2_rows", [P, UNROLL, T, F2])
            idx = s.sb("l2_idx", [P, UNROLL, T], I32)
            hold_data = s.sb("l2_hold_data", [P, H, F2, T + 1])
            hold_keep = s.sb("l2_hold_keep", [P, 2, W, T + 1])
            hold = s.sb("l2_hold", [P, H, F2, T + 1])
            prod = s.sb("l2_prod", [P, H, F2, T])
            score = s.sb("l2_score", [P, H, T + 1])
            soft = Softmax(s, "l2s", T, F2)
            outb = s.sb("l2_out", [P, 2, T, W + H])
            two = lambda n: [sem(f"l2_{n}{b}") for b in range(2)]
            four = lambda n: [sem(f"l2_{n}{b}") for b in range(UNROLL)]
            spread_in, spread_used, keep_ready = two("spread_in"), two("spread_used"), two("keep_ready")
            loaded, idx_in, got, used = four("loaded"), four("idx_in"), four("got"), four("used")
            soft.semaphores(two)
            set_up = sem("l2_set_up")
            with nc.Block() as block:
                @block.sync
                def _(sp):
                    spread_v, attr_v, src_v = g["run_of"](g["spread2_d"], B2), g["e"]["attr32"].rearrange("(p l) w -> p l w", p=P), g["run_of"](g["e"]["src"], 1)
                    for c in chunks(sp, NC):
                        wait(sp, used[c.r], c.g + 1)
                        sp.dma_start(idx[:, c.r], src_v[:, bass.ds(c.at * T, T)]).then_inc(idx_in[c.r], 16)
                        sp.dma_start(rows[:, c.r, :, C:C + D32], attr_v[:, bass.ds(c.at * T, T)]).then_inc(loaded[c.r], 16)
                        wait(sp, spread_used[c.b], c.h + 1)
                        sp.dma_start(spread[:, c.b].rearrange("p t w -> p (t w)"), spread_v[:, bass.ds(c.at * (T * B2), T * B2)]).then_inc(spread_in[c.b], 16)

                @block.gpsimd
                def _(pool):
                    for c in chunks(pool, NC):
                        wait(pool, idx_in[c.r], (c.g + 1) * 16)
                        for t in range(T):
                            pool.indirect_dma_start(rows[:, c.r, t, 0:C], None, g["h2_d"],
                                                    bass.IndirectOffsetOnAxis(ap=idx[:, c.r, t:t + 1], axis=0)).then_inc(got[c.r], 16)

                @block.scalar
                def _(act):
                    act.wait_ge(set_up, 1)

                    def keep(c):
                        wait(act, spread_in[c.b], (c.h + 1) * 16)
                        nc.scalar.activation(hold_keep[:, c.b, :, 1:], spread[:, c.b, :, W].unsqueeze(1).to_broadcast([P, W, T]),
                                             ACT.Copy, bias=1.0, scale=-1.0).then_inc(keep_ready[c.b], 1)
                    soft.scalar_program(nc, act, NC, outb, g["run_of"](g["sums2_d"], W + H), keep)

                @block.vector
                def _(v):
                    v.memset(hold_keep[:], 0.0)
                    v.memset(rows[:, :, :, F2 - 1:F2], 1.0)
                    v.tensor_copy(hold[:].rearrange("p h f t -> p (h f) t")[:, :, T], head[:, 0:W])
                    soft.start(v)
                    for b in range(2):
                        v.sem_inc(spread_used[b], 1)
                    for r in range(UNROLL):
                        v.sem_inc(used[r], 1)
                    v.drain().then_inc(set_up, 1)

                    def scores(c):
                        b = c.b
                        start = spread[:, b, :, W].unsqueeze(1).to_broadcast([P, H, T])
                        wait(v, spread_in[b], (c.h + 1) * 16)
                        v.tensor_copy(hold_data[:].rearrange("p h f t -> p (h f) t")[:, :, 1:], spread[:, b, :, 0:W].rearrange("p t w -> p w t"))
                        v.tensor_copy(hold_data[:, :, :, 0:1], hold[:, :, :, T:T + 1])
                        wait(v, keep_ready[b], c.h + 1)
                        v.drain()
                        v.tensor_tensor_scan(hold[:].rearrange("p h f t -> p (h f t)"), hold_keep[:, b].rearrange("p w t -> p (w t)"),
                                             hold_data[:].rearrange("p h f t -> p (h f t)"), 0.0, ALU.mult, ALU.add)
                        wait(v, loaded[c.r], (c.g + 1) * 16)
                        wait(v, got[c.r], (c.g + 1) * (16 * T))
                        v.drain()
                        for h in range(H):
                            v.tensor_tensor(prod[:, h], hold[:, h, :, 1:], rows[:, c.r].rearrange("p t f -> p f t"), ALU.mult)
                        v.drain()
                        v.tensor_reduce(score[:, :, 1:], prod[:].rearrange("p h f t -> p h t f"), AX, ALU.add)
                        soft.running_max(v, c, score, start)
                        v.drain().then_inc(spread_used[b], 1)

                    def sums(c):
                        soft.sums(v, c, rows[:, c.r].rearrange("p t f -> p f t")).then_inc(used[c.r], 1)
                        soft.scan(v, c)

                    soft.vector_program(v, NC, scores, sums)
                    soft.keep_tail(v, tail)

        summed = collect_softmax(nc, sem, g, outer, "l2", "dst", g["sums2_d"], tail, F2)
        with ExitStack() as stack:
            s = Space(nc, stack)
            vals, wp = s.sb("l2_vals", [F2, H, C]), s.sb("l2_wp", [C, H, C])
            w1, w2, b1 = s.sb("l2_w1", [C, C]), s.sb("l2_w2", [C, C]), s.sb("l2_b1", [C, 1])
            bp, b2 = s.sb("l2_bp", [P, C]), s.sb("l2_b2", [P, C])
            gain, shift = s.sb("l2_gain2", [P, C]), s.sb("l2_shift2", [P, C])
            recip = s.sb("l2_recip", [P, NT, H])
            res, acc, hidden = s.sb("l2_res", [P, NT, C]), s.sb("l2_acc", [P, NT, C]), s.sb("l2_hidden2", [P, NT, C])
            stat = s.sb("l2_stat2", [P, 3, NT])
            sum_t, mean_t = s.sb("l2_sum_t", [F2, 2, H, P]), s.sb("l2_mean_t", [C, 2, H, P])
            ps_a, ps_b, ps_c = s.ps("l2_psd", [P, 2, 512]), s.ps("l2_pse", [P, 2, 512]), s.ps("l2_psf", [P, 2, 512])
            loaded, scaled, ready = (sem(f"l2c_{n}") for n in ("loaded", "scaled", "ready"))
            sems = sem("l2c_centred"), sem("l2c_rooted")
            pipe, mlp = Pipeline(sem, "l2c", 3), Pipeline(sem, "l2m", 3)
            loads = [(vals, a["values2"]), (wp, a["wp"]), (w1, a["w1"]), (w2, a["w2"]), (b1, a["b1"])] + [
                (t, a[k].to_broadcast([P, C])) for t, k in ((bp, "bp"), (b2, "b2"), (gain, "ln2_g"), (shift, "ln2_b"))]
            with nc.Block() as block:
                @block.sync
                def _(sp):
                    for t, of in loads:
                        sp.dma_start(t[:], of).then_inc(loaded, 16)

                @block.vector
                def _(v):
                    den = summed[:, :, 0:H * F2].rearrange("p t (h f) -> p t h f", h=H)[:, :, :, F2 - 1]
                    v.tensor_scalar(recip[:], den, 1e-8, None, ALU.add)
                    v.drain()
                    v.reciprocal(recip[:], recip[:])
                    v.drain()
                    for h in range(H):
                        part = summed[:, :, h * F2:(h + 1) * F2]
                        v.tensor_tensor(part, part, recip[:, :, h].unsqueeze(2).to_broadcast([P, NT, F2]), ALU.mult)
                    v.drain().then_inc(scaled, 1)
                    v.wait_ge(loaded, 16 * len(loads))
                    v.tensor_tensor(res[:], x[:], bp[:].unsqueeze(1).to_broadcast([P, NT, C]), ALU.add)
                    v.drain()
                    pipe.vector(v, lambda i: v.tensor_tensor(res[:, i], res[:, i], ps_c[:, i % 2, 0:C], ALU.add))
                    v.drain()
                    v.tensor_copy(acc[:], res[:])
                    v.drain()
                    normalise(nc, v, None, acc[:], hidden[:], hidden[:], stat, sems, 1, gain, shift)
                    v.tensor_tensor(acc[:], x[:], res[:], ALU.add)
                    v.drain()
                    v.tensor_tensor(acc[:], acc[:], b2[:].unsqueeze(1).to_broadcast([P, NT, C]), ALU.add)
                    v.drain().then_inc(ready, 1)
                    mlp.vector(v, lambda i: v.tensor_tensor(acc[:, i], acc[:, i], ps_c[:, i % 2, C:2 * C], ALU.add))
                    v.drain()
                    normalise(nc, v, None, acc[:], x[:], res[:], stat, sems, 2)

                @block.scalar
                def _(act):
                    act.wait_ge(loaded, 16 * len(loads))
                    pipe.scalar(act, [
                        lambda i: nc.scalar.copy(sum_t[:, i % 2].rearrange("f h e -> f (h e)"), ps_a[0:F2, i % 2, 0:H * P]),
                        lambda i: nc.scalar.copy(mean_t[:, i % 2].rearrange("f h e -> f (h e)"), ps_b[0:C, i % 2, 0:H * P])])
                    normalise(nc, None, act, None, None, None, stat, sems, 1)
                    mlp.scalar(act, [
                        lambda i: nc.scalar.copy(mean_t[:, i % 2, 0], ps_a[0:C, i % 2, 256:256 + P]),
                        lambda i: nc.scalar.activation(mean_t[:, i % 2, 1], ps_b[0:C, i % 2, 256:256 + P], ACT.Gelu, bias=b1[:, 0:1])])
                    normalise(nc, None, act, None, None, None, stat, sems, 2)

                @block.tensor
                def _(pe):
                    def turn(i):
                        for h in range(H):
                            last = nc.tensor.transpose(ps_a[0:F2, i % 2, h * P:(h + 1) * P], summed[:, i, h * F2:(h + 1) * F2], ident[:])
                        return last

                    def means(i):
                        for h in range(H):
                            last = nc.tensor.matmul(ps_b[0:C, i % 2, h * P:(h + 1) * P], vals[:, h], sum_t[:, i % 2, h], start=True, stop=True)
                        return last

                    def project(i):
                        for h in range(H):
                            last = nc.tensor.matmul(ps_c[:, i % 2, 0:C], mean_t[:, i % 2, h], wp[:, h], start=(h == 0), stop=(h == H - 1))
                        return last
                    pe.wait_ge(loaded, 16 * len(loads))
                    pe.wait_ge(scaled, 1)
                    pipe.tensor(pe, [turn, means, project])
                    pe.wait_ge(ready, 1)
                    mlp.tensor(pe, [
                        lambda i: nc.tensor.transpose(ps_a[0:C, i % 2, 256:256 + P], hidden[:, i], ident[:]),
                        lambda i: nc.tensor.matmul(ps_b[0:C, i % 2, 256:256 + P], w1[:], mean_t[:, i % 2, 0], start=True, stop=True),
                        lambda i: nc.tensor.matmul(ps_c[:, i % 2, C:2 * C], mean_t[:, i % 2, 1], w2[:], start=True, stop=True)])


def layer3(nc, a, sem, g, out):
    x = g["x"]
    ident = g["identity"]
    T, NC = T2, L // T2
    with ExitStack() as outer:
        s0 = Space(nc, outer)
        tail = s0.sb("l3_tail", [P, C])
        rooted_x = s0.sb("l3_rooted_x", [P, NT, C])
        with ExitStack() as stack:
            s = Space(nc, stack)
            spline, root = s.sb("l3_spline", [C, S3 * C]), s.sb("l3_root", [C, C])
            x_t = s.sb("l3_x_t", [C, 2, P])
            row = s.sb("l3_row", [P, 2, S3 * C])
            ps_a, ps_b, ps_c = s.ps("l3_psa", [P, 2, 512]), s.ps("l3_psb", [P, 2, 512]), s.ps("l3_psc", [P, 2, 512])
            loaded, made, brought, tabled, copied, read = (sem(f"l3a_{n}") for n in ("loaded", "made", "brought", "tabled", "copied", "read"))
            stored = [sem(f"l3a_stored{b}") for b in range(2)]
            with nc.Block() as block:
                @block.sync
                def _(sp):
                    sp.dma_start(spline[:], a["spline"]).then_inc(loaded, 16)
                    sp.dma_start(root[:], a["root"]).then_inc(loaded, 16)
                    for i in range(NT):
                        sp.wait_ge(copied, i + 1)
                        sp.dma_start(g["table3_d"][i * P:(i + 1) * P], row[:, i % 2]).then_inc(stored[i % 2], 16)
                    sp.wait_ge(stored[0], 16 * ((NT + 1) // 2))
                    sp.wait_ge(stored[1], 16 * (NT // 2))

                @block.tensor
                def _(pe):
                    pe.wait_ge(loaded, 32)

                    def turn(i):
                        if i >= 2:
                            pe.wait_ge(brought, i - 1)
                        nc.tensor.transpose(ps_a[0:C, i % 2, 0:P], x[:, i], ident[:]).then_inc(made, 1)
                    turn(0)
                    for i in range(NT):
                        if i + 1 < NT:
                            turn(i + 1)
                        pe.wait_ge(brought, i + 1)
                        if i >= 2:
                            pe.wait_ge(copied, i - 1)
                            pe.wait_ge(read, i - 1)
                        nc.tensor.matmul(ps_b[:, i % 2], x_t[:, i % 2], spline[:], start=True, stop=True)
                        nc.tensor.matmul(ps_c[:, i % 2, 0:C], x_t[:, i % 2], root[:], start=True, stop=True).then_inc(tabled, 1)

                @block.scalar
                def _(act):
                    for i in range(NT):
                        act.wait_ge(made, i + 1)
                        if i >= 2:
                            act.wait_ge(tabled, i - 1)
                        nc.scalar.copy(x_t[:, i % 2], ps_a[0:C, i % 2, 0:P]).then_inc(brought, 1)
                        if i >= 1:
                            act.wait_ge(tabled, i)
                            nc.scalar.copy(rooted_x[:, i - 1], ps_c[:, (i - 1) % 2, 0:C]).then_inc(read, 1)
                    act.wait_ge(tabled, NT)
                    nc.scalar.copy(rooted_x[:, NT - 1], ps_c[:, (NT - 1) % 2, 0:C]).then_inc(read, 1)

                @block.vector
                def _(v):
                    for i in range(NT):
                        v.wait_ge(tabled, i + 1)
                        if i >= 2:
                            v.wait_ge(stored[i % 2], 16 * (i // 2))
                        v.tensor_copy(row[:, i % 2], ps_b[:, i % 2]).then_inc(copied, 1)

        with ExitStack() as stack:
            s = Space(nc, stack)
            idx = s.sb("l3_idx", [P, 2, T], I32)
            rows = s.sb("l3_rows", [P, 2, T, S3 * C])
            data = s.sb("l3_data", [P, C, T + 1])
            keep = s.sb("l3_keep", [P, 2, C, T + 1])
            run = s.sb("l3_run", [P, 2, C, T + 1])
            outb = s.sb("l3_out", [P, 2, T, C])
            frac = s.sb("l3_frac", [P, L * D3])
            bits = s.sb("l3_bits", [P, T, D3, 2])
            pairs = s.sb("l3_pairs", [P, T, 2, 2])
            basis = s.sb("l3_basis", [P, T, S3])
            keys, prev, same = s.sb("l3_keys", [P, L], I32), s.sb("l3_prev", [P, L], I32), s.sb("l3_same", [P, L])
            two = lambda n: [sem(f"l3_{n}{b}") for b in range(2)]
            idx_in, got, rows_used, keep_ready, scanned, copied, stored = (two(n) for n in (
                "idx_in", "got", "rows_used", "keep_ready", "scanned", "copied", "stored"))
            loaded, flags = sem("l3_loaded"), sem("l3_flags")
            with nc.Block() as block:
                @block.sync
                def _(sp):
                    sp.dma_start(frac[:], g["run_of"](g["e"]["attr3"], D3)).then_inc(loaded, 16)
                    sp.dma_start(keys[:], g["run_of"](g["e"]["dst"], 1)).then_inc(loaded, 16)
                    sp.dma_start(prev[:], g["run_of"](g["e"]["dst_before"], 1)).then_inc(loaded, 16)
                    src = g["run_of"](g["e"]["src"], 1)
                    with sp.Fori(0, NC // 2) as h:
                        for b in range(2):
                            wait(sp, rows_used[b], h + 1)
                            sp.dma_start(idx[:, b], src[:, bass.ds((h * 2 + b) * T, T)]).then_inc(idx_in[b], 16)

                @block.gpsimd
                def _(pool):
                    with pool.Fori(0, NC // 2) as h:
                        for b in range(2):
                            wait(pool, idx_in[b], (h + 1) * 16)
                            for t in range(T):
                                pool.indirect_dma_start(rows[:, b, t], None, g["table3_d"],
                                                        bass.IndirectOffsetOnAxis(ap=idx[:, b, t:t + 1], axis=0)) \
                                    .then_inc(got[b], 16)

                @block.vector
                def _(v):
                    v.memset(run[:], 0.0)
                    v.memset(keep[:], 0.0)
                    v.sem_inc(rows_used[0], 1)
                    v.sem_inc(rows_used[1], 1)
                    v.wait_ge(loaded, 48)
                    v.tensor_tensor(same[:], keys[:], prev[:], ALU.is_equal)
                    v.tensor_scalar(frac[:], frac[:], 0.0, 1.0, ALU.max, ALU.min)
                    v.drain().then_inc(flags, 1)
                    with v.Fori(0, NC // 2) as h:
                        for b in range(2):
                            c = h * 2 + b
                            up = frac[:, bass.ds(c * (T * D3), T * D3)].rearrange("p (t d) -> p t d", d=D3)
                            v.tensor_scalar(bits[:, :, :, 0], up, -1.0, 1.0, ALU.mult, ALU.add)
                            v.tensor_copy(bits[:, :, :, 1], up)
                            v.drain()
                            v.tensor_tensor(pairs[:], bits[:, :, 1].unsqueeze(3).to_broadcast([P, T, 2, 2]),
                                            bits[:, :, 0].unsqueeze(2).to_broadcast([P, T, 2, 2]), ALU.mult)
                            v.drain()
                            v.tensor_tensor(basis[:].rearrange("p t (k j) -> p t k j", k=2),
                                            bits[:, :, 2].unsqueeze(3).to_broadcast([P, T, 2, 4]),
                                            pairs[:].rearrange("p t k j -> p t (k j)").unsqueeze(2).to_broadcast([P, T, 2, 4]), ALU.mult)
                            wait(v, got[b], (h + 1) * (16 * T))
                            v.drain()
                            r4 = rows[:, b].rearrange("p t (s f) -> p (t s) f", s=S3)
                            v.tensor_tensor(r4, r4, basis[:].rearrange("p t s -> p (t s)").unsqueeze(2).to_broadcast([P, T * S3, C]), ALU.mult)
                            v.drain()
                            v.tensor_reduce(data[:, :, 1:].rearrange("p f t -> p t f"), rows[:, b].rearrange("p t (s f) -> p t f s", s=S3),
                                            AX, ALU.add).then_inc(rows_used[b], 1)
                            v.tensor_copy(data[:, :, 0:1], run[:, 1 - b, :, T:T + 1])
                            wait(v, keep_ready[b], h + 1)
                            wait(v, copied[b], h + 1)
                            v.drain()
                            v.tensor_tensor_scan(run[:, b].rearrange("p f t -> p (f t)"),
                                                 keep[:, b].rearrange("p f t -> p (f t)"),
                                                 data[:].rearrange("p f t -> p (f t)"), 0.0, ALU.mult, ALU.add) \
                             .then_inc(scanned[b], 1)
                            v.drain()
                    v.tensor_copy(tail[:], run[:, 1, :, T])

                @block.scalar
                def _(act):
                    act.wait_ge(flags, 1)
                    for b in range(2):
                        act.sem_inc(copied[b], 1)
                        act.sem_inc(stored[b], 16)
                        act.sem_inc(scanned[b], 1)
                    with act.Fori(0, NC // 2) as h:
                        for b in range(2):
                            wait(act, scanned[b], h + 1)
                            at = bass.ds((h * 2 + b) * T, T)
                            nc.scalar.copy(keep[:, b, :, 1:], same[:, at].unsqueeze(1).to_broadcast([P, C, T])) \
                              .then_inc(keep_ready[b], 1)
                            wait(act, scanned[b], h + 2)
                            wait(act, stored[b], (h + 1) * 16)
                            nc.scalar.copy(outb[:, b], run[:, b, :, 1:].rearrange("p f t -> p t f")).then_inc(copied[b], 1)
                            wait(act, copied[b], h + 2)
                            act.dma_start(g["run_of"](g["sums3_d"], C)[:, bass.ds((h * 2 + b) * (T * C), T * C)],
                                          outb[:, b].rearrange("p t f -> p (t f)")).then_inc(stored[b], 16)
                    for b in range(2):
                        act.wait_ge(stored[b], 16 * (NC // 2 + 1))

        total = collect_sums(nc, sem, g, outer, "l3", g["sums3_d"], tail)
        with ExitStack() as stack:
            s = Space(nc, stack)
            valid = s.sb("l3_valid", [P, NT])
            part = s.sb("l3_part", [P, C])
            moment = s.sb("l3_moment", [P, 2, C])
            deviation = s.sb("l3_deviation", [P, C])
            gamma, beta = s.sb("l3_gamma", [P, C]), s.sb("l3_beta", [P, C])
            ones = s.sb("l3_ones", [P, P])
            recip = s.sb("l3_recip", [P, NT])
            work, work2, stat = s.sb("l3_work", [P, NT, C]), s.sb("l3_work2", [P, NT, C]), s.sb("l3_stat", [P, 3, NT])
            summed = s.ps("l3_summed", [P, 2, 512])
            loaded, parted, added, ready, rooted_, low, high, done, finished = (sem(f"l3c_{n}") for n in (
                "loaded", "parted", "added", "ready", "rooted", "low", "high", "done", "finished"))
            sems = sem("l3c_centred"), sem("l3c_rooted_")
            with nc.Block() as block:
                @block.sync
                def _(sp):
                    sp.dma_start(gamma[:], a["gamma"].to_broadcast([P, C])).then_inc(loaded, 16)
                    sp.dma_start(beta[:], a["beta"].to_broadcast([P, C])).then_inc(loaded, 16)
                    sp.wait_ge(finished, 1)
                    sp.dma_start(out[0:NP - P].rearrange("(t p) c -> p t c", p=P), x[:, 0:NT - 1]).then_inc(done, 16)
                    sp.dma_start(out[NP - P:N], x[0:N - (NP - P), NT - 1]).then_inc(done, 16)
                    sp.wait_ge(done, 32)

                @block.tensor
                def _(pe):
                    for n in range(2):
                        pe.wait_ge(parted, n + 1)
                        nc.tensor.matmul(summed[:, n, 0:C], ones[:], part[:], start=True, stop=True).then_inc(added, 1)

                @block.vector
                def _(v):
                    over_tiles = lambda t: t[:].unsqueeze(1).to_broadcast([P, NT, C])
                    over_features = lambda t: t.unsqueeze(2).to_broadcast([P, NT, C])
                    v.memset(ones[:], 1.0)
                    v.memset(valid[:], 1.0)
                    v.tensor_scalar(recip[:], g["degree"][:], 1.0, None, ALU.max)
                    v.drain()
                    v.tensor_scalar(valid[:, NT - 1:NT], g["run_end"][:], float((N - (NP - P)) * L), None, ALU.is_le)
                    v.reciprocal(recip[:], recip[:])
                    v.drain()
                    v.tensor_tensor(total[:], total[:], over_features(recip[:]), ALU.mult)
                    v.drain()
                    v.tensor_tensor(total[:], total[:], rooted_x[:], ALU.add)
                    v.drain()
                    for n in range(2):
                        if n:
                            v.tensor_tensor(work[:], total[:], total[:], ALU.mult)
                            v.drain()
                        v.tensor_tensor(work[:], work[:] if n else total[:], over_features(valid[:]), ALU.mult)
                        v.drain()
                        v.tensor_reduce(part[:], work[:].rearrange("p t c -> p c t"), AX, ALU.add)
                        v.drain().then_inc(parted, 1)
                        v.wait_ge(added, n + 1)
                        v.tensor_scalar(moment[:, n], summed[:, n, 0:C], 1.0 / N, LN_EPS * n, ALU.mult, ALU.add)
                        v.drain()
                        if n == 0:
                            v.tensor_tensor(total[:], total[:], moment[:, 0].unsqueeze(1).to_broadcast([P, NT, C]), ALU.subtract)
                            v.drain()
                    v.drain().then_inc(ready, 1)
                    v.wait_ge(rooted_, 1)
                    v.reciprocal(deviation[:], deviation[:])
                    v.wait_ge(loaded, 32)
                    v.drain()
                    v.tensor_tensor(deviation[:], deviation[:], gamma[:], ALU.mult)
                    v.drain()
                    v.tensor_tensor(total[:], total[:], over_tiles(deviation), ALU.mult)
                    v.drain()
                    v.tensor_tensor(total[:], total[:], over_tiles(beta), ALU.add)
                    v.drain()
                    v.tensor_scalar(work[:], total[:], 0.0, None, ALU.min)
                    v.drain().then_inc(low, 1)
                    v.tensor_scalar(total[:], total[:], 0.0, -1.0, ALU.max, ALU.add)
                    v.drain()
                    v.tensor_tensor(total[:], total[:], x[:], ALU.add)
                    v.wait_ge(high, 1)
                    v.drain()
                    v.tensor_tensor(total[:], total[:], work2[:], ALU.add)
                    v.drain()
                    normalise(nc, v, None, total[:], x[:], work[:], stat, sems, 1)
                    v.drain().then_inc(finished, 1)

                @block.scalar
                def _(act):
                    act.wait_ge(ready, 1)
                    nc.scalar.activation(deviation[:], moment[:, 1], ACT.Sqrt).then_inc(rooted_, 1)
                    act.wait_ge(low, 1)
                    nc.scalar.activation(work2[:], work[:], ACT.Exp).then_inc(high, 1)
                    normalise(nc, None, act, None, None, None, stat, sems, 1)


def laid_out(inputs):
    n = {k: np.asarray(v) for k, v in inputs.items()}

    def padded(t, rows, fill=0):
        t = np.asarray(t)
        more = np.full((rows - t.shape[0],) + t.shape[1:], fill, t.dtype)
        return np.ascontiguousarray(np.concatenate([t, more]))

    arrays = {"x": padded(n["x"], NP), "edge_weight": padded(n["edge_weight"], EP).reshape(EP, 1)}
    for k in ("src", "dst"):
        arrays[k] = padded(n[k], EP, N).reshape(EP, 1)
    arrays["dst_before"] = np.concatenate([np.full((1, 1), -1, n["dst"].dtype), arrays["dst"][:-1]])
    arrays["attr3"] = padded(n["edge_attr_3"], EP)
    arrays["attr5"] = padded(n["edge_attr_5"], EP)
    arrays["attr32"] = padded(n["edge_attr_32"], EP)
    lin, edge = n["L1_gnn_W_lin"].reshape(C, H, C), n["L1_gnn_W_edge"].reshape(D5, H, C)
    b_lin, b_edge = n["L1_gnn_b_lin"].reshape(1, H, C), n["L1_gnn_b_edge"].reshape(1, H, C)
    arrays["att1"] = n["L1_gnn_att"].reshape(H, 2, C).transpose(2, 1, 0).reshape(C, 2 * H)
    arrays["proj1"] = np.concatenate([lin, b_lin, edge, b_edge]).transpose(2, 1, 0)
    arrays["out1"] = np.concatenate([lin, edge, b_lin])
    arrays["out1_bias"] = b_edge
    arrays["bias1"] = n["L1_gnn_bias"].reshape(1, C)
    wk, wv, we = (n[f"L2_gnn_{k}"].reshape(-1, H, C) for k in ("Wk", "Wv", "We"))
    bk, bv = n["L2_gnn_bk"].reshape(1, H, C), n["L2_gnn_bv"].reshape(1, H, C)
    arrays["wq"] = n["L2_gnn_Wq"]
    arrays["bq"] = n["L2_gnn_bq"].reshape(H * C, 1)
    keys = np.zeros((H, C, H, F2), n["L2_gnn_Wk"].dtype)
    for h in range(H):
        keys[h, :, h] = np.concatenate([wk, we, bk])[:, h].T
    arrays["keys2"] = keys.reshape(H * C, H * F2)
    arrays["values2"] = np.concatenate([wv, we, bv])
    arrays["wp"] = n["L2_gnn_Wp"].reshape(H, C, C).transpose(1, 0, 2)
    for k in ("ln1_g", "ln1_b", "ln2_g", "ln2_b", "bp", "b2"):
        arrays[k] = n[f"L2_gnn_{k}"].reshape(1, C)
    arrays["w1"], arrays["w2"] = n["L2_gnn_W1"], n["L2_gnn_W2"]
    arrays["b1"] = n["L2_gnn_b1"].reshape(C, 1)
    arrays["spline"] = n["L3_gnn_W"].transpose(1, 0, 2).reshape(C, S3 * C)
    arrays["root"] = n["L3_gnn_root"]
    arrays["gamma"], arrays["beta"] = n["L3_gnn_gamma"].reshape(1, C), n["L3_gnn_beta"].reshape(1, C)
    return {f"in_{k}": np.ascontiguousarray(v) for k, v in arrays.items()}


def kernel(**inputs):
    import concourse.bacc as bacc
    from concourse.bass_utils import run_bass_kernel_spmd

    arrays = laid_out(inputs)
    nc = bacc.Bacc("TRN2", target_bir_lowering=False, num_devices=1)
    a = {k[3:]: nc.dram_tensor(k, v.shape, mybir.dt.from_np(v.dtype), kind="ExternalInput").ap()
         for k, v in arrays.items()}
    out = nc.dram_tensor("out_0_dram", (N, C), F32, kind="ExternalOutput").ap()
    build(nc, a, out)
    r = run_bass_kernel_spmd(nc, [arrays], core_ids=[0])
    return r.results[0]["out_0_dram"]
```

```python
from contextlib import ExitStack

import numpy as np

import concourse.bass as bass
from concourse import mybir

F32 = mybir.dt.float32
I32 = mybir.dt.int32
BF16 = mybir.dt.bfloat16
ALU = mybir.AluOpType
ACT = mybir.ActivationFunctionType
AX = mybir.AxisListType.X

P = 128
N = 6250
E = 200000
C = 64
NT = -(-N // P)
NP = NT * P
L = 1568
EP = P * L
assert EP >= E and NP > N
H = 2
D5, D32, D3 = 5, 32, 3
FAR = 1.0e30
OFF = 1.0e7
LN_EPS = 1e-5

F1 = C + D5 + 1
R1 = F1 + H
B1 = C + H + 1
F2 = C + D32 + 1
B2 = H * F2 + H
S3 = 2 ** D3
T1 = 28
T2 = 14
SB = 7


UNROLL = 4


class Chunk:

    def __init__(self, g, r):
        self.g, self.r, self.b = g, r, r % 2
        self.h = g * (UNROLL // 2) + r // 2
        self.at = g * UNROLL + r

    def next(self, count):
        if isinstance(self.g, int) and self.at + 1 == count:
            return None
        return Chunk(self.g, self.r + 1) if self.r + 1 < UNROLL else Chunk(self.g + 1, 0)


def chunks(eng, count):
    with eng.Fori(0, count // UNROLL) as g:
        for r in range(UNROLL):
            yield Chunk(g, r)


def chunks_ahead(eng, count, first, second):
    first(Chunk(0, 0))
    with eng.Fori(0, count // UNROLL - 1) as g:
        for r in range(UNROLL):
            first(Chunk(g, r + 1) if r + 1 < UNROLL else Chunk(g + 1, 0))
            second(Chunk(g, r))
    last = count // UNROLL - 1
    for r in range(UNROLL):
        if r + 1 < UNROLL:
            first(Chunk(last, r + 1))
        second(Chunk(last, r))


def wait(eng, sem, value):
    eng.wait_ge(sem, value)
    eng.nop(nofuse=True)


def build(nc, a, out):
    top = ExitStack()

    in_use = []

    def sem(name):
        in_use.append(nc.alloc_semaphore(name=name))
        return in_use[-1]

    def clear_semaphores():
        nc.all_engine_barrier()
        nc.clear_and_free_semaphores(in_use)
        in_use.clear()
        nc.all_engine_barrier()

    def dram(name, shape, dt=F32):
        return nc.dram_tensor(name, shape, dt, kind="Internal").ap()

    first_d = {k: dram(f"first_{k}", (NP + 1, 1)) for k in ("src", "dst")}
    pos_d = dram("pos", (P, L), I32)
    sums0_d = dram("sums0", (EP, C))
    table1_d = dram("table1", (NP, B1))
    tablea_d = dram("tablea", (NP, H + 1))
    spread1_d = dram("spread1", (EP, B1))
    spreada_d = dram("spreada", (EP, H + 1))
    rows1_d = dram("rows1", (EP, R1))
    sums1_d = dram("sums1", (EP, H * F1 + H))
    h2_d = dram("h2", (NP, C))
    table2_d = dram("table2", (NP, B2))
    spread2_d = dram("spread2", (EP, B2))
    sums2_d = dram("sums2", (EP, H * F2 + H))
    table3_d = dram("table3", (NP, S3 * C))
    sums3_d = dram("sums3", (EP, C))

    e = {k: dram(f"sorted_{k}", (EP, w), dt) for k, w, dt in ARRAYS + (("dst_before", 1, I32),)}

    def run_of(t, w):
        return t.rearrange("(p l) w -> p (l w)", p=P)

    with top:
        def keep_tile(name, shape, dt=F32):
            return top.enter_context(nc.sbuf_tensor(name, shape, dt))

        x = keep_tile("x", [P, NT, C])
        identity = keep_tile("identity", [P, P])
        run_end = keep_tile("run_end", [P, 1])
        end_idx = {k: keep_tile(f"end_idx_{k}", [P, NT], I32) for k in ("src", "dst")}
        start_idx = {k: keep_tile(f"start_idx_{k}", [P, NT], I32) for k in ("src", "dst")}
        filled = {k: keep_tile(f"filled_{k}", [P, NT]) for k in ("src", "dst")}
        degree = keep_tile("degree", [P, NT])
        head_key = {k: keep_tile(f"head_key_{k}", [P, 1], I32) for k in ("src", "dst")}
        tail_key = {k: keep_tile(f"tail_key_{k}", [P, 1]) for k in ("src", "dst")}
        cross_key = {k: keep_tile(f"cross_key_{k}", [P, 1]) for k in ("src", "dst")}
        last_key = {k: keep_tile(f"last_key_{k}", [P, 1]) for k in ("src", "dst")}

        first = {k: keep_tile(f"first_pos_{k}", [P, NT]) for k in ("src", "dst")}
        zeros = keep_tile("zeros", [P, 2048])
        iota_b, ident_b, not_upper_b = (keep_tile(n, [P, P], BF16) for n in ("iota_b", "ident_b", "not_upper_b"))
        upper, ones = keep_tile("upper", [P, P]), keep_tile("ones", [P, P])
        zero_b = keep_tile("zero_b", [P, P], BF16)
        total = keep_tile("total_edges", [1, 2])
        unsorted = keep_tile("unsorted", [P, 1], I32)
        iota_f, tile_base = keep_tile("iota_f", [P, P]), keep_tile("tile_base", [P, NT])
        ordering(nc, a, sem, dict(locals()))
        layer0(nc, a, sem, dict(locals()))
        layer1(nc, a, sem, dict(locals()))
        clear_semaphores()
        layer2(nc, a, sem, dict(locals()))
        layer3(nc, a, sem, dict(locals()), out)


def clear_part(g, sp, cleared, target, w, turn, turns):
    width = L * w // turns
    assert width * turns == L * w
    step = max(d for d in range(1, 2049) if width % d == 0)
    for c in range(width // step):
        sp.dma_start(g["run_of"](g[target], w)[:, bass.ds(turn * width + c * step, step)], g["zeros"][:, 0:step]).then_inc(cleared, 16)
    return width // step


class Space:

    def __init__(self, nc, stack):
        self.nc, self.stack = nc, stack

    def sb(self, name, shape, dt=F32):
        return self.stack.enter_context(self.nc.sbuf_tensor(name, shape, dt))

    def ps(self, name, shape, dt=F32):
        return self.stack.enter_context(self.nc.psum_tensor(name, shape, dt))


class Counts:

    def __init__(self, s, sem, name):
        self.count = s.sb(f"{name}_count_of", [P, NT])
        self.col_sum, self.prefix = s.sb(f"{name}_col_sum", [P, NT + 1]), s.sb(f"{name}_prefix", [P, NT + 1])
        self.after, self.tmp, self.tmp2 = (s.sb(f"{name}_{n}", [P, NT]) for n in ("after", "tmp", "tmp2"))
        self.edge, self.ended = s.sb(f"{name}_edge", [P, 4]), s.sb(f"{name}_ended", [P, 2, 4])
        self.ones = s.sb(f"{name}_scan_ones", [P, NT + 1])
        self.sizes_ready, self.tri_ready, self.first_ready = (sem(f"{name}_{n}") for n in ("sizes_ready", "tri_ready", "first_ready"))

    def tensor(self, nc, pe, g, hist, turn):
        pe.wait_ge(self.sizes_ready, turn)
        nc.tensor.matmul(hist[:, 64:64 + NT], g["ones"][:], self.count[:], start=True, stop=True, skip_group_check=True)
        nc.tensor.matmul(hist[:, 128:128 + NT], g["upper"][:], self.count[:], start=True, stop=True,
                         skip_group_check=True).then_inc(self.tri_ready, 1)

    def first_positions(self, v, g, k, hist, turn):
        v.tensor_copy(self.count[:], hist[:, 0:NT])
        v.memset(self.col_sum[:], 0.0)
        v.memset(self.ones[:], 1.0)
        v.drain().then_inc(self.sizes_ready, 1)
        v.wait_ge(self.tri_ready, turn)
        v.tensor_copy(self.col_sum[:, 1:NT + 1], hist[:, 64:64 + NT])
        v.drain()
        v.tensor_tensor_scan(self.prefix[:], self.ones[:], self.col_sum[:], 0.0, ALU.mult, ALU.add)
        v.drain()
        first = g["first"][k]
        v.tensor_tensor(first[:], self.prefix[:, 0:NT], hist[:, 128:128 + NT], ALU.add)
        if k == "dst":
            v.tensor_copy(g["degree"][:], self.count[:])
        v.tensor_scalar(g["filled"][k][:], self.count[:], 0.5, None, ALU.is_gt)
        v.drain().then_inc(self.first_ready, 1)
        v.tensor_tensor(self.after[:], first[:], self.count[:], ALU.add)
        v.tensor_scalar(self.tmp2[:], g["filled"][k][:], -OFF, OFF, ALU.mult, ALU.add)
        v.drain()
        v.tensor_scalar(self.tmp[:], self.after[:], -1.0, 0.0, ALU.add, ALU.max)
        v.tensor_tensor(self.tmp2[:], self.tmp2[:], first[:], ALU.add)
        v.drain()
        v.tensor_copy(g["end_idx"][k][:], self.tmp[:])
        v.tensor_copy(g["start_idx"][k][:], self.tmp2[:])
        v.drain()

    def partition_nodes(self, v, g, k, ends_row, scratch_row):
        for n, past in enumerate((-float(L), -1.0, 0.0, float(L))):
            v.tensor_scalar(self.edge[:, n:n + 1], g["run_end"][:], past, None, ALU.add)
        v.drain()
        half = NP // 2
        for part in range(2):
            for n in range(4):
                v.tensor_scalar(scratch_row[:], ends_row[:, part * half:(part + 1) * half], self.edge[:, n:n + 1], 0.0,
                                ALU.is_le, ALU.add, accum_out=self.ended[:, part, n:n + 1])
                v.drain()
        v.tensor_tensor(self.ended[:, 0], self.ended[:, 0], self.ended[:, 1], ALU.add)
        v.drain()
        head, tail, through, after = (self.ended[:, 0, n:n + 1] for n in range(4))
        v.tensor_copy(g["head_key"][k][:], head)
        v.tensor_copy(g["tail_key"][k][:], tail)
        v.tensor_tensor(through, through, tail, ALU.is_gt)
        v.tensor_tensor(after, after, tail, ALU.is_gt)
        v.drain()
        v.tensor_scalar(through, through, -OFF, None, ALU.mult)
        v.tensor_scalar(after, after, OFF, -OFF, ALU.mult, ALU.add)
        v.drain()
        v.tensor_tensor(g["cross_key"][k][:], tail, through, ALU.add)
        v.drain()
        v.tensor_tensor(g["last_key"][k][:], g["cross_key"][k][:], after, ALU.add)
        return v.drain()


def split_keys(v, key, part, low, high):
    v.tensor_scalar(part[:], key[:], P - 1, None, ALU.bitwise_and)
    v.drain()
    v.tensor_copy(low[:, 0:L], part[:])
    v.drain()
    v.tensor_scalar(part[:], key[:], 7, None, ALU.arith_shift_right)
    v.drain()
    v.tensor_copy(high[:, 0:L], part[:])
    v.drain()


def one_hots(v, hot_low, hot_high, iota_b, low, high, step):
    at = bass.ds(step * SB, SB)
    v.tensor_tensor(hot_low, iota_b[:].unsqueeze(1).to_broadcast([P, SB, P]),
                    low[:, at].unsqueeze(2).to_broadcast([P, SB, P]), ALU.is_equal)
    return v.tensor_tensor(hot_high, iota_b[:, 0:NT].unsqueeze(1).to_broadcast([P, SB, NT]),
                           high[:, at].unsqueeze(2).to_broadcast([P, SB, NT]), ALU.is_equal)


HOT = 4
TURN = 8


class Ranking:

    def __init__(self, s, sem, name, g, hists):
        self.hists, self.zero_b = hists, g["zero_b"]
        self.iota_b, self.ident_b, self.not_upper_b = g["iota_b"], g["ident_b"], g["not_upper_b"]
        self.low, self.high = s.sb(f"{name}_low", [P, L + 3 * SB], BF16), s.sb(f"{name}_high", [P, L + 3 * SB], BF16)
        self.key, self.part = s.sb(f"{name}_key", [P, L], I32), s.sb(f"{name}_part", [P, L], I32)
        self.hot_low = s.sb(f"{name}_hot_low", [P, HOT, SB, P], BF16)
        self.hot_high = s.sb(f"{name}_hot_high", [P, HOT, SB, NT], BF16)
        self.low_t = s.sb(f"{name}_low_t", [P, 2, SB * P], BF16)
        self.low_tf = s.sb(f"{name}_low_tf", [P, HOT, SB * P])
        self.earlier = s.sb(f"{name}_earlier", [P, 2, SB, P], BF16)
        self.added = s.sb(f"{name}_added", [P, NT, SB + 1])
        self.goes_on = s.sb(f"{name}_goes_on", [P, NT, SB + 1])
        self.before = s.sb(f"{name}_before", [P, 2, NT, SB + 1])
        self.picked = s.sb(f"{name}_picked", [P, SB, NT])
        self.pos_f = s.sb(f"{name}_pos_f", [P, L + SB])
        self.pos_i = s.sb(f"{name}_pos_i", [P, L], I32)
        self.turned = s.ps(f"{name}_turned", [P, 2, 1024], BF16)
        self.same = s.ps(f"{name}_same", [P, 8, P])
        self.rank = s.ps(f"{name}_rank", [P, 2, 8, C])
        self.count = s.ps(f"{name}_count", [P, 2, 512])
        self.hot = [sem(f"{name}_hot{r}") for r in range(HOT)]
        self.hist_used, self.copied_f = sem(f"{name}_hist_used"), sem(f"{name}_copied_f")
        self.turned_ready, self.copied, self.same_ready, self.masked, self.counted, self.based, self.ranked, self.read, self.ready = (
            sem(f"{name}_{n}") for n in ("turned_ready", "copied", "same_ready", "masked", "counted", "based", "ranked", "read", "ready"))

    def hist(self, n):
        return self.rank[:, n].rearrange("p j c -> p (j c)")

    def hist_tensor_start(self, nc, pe, n):
        wait(pe, self.hot[0], L // SB // HOT * n + 1)
        nc.tensor.matmul(self.hist(n)[:, 0:NT], self.zero_b[:], self.zero_b[:, 0:NT], start=True, stop=False, skip_group_check=True)

    def hist_tensor(self, nc, pe, n, h):
        for r in range(TURN):
            wait(pe, self.hot[r % HOT], h * (TURN // HOT) + (L // SB // HOT * n + r // HOT + 1))
            for j in range(SB):
                last = nc.tensor.matmul(self.hist(n)[:, 0:NT], self.hot_low[:, r % HOT, j], self.hot_high[:, r % HOT, j],
                                        start=False, stop=False, skip_group_check=True)
            last.then_inc(self.hist_used, 1)

    def hist_vector_start(self, v, n):
        if n == 0:
            v.sem_inc(self.hist_used, HOT)
            v.memset(self.low[:, L:], 0.0)
            v.memset(self.high[:, L:], 0.0)
            v.drain()
        split_keys(v, self.key, self.part, self.low, self.high)

    def hist_vector(self, v, n, h):
        for r in range(TURN):
            wait(v, self.hist_used, h * TURN + (L // SB * n + r + 1))
            one_hots(v, self.hot_low[:, r % HOT], self.hot_high[:, r % HOT], self.iota_b, self.low, self.high, self.at(h, r)).then_inc(self.hot[r % HOT], 1)

    def hist_vector_end(self, v, n):
        v.wait_ge(self.hist_used, L // SB * (n + 1) + HOT)

    @staticmethod
    def at(h, r):
        return h * TURN + r

    @staticmethod
    def after(h, r, n):
        return (h, r + n) if r + n < TURN else (h + 1, r + n - TURN)

    def tensor_start(self, nc, pe):
        self.tensor_ahead(nc, pe, 0, 0)
        self.tensor_same(nc, pe, 0, 0)
        self.tensor_ahead(nc, pe, 0, 1)

    def tensor_ahead(self, nc, pe, h, r):
        q = r % HOT
        wait(pe, self.hot[q], h * (TURN // HOT) + (L // SB // HOT * self.hists + r // HOT + 1))
        for j in range(SB):
            last = nc.tensor.matmul(self.count[:, r % 2, j * NT:(j + 1) * NT], self.hot_low[:, q, j], self.hot_high[:, q, j], start=True, stop=True)
        last.then_inc(self.counted, 1)
        for j in range(SB):
            last = nc.tensor.transpose(self.turned[:, r % 2, j * P:(j + 1) * P], self.hot_low[:, q, j], self.ident_b[:])
        last.then_inc(self.turned_ready, 1)

    def tensor_same(self, nc, pe, h, r):
        wait(pe, self.copied, self.at(h, r) + 1)
        for j in range(SB):
            t = self.low_t[:, r % 2, j * P:(j + 1) * P]
            nc.tensor.matmul(self.same[:, j], t, t, start=True, stop=False)
            last = nc.tensor.matmul(self.same[:, j], self.ident_b[:], self.not_upper_b[:], start=False, stop=True)
        last.then_inc(self.same_ready, 1)

    def tensor_step(self, nc, pe, h, r):
        s, b = self.at(h, r), r % 2
        wait(pe, self.masked, s + 1)
        self.tensor_same(nc, pe, *self.after(h, r, 1))
        wait(pe, self.based, s + 1)
        self.tensor_ahead(nc, pe, *self.after(h, r, 2))
        wait(pe, self.read, s + 1)
        for j in range(SB):
            nc.tensor.matmul(self.rank[:, b, j, 0:NT], self.earlier[:, b, j], self.hot_high[:, r % HOT, j], start=True, stop=False)
            last = nc.tensor.matmul(self.rank[:, b, j, 0:NT], self.low_tf[:, r % HOT, j * P:(j + 1) * P], self.before[:, b, :, j], start=False, stop=True)
        last.then_inc(self.ranked, 1)

    def scalar_start(self, nc, act):
        self.scalar_copies(nc, act, 0, 0)

    def scalar_copies(self, nc, act, h, r):
        wait(act, self.turned_ready, self.at(h, r) + 1)
        nc.scalar.copy(self.low_t[:, r % 2], self.turned[:, r % 2, 0:SB * P]).then_inc(self.copied, 1)
        nc.scalar.copy(self.low_tf[:, r % HOT], self.turned[:, r % 2, 0:SB * P]).then_inc(self.copied_f, 1)

    def scalar_step(self, nc, act, h, r):
        wait(act, self.same_ready, self.at(h, r) + 1)
        wait(act, self.copied_f, self.at(h, r) + 1)
        nc.scalar.activation(self.earlier[:, r % 2], self.same[:, 0:SB], ACT.Relu).then_inc(self.masked, 1)
        self.scalar_copies(nc, act, *self.after(h, r, 1))

    def vector_start(self, v, first):
        v.memset(self.goes_on[:], 1.0)
        v.memset(self.rank[:], 0.0)
        v.memset(self.hot_high[:], 0.0)
        v.sem_inc(self.ranked, 1)
        v.sem_inc(self.read, 1)
        v.drain()
        v.memset(self.goes_on[:, :, 0], 0.0)
        v.tensor_copy(self.before[:, 1, :, SB], first[:])
        v.drain()
        for r in range(3):
            one_hots(v, self.hot_low[:, r], self.hot_high[:, r], self.iota_b, self.low, self.high, r).then_inc(self.hot[r], 1)
        self.bases(v, 0, 0)

    def bases(self, v, h, r):
        b = r % 2
        wait(v, self.counted, self.at(h, r) + 1)
        v.tensor_copy(self.added[:, :, 1:], self.count[:, b, 0:SB * NT].rearrange("p (j n) -> p n j", j=SB))
        v.tensor_copy(self.added[:, :, 0], self.before[:, 1 - b, :, SB])
        v.drain()
        v.tensor_tensor_scan(self.before[:, b].rearrange("p n j -> p (n j)"), self.goes_on[:].rearrange("p n j -> p (n j)"),
                             self.added[:].rearrange("p n j -> p (n j)"), 0.0, ALU.mult, ALU.add).then_inc(self.based, 1)

    def pick(self, v, s, r):
        b = (r - 1) % 2
        wait(v, self.ranked, s + 1)
        v.tensor_tensor(self.picked[:], self.rank[:, b, 0:SB, 0:NT], self.hot_high[:, (r - 1) % HOT], ALU.mult).then_inc(self.read, 1)
        v.drain()
        v.tensor_reduce(self.pos_f[:, bass.ds(s * SB, SB)], self.picked[:], AX, ALU.add)

    def vector_step(self, v, h, r):
        s, q = self.at(h, r), (r + 3) % HOT
        self.pick(v, s, r)
        self.bases(v, *self.after(h, r, 1))
        one_hots(v, self.hot_low[:, q], self.hot_high[:, q], self.iota_b, self.low, self.high, s + 3).then_inc(self.hot[q], 1)
        v.drain()

    def vector_end(self, v):
        self.pick(v, L // SB, 0)
        v.drain()
        v.tensor_copy(self.pos_i[:], self.pos_f[:, SB:])
        v.drain().then_inc(self.ready, 1)


ARRAYS = (("src", 1, I32), ("dst", 1, I32), ("edge_weight", 1, F32), ("attr3", D3, F32), ("attr5", D5, F32), ("attr32", D32, F32))


def branch(eng, g, sort, keep=None):
    unsorted = eng.value_load(g["unsorted"][0:1, 0:1], min_val=0, max_val=1)
    with eng.If(unsorted > 0):
        sort()
    with eng.Else():
        if keep:
            keep()
        else:
            eng.nop()


def ordering(nc, a, sem, g):
    with ExitStack() as stack:
        s = Space(nc, stack)
        flag = g["unsorted"]
        minus = s.sb("minus", [1, 2], I32)
        with ExitStack() as inner:
            s = Space(nc, inner)
            iota_i, row_i, tiles_i = s.sb("iota_i", [P, P], I32), s.sb("row_i", [P, 1], I32), s.sb("tiles_i", [P, NT], I32)
            row_f, col_f = s.sb("row_f", [P, 1]), g["iota_f"]
            key, before_key = s.sb("o_key", [P, L], I32), s.sb("o_before_key", [P, L], I32)
            falls, fell = s.sb("falls", [P, L], BF16), s.sb("fell", [P, 1])
            fall_ps = s.ps("fall_ps", [P, 512])
            loaded, drawn, checked, fallen = (sem(f"o_{n}") for n in ("loaded", "drawn", "checked", "fallen"))
            with nc.Block() as block:
                @block.sync
                def _(sp):
                    sp.dma_start(key[:], g["run_of"](a["dst"], 1)).then_inc(loaded, 16)
                    sp.dma_start(before_key[:], g["run_of"](a["dst_before"], 1)).then_inc(loaded, 16)

                @block.gpsimd
                def _(pool):
                    nc.gpsimd.iota(iota_i[:], [[1, P]], base=0, channel_multiplier=0).then_inc(drawn, 1)
                    nc.gpsimd.iota(tiles_i[:], [[P, NT]], base=0, channel_multiplier=0).then_inc(drawn, 1)
                    nc.gpsimd.iota(row_i[:], [[0, 1]], base=0, channel_multiplier=1).then_inc(drawn, 1)

                @block.tensor
                def _(pe):
                    pe.wait_ge(checked, 1)
                    nc.tensor.matmul(fall_ps[:, 0:1], g["ones"][:], fell[:], start=True, stop=True).then_inc(fallen, 1)

                @block.vector
                def _(v):
                    v.wait_ge(drawn, 3)
                    v.tensor_copy(g["tile_base"][:], tiles_i[:])
                    v.tensor_copy(g["iota_b"][:], iota_i[:])
                    v.tensor_copy(col_f[:], iota_i[:])
                    v.tensor_copy(row_f[:], row_i[:])
                    v.memset(g["ones"][:], 1.0)
                    v.memset(g["zero_b"][:], 0.0)
                    v.memset(g["zeros"][:], 0.0)
                    v.memset(g["total"][:], float(EP))
                    v.memset(minus[:], -1)
                    v.drain()
                    row = row_f[:, 0:1]
                    v.tensor_scalar(g["identity"][:], col_f[:], row, None, ALU.is_equal)
                    v.tensor_scalar(g["ident_b"][:], col_f[:], row, None, ALU.is_equal)
                    v.tensor_scalar(g["upper"][:], col_f[:], row, None, ALU.is_gt)
                    v.tensor_scalar(g["not_upper_b"][:], col_f[:], row, -1.0, ALU.is_gt, ALU.add)
                    v.tensor_scalar(g["run_end"][:], row_f[:], float(L), float(L), ALU.mult, ALU.add)
                    v.wait_ge(loaded, 32)
                    v.tensor_tensor(falls[:], key[:], before_key[:], ALU.is_lt)
                    v.drain()
                    v.tensor_reduce(fell[:], falls[:], AX, ALU.max)
                    v.drain().then_inc(checked, 1)
                    v.wait_ge(fallen, 1)
                    v.tensor_scalar(fell[:], fall_ps[:, 0:1], 1.0, None, ALU.min)
                    v.drain()
                    v.tensor_copy(flag[:], fell[:])

        with ExitStack() as inner:
            s = Space(nc, inner)
            ranking = Ranking(s, sem, "d", g, 1)
            counts = Counts(s, sem, "d")
            T, NC = T1, L // T1
            idx = s.sb("d_idx", [P, T], I32)
            rows = {k: s.sb(f"d_{k}", [P, T, w], dt) for k, w, dt in ARRAYS}
            keys_in, pos_out, chunk_in, chunk_free, soon, shifted = (sem(f"d_{n}") for n in (
                "keys_in", "pos_out", "chunk_in", "chunk_free", "soon", "shifted"))
            sent = {k: sem(f"d_sent_{k}") for k, _, _ in ARRAYS}
            turns = L // SB // TURN
            with nc.Block() as block:
                @block.sync
                def _(sp):
                    def sort():
                        sp.dma_start(ranking.key[:], g["run_of"](a["dst"], 1)).then_inc(keys_in, 16)
                        sp.wait_ge(ranking.ready, 1)
                        sp.dma_start(g["pos_d"], ranking.pos_i[:]).then_inc(pos_out, 16)
                        sp.wait_ge(pos_out, 16)
                        with sp.Fori(0, NC) as c:
                            wait(sp, chunk_free, c + 1)
                            sp.dma_start(idx[:], g["pos_d"][:, bass.ds(c * T, T)]).then_inc(chunk_in, 16)
                            for k, w, _ in ARRAYS:
                                sp.dma_start(rows[k][:].rearrange("p t w -> p (t w)"), g["run_of"](a[k], w)[:, bass.ds(c * (T * w), T * w)]).then_inc(chunk_in, 16)
                        sp.wait_ge(chunk_free, NC + 1)
                        sp.dma_start(g["e"]["dst_before"][1:EP], g["e"]["dst"][0:EP - 1]).then_inc(shifted, 16)
                        sp.dma_start(g["e"]["dst_before"][0:1], minus[:, 0:1]).then_inc(shifted, 16)
                        sp.wait_ge(shifted, 32)

                    def keep():
                        for k, w in (("src", 1), ("dst", 1), ("dst_before", 1), ("edge_weight", 1)):
                            sp.dma_start(g["run_of"](g["e"][k], w), g["run_of"](a[k], w)).then_inc(soon, 16)
                        sp.wait_ge(soon, 64)
                    branch(sp, g, sort, keep)

                @block.tensor
                def _(pe):
                    def sort():
                        ranking.hist_tensor_start(nc, pe, 0)
                        with pe.Fori(0, turns) as h:
                            ranking.hist_tensor(nc, pe, 0, h)
                        counts.tensor(nc, pe, g, ranking.hist(0), 1)
                        ranking.tensor_start(nc, pe)
                        with pe.Fori(0, turns) as h:
                            for r in range(TURN):
                                ranking.tensor_step(nc, pe, h, r)
                    branch(pe, g, sort)

                @block.scalar
                def _(act):
                    def sort():
                        ranking.scalar_start(nc, act)
                        with act.Fori(0, turns) as h:
                            for r in range(TURN):
                                ranking.scalar_step(nc, act, h, r)
                    branch(act, g, sort)

                @block.vector
                def _(v):
                    def sort():
                        v.wait_ge(keys_in, 16)
                        ranking.hist_vector_start(v, 0)
                        with v.Fori(0, turns) as h:
                            ranking.hist_vector(v, 0, h)
                        ranking.hist_vector_end(v, 0)
                        counts.first_positions(v, g, "dst", ranking.hist(0), 1)
                        ranking.vector_start(v, g["first"]["dst"])
                        with v.Fori(0, turns) as h:
                            for r in range(TURN):
                                ranking.vector_step(v, h, r)
                        ranking.vector_end(v)
                    branch(v, g, sort)

                @block.gpsimd
                def _(pool):
                    def sort():
                        pool.sem_inc(chunk_free, 1)
                        with pool.Fori(0, NC) as c:
                            wait(pool, chunk_in, (c + 1) * (16 * (1 + len(ARRAYS))))
                            for k, w, _ in ARRAYS:
                                for t in range(T):
                                    pool.indirect_dma_start(g["e"][k], bass.IndirectOffsetOnAxis(ap=idx[:, t:t + 1], axis=0),
                                                            rows[k][:, t], None).then_inc(sent[k], 16)
                            for k, _, _ in ARRAYS:
                                wait(pool, sent[k], (c + 1) * (16 * T))
                            pool.sem_inc(chunk_free, 1)
                    branch(pool, g, sort)


def node_mask(v, g, key, tiles, mask):
    v.tensor_scalar(tiles, g["tile_base"][:], -1.0, key[:, 0:1], ALU.mult, ALU.add)
    v.drain()
    v.tensor_tensor(mask[:].rearrange("p (t n) -> p t n", n=P), g["iota_f"][:].unsqueeze(1).to_broadcast([P, NT, P]),
                    tiles.unsqueeze(2).to_broadcast([P, NT, P]), ALU.is_equal)
    return v.drain()


def normalise(nc, v, act, sums, out_, work, stat, sems, turn, gain=None, shift=None):
    centred, rooted = sems
    if v is not None:
        v.tensor_reduce(stat[:, 0], sums, AX, ALU.add)
        v.drain()
        v.tensor_scalar(stat[:, 0], stat[:, 0], 1.0 / C, None, ALU.mult)
        v.drain()
        v.tensor_tensor(sums, sums, stat[:, 0].unsqueeze(2).to_broadcast([P, NT, C]), ALU.subtract)
        v.drain()
        v.tensor_tensor(work, sums, sums, ALU.mult)
        v.drain()
        v.tensor_reduce(stat[:, 1], work, AX, ALU.add)
        v.drain()
        v.tensor_scalar(stat[:, 1], stat[:, 1], 1.0 / C, LN_EPS, ALU.mult, ALU.add).then_inc(centred, 1)
        v.wait_ge(rooted, turn)
        v.reciprocal(stat[:, 1], stat[:, 2])
        v.drain()
        v.tensor_tensor(out_, sums, stat[:, 1].unsqueeze(2).to_broadcast([P, NT, C]), ALU.mult)
        v.drain()
        if gain is not None:
            v.tensor_tensor(out_, out_, gain[:].unsqueeze(1).to_broadcast([P, NT, C]), ALU.mult)
            v.drain()
            v.tensor_tensor(out_, out_, shift[:].unsqueeze(1).to_broadcast([P, NT, C]), ALU.add)
            v.drain()
    if act is not None:
        act.wait_ge(centred, turn)
        nc.scalar.activation(stat[:, 2], stat[:, 1], ACT.Sqrt).then_inc(rooted, 1)


def layer0(nc, a, sem, g):
    T, NC = T1, L // T1
    x, e = g["x"], g["e"]
    turns = L // SB // TURN
    assert turns == NC // 2 and turns % 4 == 0
    KEYS = ("dst", "src")
    with ExitStack() as outer:
        tail = Space(nc, outer).sb("l0_tail", [P, C])
        with ExitStack() as stack:
            s = Space(nc, stack)
            ranking = Ranking(s, sem, "r", g, len(KEYS))
            counts = Counts(s, sem, "r")
            ends_row, scratch_row = s.sb("l0_ends_row", [P, NP]), s.sb("l0_scratch_row", [P, NP // 2], BF16)
            idx = s.sb("l0_idx", [P, 2, T], I32)
            rows = s.sb("l0_rows", [P, 2, T, C])
            data = s.sb("l0_data", [P, C, T + 1])
            keep = s.sb("l0_keep", [P, 2, C, T + 1])
            run = s.sb("l0_run", [P, 2, C, T + 1])
            outb = s.sb("l0_out", [P, 2, T, C])
            weight = s.sb("l0_weight", [P, L])
            prev = ranking.pos_i
            same = s.sb("l0_same", [P, L])
            two = lambda n: [sem(f"l0_{n}{b}") for b in range(2)]
            idx_in, got, rows_used, keep_ready, scanned, copied, stored = (two(n) for n in (
                "idx_in", "got", "rows_used", "keep_ready", "scanned", "copied", "stored"))
            loaded, flags, x_in, keys_in, keys_split, cleared, pos_out, first_out, ends_in, ends_read, attr_copied = (sem(f"l0_{n}") for n in (
                "loaded", "flags", "x_in", "keys_in", "keys_split", "cleared", "pos_out", "first_out", "ends_in", "ends_read", "attr_copied"))
            with nc.Block() as block:
                @block.sync
                def _(sp):
                    sp.dma_start(ranking.key[:], g["run_of"](e["dst"], 1)).then_inc(keys_in, 16)
                    sp.dma_start(prev[:], g["run_of"](e["dst_before"], 1)).then_inc(keys_in, 16)
                    sp.dma_start(weight[:], g["run_of"](e["edge_weight"], 1)).then_inc(loaded, 16)
                    sp.wait_ge(keys_split, 1)
                    sp.dma_start(ranking.key[:], g["run_of"](e["src"], 1)).then_inc(keys_in, 16)
                    sp.dma_start(x[:], a["x"].rearrange("(t p) c -> p t c", p=P)).then_inc(x_in, 16)
                    src = g["run_of"](e["src"], 1)

                    def loads(attributes):
                        with sp.Fori(0, NC // 2) as h:
                            for b in range(2):
                                wait(sp, rows_used[b], h + 1)
                                sp.dma_start(idx[:, b], src[:, bass.ds((h * 2 + b) * T, T)]).then_inc(idx_in[b], 16)
                            parts = clear_part(g, sp, cleared, "spread1_d", B1, h, NC // 2)
                            parts += clear_part(g, sp, cleared, "spreada_d", H + 1, h, NC // 2)
                            for k, w in attributes:
                                part = bass.ds(h * (2 * T * w), 2 * T * w)
                                sp.dma_start(g["run_of"](g["e"][k], w)[:, part], g["run_of"](a[k], w)[:, part]).then_inc(attr_copied, 16)
                        sp.wait_ge(cleared, 16 * parts * (NC // 2))

                    def keep():
                        attributes = ("attr5", D5), ("attr32", D32), ("attr3", D3)
                        loads(attributes)
                        sp.wait_ge(attr_copied, 16 * len(attributes) * (NC // 2))
                    branch(sp, g, lambda: loads(()), keep)
                    sp.wait_ge(x_in, 16)
                    sp.wait_ge(ranking.ready, 1)
                    sp.dma_start(g["pos_d"], ranking.pos_i[:]).then_inc(pos_out, 16)
                    sp.wait_ge(pos_out, 16)

                @block.gpsimd
                def _(pool):
                    with pool.Fori(0, NC // 2) as h:
                        for b in range(2):
                            wait(pool, idx_in[b], (h + 1) * 16)
                            for t in range(T):
                                pool.indirect_dma_start(rows[:, b, t], None, a["x"],
                                                        bass.IndirectOffsetOnAxis(ap=idx[:, b, t:t + 1], axis=0)) \
                                    .then_inc(got[b], 16)

                @block.tensor
                def _(pe):
                    for n in range(len(KEYS)):
                        ranking.hist_tensor_start(nc, pe, n)
                        with pe.Fori(0, turns) as h:
                            ranking.hist_tensor(nc, pe, n, h)
                        counts.tensor(nc, pe, g, ranking.hist(n), n + 1)
                    ranking.tensor_start(nc, pe)
                    with pe.Fori(0, turns) as h:
                        for r in range(TURN):
                            ranking.tensor_step(nc, pe, h, r)

                @block.vector
                def _(v):
                    v.memset(run[:], 0.0)
                    v.memset(keep[:], 0.0)
                    v.sem_inc(rows_used[0], 1)
                    v.sem_inc(rows_used[1], 1)
                    v.wait_ge(keys_in, 32)
                    v.tensor_tensor(same[:], ranking.key[:], prev[:], ALU.is_equal)
                    v.drain().then_inc(flags, 1)

                    def sum_rows(h, b):
                        wait(v, got[b], (h + 1) * (16 * T))
                        at = bass.ds((h * 2 + b) * T, T)
                        v.tensor_tensor(data[:, :, 1:], rows[:, b].rearrange("p t f -> p f t"),
                                        weight[:, at].unsqueeze(1).to_broadcast([P, C, T]), ALU.mult) \
                         .then_inc(rows_used[b], 1)
                        v.tensor_copy(data[:, :, 0:1], run[:, 1 - b, :, T:T + 1])
                        wait(v, keep_ready[b], h + 1)
                        wait(v, copied[b], h + 1)
                        v.drain()
                        v.tensor_tensor_scan(run[:, b].rearrange("p f t -> p (f t)"),
                                             keep[:, b].rearrange("p f t -> p (f t)"),
                                             data[:].rearrange("p f t -> p (f t)"), 0.0, ALU.mult, ALU.add) \
                         .then_inc(scanned[b], 1)
                        v.drain()

                    for n, k in enumerate(KEYS):
                        v.wait_ge(keys_in, 16 * (n + 2))
                        ranking.hist_vector_start(v, n)
                        if n == 0:
                            v.sem_inc(keys_split, 1)
                            v.wait_ge(loaded, 16)
                        with v.Fori(0, turns // 4) as h:
                            for b in range(2):
                                ranking.hist_vector(v, n, h * 4 + b * 2)
                                ranking.hist_vector(v, n, h * 4 + (b * 2 + 1))
                                sum_rows(h + turns // 4 * n, b)
                        ranking.hist_vector_end(v, n)
                        counts.first_positions(v, g, k, ranking.hist(n), n + 1)

                    ranking.vector_start(v, g["first"]["src"])
                    for n, k in enumerate(KEYS):
                        with v.Fori(turns // 4 * n, turns // 4 * (n + 1)) as h:
                            for b in range(2):
                                for r in range(TURN):
                                    ranking.vector_step(v, h * 2 + b, r)
                                sum_rows(h + turns // 2, b)
                        if n == 1:
                            ranking.vector_end(v)
                        v.wait_ge(ends_in, 16 * (n + 1))
                        counts.partition_nodes(v, g, k, ends_row, scratch_row).then_inc(ends_read, 1)
                    v.tensor_copy(tail[:], run[:, 1, :, T])

                @block.scalar
                def _(act):
                    act.wait_ge(flags, 1)
                    for b in range(2):
                        act.sem_inc(copied[b], 1)
                        act.sem_inc(stored[b], 16)
                        act.sem_inc(scanned[b], 1)

                    def keeps(h, b):
                        wait(act, scanned[b], h + 1)
                        at = bass.ds((h * 2 + b) * T, T)
                        nc.scalar.copy(keep[:, b, :, 1:], same[:, at].unsqueeze(1).to_broadcast([P, C, T])) \
                          .then_inc(keep_ready[b], 1)

                    def store(h, b):
                        wait(act, scanned[b], h + 2)
                        wait(act, stored[b], (h + 1) * 16)
                        nc.scalar.copy(outb[:, b], run[:, b, :, 1:].rearrange("p f t -> p t f")).then_inc(copied[b], 1)
                        wait(act, copied[b], h + 2)
                        act.dma_start(g["run_of"](g["sums0_d"], C)[:, bass.ds((h * 2 + b) * (T * C), T * C)],
                                      outb[:, b].rearrange("p t f -> p (t f)")).then_inc(stored[b], 16)

                    def write_first(n):
                        act.wait_ge(counts.first_ready, n + 1)
                        first_d = g["first_d"][KEYS[n]]
                        act.dma_start(first_d[0:NP].rearrange("(t p) o -> p (t o)", p=P), g["first"][KEYS[n]][:],
                                      allow_slow_non_contiguous=True).then_inc(first_out, 16)
                        act.dma_start(first_d[NP:NP + 1], g["total"][:, 0:1]).then_inc(first_out, 16)

                    def read_ends(n):
                        act.wait_ge(first_out, 32 * len(KEYS))
                        act.dma_start(ends_row[:], g["first_d"][KEYS[n]][1:NP + 1].rearrange("n o -> o n").to_broadcast([P, NP])).then_inc(ends_in, 16)

                    for n in range(len(KEYS)):
                        with act.Fori(turns // 4 * n, turns // 4 * (n + 1)) as h:
                            for b in range(2):
                                keeps(h, b)
                                store(h, b)
                        write_first(n)

                    def turn(h, b, before):
                        ranking.scalar_step(nc, act, h * 2 + b, 0)
                        if before:
                            store(*before)
                        keeps(h + turns // 2, b)
                        for r in range(1, TURN):
                            ranking.scalar_step(nc, act, h * 2 + b, r)

                    ranking.scalar_start(nc, act)
                    turn(0, 0, None)
                    turn(0, 1, (turns // 2, 0))
                    read_ends(0)
                    with act.Fori(1, turns // 2) as h:
                        turn(h, 0, (h + (turns // 2 - 1), 1))
                        turn(h, 1, (h + turns // 2, 0))
                    store(turns - 1, 1)
                    act.wait_ge(ends_read, 1)
                    read_ends(1)
                    for b in range(2):
                        act.wait_ge(stored[b], 16 * (NC // 2 + 1))

        total = collect_sums(nc, sem, g, outer, "l0", g["sums0_d"], tail)
        with ExitStack() as stack:
            s = Space(nc, stack)
            work, stat = s.sb("l0_work", [P, NT, C]), s.sb("l0_stat", [P, 3, NT])
            sems = sem("l0_centred"), sem("l0_rooted")
            with nc.Block() as block:
                @block.vector
                def _(v):
                    v.tensor_tensor(total[:], total[:], x[:], ALU.add)
                    v.drain()
                    normalise(nc, v, None, total[:], x[:], work[:], stat, sems, 1)

                @block.scalar
                def _(act):
                    normalise(nc, None, act, None, None, None, stat, sems, 1)


def collect_sums(nc, sem, g, outer, name, sums_d, tail):
    s0 = Space(nc, outer)
    total = s0.sb(f"{name}_total", [P, NT, C])
    with ExitStack() as stack:
        s = Space(nc, stack)
        masks = s.sb(f"{name}_masks", [P, NP])
        more = s.ps(f"{name}_more", [P, 2, 8, C])
        tiles = s.sb(f"{name}_tiles", [P, NT])
        got, read, mult, masked = (sem(f"{name}_c{n}") for n in ("got", "read", "mult", "masked"))
        groups = [range(i, min(i + 8, NT)) for i in range(0, NT, 8)]
        with nc.Block() as block:
            @block.gpsimd
            def _(pool):
                for i in range(NT):
                    pool.indirect_dma_start(total[:, i], None, sums_d,
                                            bass.IndirectOffsetOnAxis(ap=g["end_idx"]["dst"][:, i:i + 1], axis=0)).then_inc(got, 16)

            @block.tensor
            def _(pe):
                pe.wait_ge(masked, 1)
                for n, group in enumerate(groups):
                    if n >= 2:
                        pe.wait_ge(read, n - 1)
                    for j, i in enumerate(group):
                        last = nc.tensor.matmul(more[:, n % 2, j], masks[:, i * P:(i + 1) * P], tail[:], start=True, stop=True)
                    last.then_inc(mult, 1)

            @block.vector
            def _(v):
                node_mask(v, g, g["cross_key"]["dst"], tiles[:], masks).then_inc(masked, 1)
                v.wait_ge(got, 16 * NT)
                v.tensor_tensor(total[:], total[:], g["filled"]["dst"][:].unsqueeze(2).to_broadcast([P, NT, C]), ALU.mult)
                v.drain()
                for n, group in enumerate(groups):
                    v.wait_ge(mult, n + 1)
                    at = slice(group[0], group[-1] + 1)
                    v.tensor_tensor(total[:, at], total[:, at], more[:, n % 2, 0:len(group)], ALU.add).then_inc(read, 1)
    return total


def layer1(nc, a, sem, g):
    x = g["x"]
    with ExitStack() as outer:
        s0 = Space(nc, outer)
        tail = s0.sb("l1_tail", [P, H * F1 + H])
        head = s0.sb("l1_head", [P, B1])
        head_a = s0.sb("l1_heada", [P, H + 1])
        edge_w = s0.sb("l1_edge_w", [P, H, D5])
        with ExitStack() as stack:
            s = Space(nc, stack)
            att = s.sb("l1_att", [C, 2 * H])
            att_wide = s.sb("l1_att_wide", [C, 2 * H, P])
            proj = s.sb("l1_proj", [C, H, F1 + 1])
            node_w = s.sb("l1_node_w", [P, 2, H, F1 + 1])
            const = s.sb("l1_const", [P, H])
            rows = s.sb("l1_node_rows", [P, NT, B1])
            rows_a = s.sb("l1_node_rows_a", [P, NT, H + 1])
            prod = s.sb("l1_node_prod", [P, NT, C])
            score = s.sb("l1_node_score", [P, 2, H, NT])
            dots = s.ps("l1_dots", [P, 2, H, P])
            loaded, wide, dotted, tabled, saved, fetched = (sem(f"l1_{n}") for n in ("loaded", "wide", "dotted", "tabled", "saved", "fetched"))
            with nc.Block() as block:
                @block.sync
                def _(sp):
                    sp.dma_start(att[:], a["att1"]).then_inc(loaded, 16)
                    sp.dma_start(proj[:], a["proj1"]).then_inc(loaded, 16)
                    sp.wait_ge(tabled, 2)
                    sp.dma_start(g["table1_d"].rearrange("(t p) w -> p t w", p=P), rows[:]).then_inc(saved, 16)
                    sp.dma_start(g["tablea_d"].rearrange("(t p) w -> p t w", p=P), rows_a[:]).then_inc(saved, 16)

                @block.tensor
                def _(pe):
                    pe.wait_ge(loaded, 32)
                    pe.wait_ge(wide, 1)
                    for side in range(2):
                        for h in range(H):
                            last = nc.tensor.matmul(dots[:, side, h, 0:F1 + 1], att_wide[:, side * H + h], proj[:, h],
                                                    start=True, stop=True)
                    last.then_inc(dotted, 1)

                @block.vector
                def _(v):
                    v.wait_ge(loaded, 32)
                    v.tensor_copy(att_wide[:], att[:].unsqueeze(2).to_broadcast([C, 2 * H, P])).then_inc(wide, 1)
                    v.memset(rows[:], 1.0)
                    v.memset(rows_a[:], 1.0)
                    v.wait_ge(dotted, 1)
                    v.tensor_copy(node_w[:], dots[:, :, :, 0:F1 + 1])
                    v.drain()
                    v.tensor_copy(edge_w[:], node_w[:, 1, :, C + 1:C + 1 + D5])
                    v.tensor_tensor(const[:], node_w[:, 1, :, C], node_w[:, 1, :, F1], ALU.add)
                    v.tensor_copy(rows[:, :, 0:C], x[:])
                    v.drain()
                    for side in range(2):
                        for h in range(H):
                            v.tensor_tensor(prod[:], x[:], node_w[:, side, h, 0:C].unsqueeze(1).to_broadcast([P, NT, C]), ALU.mult)
                            v.drain()
                            v.tensor_reduce(score[:, side, h], prod[:], AX, ALU.add)
                            v.drain()
                        for h in range(H):
                            if side == 0:
                                v.tensor_scalar(rows_a[:, :, h], score[:, 0, h], node_w[:, 0, h, C:C + 1], None, ALU.add)
                            else:
                                v.tensor_scalar(rows[:, :, C + h], score[:, 1, h], const[:, h:h + 1], None, ALU.add)
                        v.drain().then_inc(tabled, 1)

                @block.gpsimd
                def _(pool):
                    for n, (table, target, k) in enumerate(((rows_a, "spreada_d", "src"), (rows, "spread1_d", "dst"))):
                        pool.wait_ge(tabled, n + 1)
                        for i in range(NT):
                            pool.indirect_dma_start(g[target], bass.IndirectOffsetOnAxis(ap=g["start_idx"][k][:, i:i + 1], axis=0),
                                                    table[:, i], None, bounds_check=EP - 1, oob_is_err=False).then_inc(fetched, 16)
                    pool.wait_ge(saved, 32)
                    pool.indirect_dma_start(head[:], None, g["table1_d"],
                                            bass.IndirectOffsetOnAxis(ap=g["head_key"]["dst"][:], axis=0)).then_inc(fetched, 16)
                    pool.indirect_dma_start(head_a[:], None, g["tablea_d"],
                                            bass.IndirectOffsetOnAxis(ap=g["head_key"]["src"][:], axis=0)).then_inc(fetched, 16)
                    pool.wait_ge(fetched, 16 * (2 * NT + 2))

        T, NC = T1, L // T1
        with ExitStack() as stack:
            s = Space(nc, stack)
            W = C + H
            spread = s.sb("l1_spread", [P, 2, T, B1])
            attr = s.sb("l1_attr", [P, 2, T, D5])
            idx = s.sb("l1_idx", [P, 2, T], I32)
            data = s.sb("l1_data", [P, W, T + 1])
            keep = s.sb("l1_keep", [P, 2, W, T + 1])
            run = s.sb("l1_run", [P, 2, W, T + 1])
            rows = s.sb("l1_rows", [P, 2, T, R1])
            prod = s.sb("l1_prod", [P, T, H, D5])
            dot = s.sb("l1_dot", [P, T, H])
            two = lambda n: [sem(f"l1d_{n}{b}") for b in range(2)]
            loaded, used, keep_ready, scanned, filled, sent, scored, free = (two(n) for n in (
                "loaded", "used", "keep_ready", "scanned", "filled", "sent", "scored", "free"))
            set_up, cleared = sem("l1d_set_up"), sem("l1d_cleared")
            with nc.Block() as block:
                @block.sync
                def _(sp):
                    spread_v, attr_v = g["run_of"](g["spread1_d"], B1), g["run_of"](g["e"]["attr5"], D5)
                    with sp.Fori(0, NC // 2) as h:
                        for b in range(2):
                            c = h * 2 + b
                            wait(sp, used[b], h + 1)
                            wait(sp, keep_ready[b], h + 1)
                            wait(sp, free[b], h + 1)
                            sp.dma_start(spread[:, b].rearrange("p t w -> p (t w)"), spread_v[:, bass.ds(c * (T * B1), T * B1)]).then_inc(loaded[b], 16)
                            sp.dma_start(attr[:, b].rearrange("p t w -> p (t w)"), attr_v[:, bass.ds(c * (T * D5), T * D5)]).then_inc(loaded[b], 16)
                            sp.dma_start(idx[:, b], g["pos_d"][:, bass.ds(c * T, T)]).then_inc(loaded[b], 16)
                        parts = clear_part(g, sp, cleared, "spread2_d", B2, h, NC // 2)
                    sp.wait_ge(cleared, 16 * parts * (NC // 2))

                @block.scalar
                def _(act):
                    act.wait_ge(set_up, 1)
                    with act.Fori(0, NC // 2) as h:
                        for b in range(2):
                            wait(act, loaded[b], (h + 1) * 48)
                            wait(act, scanned[b], h + 1)
                            nc.scalar.activation(keep[:, b, :, 1:], spread[:, b, :, B1 - 1].unsqueeze(1).to_broadcast([P, W, T]),
                                                 ACT.Copy, bias=1.0, scale=-1.0).then_inc(keep_ready[b], 1)
                            wait(act, scanned[b], h + 2)
                            wait(act, free[b], h + 1)
                            nc.scalar.copy(rows[:, b, :, 0:C], run[:, b, 0:C, 1:].rearrange("p f t -> p t f"))
                            nc.scalar.copy(rows[:, b, :, C:C + D5], attr[:, b]).then_inc(filled[b], 1)

                @block.vector
                def _(v):
                    v.memset(keep[:], 0.0)
                    v.memset(rows[:], 1.0)
                    v.memset(run[:], 0.0)
                    v.drain()
                    v.tensor_copy(run[:, 1, :, T], head[:, 0:W])
                    for b in range(2):
                        v.sem_inc(used[b], 1)
                        v.sem_inc(keep_ready[b], 1)
                        v.sem_inc(scanned[b], 1)
                        v.sem_inc(free[b], 1)
                        v.sem_inc(filled[b], 1)
                    v.drain().then_inc(set_up, 1)
                    with v.Fori(0, NC // 2) as h:
                        for b in range(2):
                            wait(v, loaded[b], (h + 1) * 48)
                            v.tensor_copy(data[:, :, 1:], spread[:, b, :, 0:W].rearrange("p t f -> p f t"))
                            v.tensor_copy(data[:, :, 0:1], run[:, 1 - b, :, T:T + 1])
                            v.tensor_tensor(prod[:], attr[:, b].unsqueeze(2).to_broadcast([P, T, H, D5]),
                                            edge_w[:].unsqueeze(1).to_broadcast([P, T, H, D5]), ALU.mult)
                            v.drain().then_inc(used[b], 1)
                            v.tensor_reduce(dot[:], prod[:], AX, ALU.add)
                            wait(v, keep_ready[b], h + 2)
                            wait(v, filled[b], h + 1)
                            v.tensor_tensor_scan(run[:, b].rearrange("p f t -> p (f t)"), keep[:, b].rearrange("p f t -> p (f t)"),
                                                 data[:].rearrange("p f t -> p (f t)"), 0.0, ALU.mult, ALU.add).then_inc(scanned[b], 1)
                            wait(v, free[b], h + 1)
                            v.drain()
                            v.tensor_tensor(rows[:, b, :, F1:R1], run[:, b, C:W, 1:].rearrange("p f t -> p t f"), dot[:], ALU.add) \
                             .then_inc(scored[b], 1)

                @block.gpsimd
                def _(pool):
                    def scatter(h, b, first=False):
                        wait(pool, filled[b], h + 2)
                        wait(pool, scored[b], h + 1)
                        for t in range(T):
                            pool.indirect_dma_start(g["rows1_d"], bass.IndirectOffsetOnAxis(ap=idx[:, b, t:t + 1], axis=0),
                                                    rows[:, b, t], None).then_inc(sent[b], 16)
                            if t == T // 2 and not first:
                                wait(pool, sent[1 - b], (h + b) * (16 * T))
                                pool.sem_inc(free[1 - b], 1)
                    scatter(0, 0, True)
                    scatter(0, 1)
                    with pool.Fori(1, NC // 2) as h:
                        for b in range(2):
                            scatter(h, b)
                    for b in range(2):
                        pool.wait_ge(sent[b], 16 * T * (NC // 2))

        with ExitStack() as stack:
            s = Space(nc, stack)
            W = H * F1
            rows = s.sb("l1s_rows", [P, UNROLL, T, R1])
            side = s.sb("l1s_side", [P, UNROLL, T, H + 1])
            hold = s.sb("l1s_hold", [P, 2, H, T + 1])
            hold_data = s.sb("l1s_hold_data", [P, H, T + 1])
            hold_keep = s.sb("l1s_hold_keep", [P, H, T + 1])
            score = s.sb("l1s_score", [P, H, T + 1])
            leak = s.sb("l1s_leak", [P, H, T])
            soft = Softmax(s, "l1s", T, F1)
            outb = s.sb("l1s_out", [P, 2, T, W + H])
            two = lambda n: [sem(f"l1s_{n}{b}") for b in range(2)]
            loaded, used = ([sem(f"l1s_{n}{r}") for r in range(UNROLL)] for n in ("loaded", "used"))
            soft.semaphores(two)
            set_up = sem("l1s_set_up")
            with nc.Block() as block:
                @block.sync
                def _(sp):
                    rows_v, side_v = g["run_of"](g["rows1_d"], R1), g["run_of"](g["spreada_d"], H + 1)
                    for c in chunks(sp, NC):
                        wait(sp, used[c.r], c.g + 1)
                        sp.dma_start(rows[:, c.r].rearrange("p t w -> p (t w)"), rows_v[:, bass.ds(c.at * (T * R1), T * R1)]).then_inc(loaded[c.r], 16)
                        sp.dma_start(side[:, c.r].rearrange("p t w -> p (t w)"), side_v[:, bass.ds(c.at * (T * (H + 1)), T * (H + 1))]).then_inc(loaded[c.r], 16)

                @block.scalar
                def _(act):
                    act.wait_ge(set_up, 1)
                    soft.scalar_program(nc, act, NC, outb, g["run_of"](g["sums1_d"], W + H))

                @block.vector
                def _(v):
                    v.memset(hold[:], 0.0)
                    v.memset(hold_keep[:], 0.0)
                    v.drain()
                    v.tensor_copy(hold[:, 1, :, T], head_a[:, 0:H])
                    soft.start(v)
                    for r in range(UNROLL):
                        v.sem_inc(used[r], 1)
                    v.drain().then_inc(set_up, 1)

                    def scores(c):
                        b, r = c.b, c.r
                        wait(v, loaded[r], (c.g + 1) * 32)
                        start = side[:, r, :, H].unsqueeze(1).to_broadcast([P, H, T])
                        v.tensor_scalar(hold_keep[:, :, 1:], start, -1.0, 1.0, ALU.mult, ALU.add)
                        v.tensor_copy(hold_data[:, :, 1:], side[:, r, :, 0:H].rearrange("p t h -> p h t"))
                        v.tensor_copy(hold_data[:, :, 0:1], hold[:, 1 - b, :, T:T + 1])
                        v.drain()
                        v.tensor_tensor_scan(hold[:, b].rearrange("p h t -> p (h t)"), hold_keep[:].rearrange("p h t -> p (h t)"),
                                             hold_data[:].rearrange("p h t -> p (h t)"), 0.0, ALU.mult, ALU.add)
                        v.drain()
                        v.tensor_tensor(leak[:], hold[:, b, :, 1:], rows[:, r, :, F1:R1].rearrange("p t h -> p h t"), ALU.add)
                        v.drain()
                        v.scalar_tensor_tensor(out=score[:, :, 1:], in0=leak[:], scalar=0.2, in1=leak[:], op0=ALU.mult, op1=ALU.max)
                        soft.running_max(v, c, score, start)

                    def sums(c):
                        soft.sums(v, c, rows[:, c.r, :, 0:F1].rearrange("p t f -> p f t")).then_inc(used[c.r], 1)
                        soft.scan(v, c)

                    soft.vector_program(v, NC, scores, sums)
                    soft.keep_tail(v, tail)

        summed = collect_softmax(nc, sem, g, outer, "l1", "src", g["sums1_d"], tail, F1)
        with ExitStack() as stack:
            s = Space(nc, stack)
            out_w = s.sb("l1_out_w", [F1, H, C])
            bias = s.sb("l1_bias", [P, C])
            recip = s.sb("l1_recip", [P, NT, H])
            turned_s = s.sb("l1_turned", [F1, 2, H, P])
            work, stat = s.sb("l1_work", [P, NT, C]), s.sb("l1_stat", [P, 3, NT])
            acc = s.sb("l1_acc", [P, NT, C])
            turned = s.ps("l1_turned_ps", [P, 2, 512])
            made = s.ps("l1_made", [P, 2, 512])
            loaded, added, scaled, turned_ready, copied, made_ready, read = (sem(f"l1n_{n}") for n in (
                "loaded", "added", "scaled", "turned", "copied", "made", "read"))
            sems = sem("l1_centred"), sem("l1_rooted")
            with nc.Block() as block:
                @block.gpsimd
                def _(pool):
                    pool.dma_start(out_w[:], a["out1"]).then_inc(loaded, 16)
                    pool.dma_start(bias[:], a["bias1"].to_broadcast([P, C])).then_inc(added, 16)
                    pool.wait_ge(loaded, 16)
                    pool.dma_start(out_w[F1 - 1:F1], a["out1_bias"], accum_op=ALU.add).then_inc(added, 16)
                    pool.wait_ge(added, 32)

                @block.vector
                def _(v):
                    den = summed[:, :, 0:H * F1].rearrange("p t (h f) -> p t h f", h=H)[:, :, :, F1 - 1]
                    v.tensor_scalar(recip[:], den, 1e-16, float(H), ALU.add, ALU.mult)
                    v.drain()
                    v.reciprocal(recip[:], recip[:])
                    v.drain()
                    for h in range(H):
                        part = summed[:, :, h * F1:(h + 1) * F1]
                        v.tensor_tensor(part, part, recip[:, :, h].unsqueeze(2).to_broadcast([P, NT, F1]), ALU.mult)
                    v.drain().then_inc(scaled, 1)
                    v.wait_ge(added, 32)
                    v.tensor_tensor(acc[:], x[:], bias[:].unsqueeze(1).to_broadcast([P, NT, C]), ALU.add)
                    for i in range(NT):
                        v.wait_ge(made_ready, i + 1)
                        v.drain()
                        v.tensor_tensor(acc[:, i], acc[:, i], made[:, i % 2, 0:C], ALU.add).then_inc(read, 1)
                    v.drain()
                    normalise(nc, v, None, acc[:], x[:], work[:], stat, sems, 1)

                @block.scalar
                def _(act):
                    for i in range(NT):
                        act.wait_ge(turned_ready, i + 1)
                        if i >= 2:
                            act.wait_ge(made_ready, i - 1)
                        nc.scalar.copy(turned_s[:, i % 2].rearrange("f h e -> f (h e)"), turned[0:F1, i % 2, 0:H * P]).then_inc(copied, 1)
                    normalise(nc, None, act, None, None, None, stat, sems, 1)

                @block.tensor
                def _(pe):
                    pe.wait_ge(scaled, 1)
                    pe.wait_ge(added, 32)

                    def turn(i):
                        if i >= 2:
                            pe.wait_ge(copied, i - 1)
                        for h in range(H):
                            last = nc.tensor.transpose(turned[0:F1, i % 2, h * P:(h + 1) * P], summed[:, i, h * F1:(h + 1) * F1],
                                                       g["identity"][:])
                        last.then_inc(turned_ready, 1)
                    turn(0)
                    for i in range(NT):
                        if i + 1 < NT:
                            turn(i + 1)
                        pe.wait_ge(copied, i + 1)
                        if i >= 2:
                            pe.wait_ge(read, i - 1)
                        for h in range(H):
                            last = nc.tensor.matmul(made[:, i % 2, 0:C], turned_s[:, i % 2, h], out_w[:, h],
                                                    start=(h == 0), stop=(h == H - 1))
                        last.then_inc(made_ready, 1)


class Softmax:

    def __init__(self, s, name, T, F):
        self.T, self.F = T, F
        self.fresh = s.sb(f"{name}_fresh", [P, H, T + 1])
        self.top = s.sb(f"{name}_top", [P, 2, H, T + 1])
        self.arg = s.sb(f"{name}_arg", [P, 2, 2, H, T])
        self.exp = s.sb(f"{name}_exp", [P, 2, 2, H, T])
        self.scale = s.sb(f"{name}_scale", [P, 2, H, F, T + 1])
        self.data = s.sb(f"{name}_data", [P, H, F, T + 1])
        self.run = s.sb(f"{name}_run", [P, 2, H, F, T + 1])

    def semaphores(self, two):
        self.args_ready, self.exp_ready, self.scale_ready, self.scanned, self.copied, self.stored = (
            two(n) for n in ("args", "exp", "scale", "scanned", "copied", "stored"))

    def start(self, v):
        v.memset(self.fresh[:], -FAR)
        v.memset(self.top[:], -FAR)
        v.memset(self.scale[:], 0.0)
        v.memset(self.run[:], 0.0)
        for b in range(2):
            v.sem_inc(self.scanned[b], 1)
            v.sem_inc(self.copied[b], 1)
            v.sem_inc(self.exp_ready[b], 1)
            v.sem_inc(self.stored[b], 16)

    def running_max(self, v, c, score, start):
        T, h, b = self.T, c.h, c.b
        v.tensor_scalar(self.fresh[:, :, 1:], start, -FAR, None, ALU.mult)
        v.tensor_copy(score[:, :, 0:1], self.top[:, 1 - b, :, T:T + 1])
        wait(v, self.copied[b], h + 1)
        wait(v, self.exp_ready[b], h + 1)
        v.drain()
        v.tensor_tensor_scan(self.top[:, b].rearrange("p h t -> p (h t)"), self.fresh[:].rearrange("p h t -> p (h t)"),
                             score[:].rearrange("p h t -> p (h t)"), -FAR, ALU.add, ALU.max)
        v.drain()
        v.tensor_tensor(self.arg[:, b, 0], self.top[:, b, :, 0:T], self.fresh[:, :, 1:], ALU.add)
        v.tensor_tensor(self.arg[:, b, 1], score[:, :, 1:], self.top[:, b, :, 1:], ALU.subtract)
        v.drain()
        v.tensor_tensor(self.arg[:, b, 0], self.arg[:, b, 0], self.top[:, b, :, 1:], ALU.subtract).then_inc(self.args_ready[b], 1)

    def sums(self, v, c, rows):
        T, h, b = self.T, c.h, c.b
        wait(v, self.exp_ready[b], h + 2)
        for head in range(H):
            v.tensor_tensor(self.data[:, head, :, 1:], rows,
                            self.exp[:, b, 1, head].unsqueeze(1).to_broadcast([P, self.F, T]), ALU.mult)
        return v.drain()

    def scan(self, v, c):
        T, h, b = self.T, c.h, c.b
        v.tensor_copy(self.data[:, :, :, 0:1], self.run[:, 1 - b, :, :, T:T + 1])
        wait(v, self.scale_ready[b], h + 1)
        wait(v, self.copied[b], h + 1)
        v.drain()
        v.tensor_tensor_scan(self.run[:, b].rearrange("p h f t -> p (h f t)"), self.scale[:, b].rearrange("p h f t -> p (h f t)"),
                             self.data[:].rearrange("p h f t -> p (h f t)"), 0.0, ALU.mult, ALU.add).then_inc(self.scanned[b], 1)
        v.drain()

    def vector_program(self, v, count, scores, sums):
        chunks_ahead(v, count, scores, sums)

    def keep_tail(self, v, tail):
        T, W = self.T, H * self.F
        v.tensor_copy(tail[:, 0:W], self.run[:, 1].rearrange("p h f t -> p (h f) t")[:, :, T])
        v.tensor_copy(tail[:, W:W + H], self.top[:, 1, :, T])

    def scalar_program(self, nc, act, count, outb, sums_v, before=lambda c: None):
        T, W = self.T, H * self.F

        def exponentials(c):
            h, b = c.h, c.b
            wait(act, self.args_ready[b], h + 1)
            nc.scalar.activation(self.exp[:, b], self.arg[:, b], ACT.Exp).then_inc(self.exp_ready[b], 1)
            after = c.next(count)
            if after:
                before(after)
            wait(act, self.exp_ready[b], h + 2)
            wait(act, self.scanned[b], h + 1)
            for head in range(H):
                last = nc.scalar.copy(self.scale[:, b, head, :, 1:], self.exp[:, b, 0, head].unsqueeze(1).to_broadcast([P, self.F, T]))
            last.then_inc(self.scale_ready[b], 1)

        def store(c):
            h, b = c.h, c.b
            wait(act, self.scanned[b], h + 2)
            wait(act, self.stored[b], (h + 1) * 16)
            nc.scalar.copy(outb[:, b, :, 0:W], self.run[:, b].rearrange("p h f t -> p (h f) t")[:, :, 1:].rearrange("p w t -> p t w"))
            nc.scalar.copy(outb[:, b, :, W:W + H], self.top[:, b, :, 1:].rearrange("p h t -> p t h")).then_inc(self.copied[b], 1)
            wait(act, self.copied[b], h + 2)
            wide = T * outb.shape[-1]
            act.dma_start(sums_v[:, bass.ds(c.at * wide, wide)], outb[:, b].rearrange("p t w -> p (t w)")).then_inc(self.stored[b], 16)

        before(Chunk(0, 0))
        chunks_ahead(act, count, exponentials, store)
        for b in range(2):
            act.wait_ge(self.stored[b], 16 * (count // 2 + 1))


def collect_softmax(nc, sem, g, outer, name, k, sums_d, tail, F):
    W = H * F
    total = Space(nc, outer).sb(f"{name}_total", [P, NT, W + H])
    with ExitStack() as stack:
        s = Space(nc, stack)
        masks = s.sb(f"{name}_masks", [P, NP])
        last_only = s.sb(f"{name}_last_only", [P, NP])
        tiles = s.sb(f"{name}_tiles", [P, 2, NT])
        ones = s.sb(f"{name}_ones", [P, P])
        diag = s.sb(f"{name}_diag", [P, H + 1, P])
        other = s.sb(f"{name}_other", [P, P])
        pair = s.sb(f"{name}_pair", [P, H, P])
        top = s.sb(f"{name}_gtop", [P, H + 1])
        factor = s.sb(f"{name}_factor", [P, H])
        scaled = s.sb(f"{name}_scaled", [P, W])
        crossing = s.sb(f"{name}_crossing", [P, NT, H + 1])
        best = s.sb(f"{name}_best", [P, NT, H])
        args = s.sb(f"{name}_args", [P, 2, NT, H])
        exps = s.sb(f"{name}_exps", [P, 2, NT, H])
        wide = s.ps(f"{name}_wide", [P, 512])
        found = s.ps(f"{name}_found", [P, 512])
        more = s.ps(f"{name}_more", [P, 2, 512])
        got, read, mult, diag_ready, spread, arg_ready, exp_ready, top_ready, found_ready, tail_ready = (
            sem(f"{name}_s{n}") for n in ("got", "read", "mult", "diag", "spread", "arg", "exp", "top", "found", "tail"))
        with nc.Block() as block:
            @block.gpsimd
            def _(pool):
                for i in range(NT):
                    pool.indirect_dma_start(total[:, i], None, sums_d,
                                            bass.IndirectOffsetOnAxis(ap=g["end_idx"][k][:, i:i + 1], axis=0)).then_inc(got, 16)

            @block.tensor
            def _(pe):
                pe.wait_ge(diag_ready, 1)
                nc.tensor.matmul(wide[:, 0:(H + 1) * P], ones[:], diag[:].rearrange("p a q -> p (a q)"), start=True, stop=True).then_inc(spread, 1)
                pe.wait_ge(top_ready, 1)
                for i in range(NT):
                    last = nc.tensor.matmul(found[:, i * (H + 1):(i + 1) * (H + 1)], last_only[:, i * P:(i + 1) * P], top[:],
                                            start=True, stop=True)
                last.then_inc(found_ready, 1)
                pe.wait_ge(tail_ready, 1)
                for i in range(NT):
                    if i >= 2:
                        pe.wait_ge(read, i - 1)
                    nc.tensor.matmul(more[:, i % 2, 0:W], masks[:, i * P:(i + 1) * P], scaled[:], start=True, stop=True).then_inc(mult, 1)

            @block.scalar
            def _(act):
                act.wait_ge(arg_ready, 1)
                nc.scalar.activation(factor[:], factor[:], ACT.Exp).then_inc(exp_ready, 1)
                act.wait_ge(arg_ready, 2)
                nc.scalar.activation(exps[:], args[:], ACT.Exp).then_inc(exp_ready, 1)

            @block.vector
            def _(v):
                v.memset(ones[:], 1.0)
                v.memset(top[:], 1.0)
                ident = g["identity"]
                for j in range(H):
                    v.tensor_scalar(diag[:, j], ident[:], tail[:, W + j:W + j + 1], None, ALU.mult)
                v.tensor_scalar(diag[:, H], ident[:], g["tail_key"][k][:, 0:1], None, ALU.mult)
                v.drain().then_inc(diag_ready, 1)
                node_mask(v, g, g["last_key"][k], tiles[:, 0], last_only)
                node_mask(v, g, g["cross_key"][k], tiles[:, 1], masks)
                v.wait_ge(spread, 1)
                v.tensor_scalar(other[:], wide[:, H * P:(H + 1) * P], g["tail_key"][k][:, 0:1], None, ALU.is_equal)
                v.drain()
                v.tensor_scalar(other[:], other[:], FAR, -FAR, ALU.mult, ALU.add)
                v.drain()
                v.tensor_tensor(pair[:], wide[:, 0:H * P].rearrange("p (h q) -> p h q", h=H),
                                other[:].unsqueeze(1).to_broadcast([P, H, P]), ALU.add)
                v.drain()
                v.tensor_reduce(top[:, 0:H], pair[:], AX, ALU.max)
                v.drain().then_inc(top_ready, 1)
                v.tensor_tensor(factor[:], tail[:, W:W + H], top[:, 0:H], ALU.subtract)
                v.drain().then_inc(arg_ready, 1)
                v.wait_ge(exp_ready, 1)
                for h in range(H):
                    v.tensor_scalar(scaled[:, h * F:(h + 1) * F], tail[:, h * F:(h + 1) * F], factor[:, h:h + 1], None, ALU.mult)
                v.drain().then_inc(tail_ready, 1)
                v.wait_ge(found_ready, 1)
                v.tensor_copy(crossing[:].rearrange("p t a -> p (t a)"), found[:, 0:NT * (H + 1)])
                v.drain()
                v.tensor_scalar(crossing[:, :, H], crossing[:, :, H], FAR, -FAR, ALU.mult, ALU.add)
                v.drain()
                v.tensor_tensor(crossing[:, :, 0:H], crossing[:, :, 0:H], crossing[:, :, H].unsqueeze(2).to_broadcast([P, NT, H]), ALU.add)
                v.wait_ge(got, 16 * NT)
                v.drain()
                v.tensor_tensor(best[:], crossing[:, :, 0:H], total[:, :, W:W + H], ALU.max)
                v.drain()
                v.tensor_tensor(args[:, 0], total[:, :, W:W + H], best[:], ALU.subtract)
                v.tensor_tensor(args[:, 1], crossing[:, :, 0:H], best[:], ALU.subtract)
                v.drain().then_inc(arg_ready, 1)
                v.wait_ge(exp_ready, 2)
                v.tensor_tensor(exps[:, 0], exps[:, 0], g["filled"][k][:].unsqueeze(2).to_broadcast([P, NT, H]), ALU.mult)
                v.drain()
                for h in range(H):
                    part = total[:, :, h * F:(h + 1) * F]
                    v.tensor_tensor(part, part, exps[:, 0, :, h].unsqueeze(2).to_broadcast([P, NT, F]), ALU.mult)
                v.drain()
                for i in range(NT):
                    v.wait_ge(mult, i + 1)
                    for h in range(H):
                        last = v.scalar_tensor_tensor(out=total[:, i, h * F:(h + 1) * F], in0=more[:, i % 2, h * F:(h + 1) * F],
                                                      scalar=exps[:, 1, i, h:h + 1], in1=total[:, i, h * F:(h + 1) * F],
                                                      op0=ALU.mult, op1=ALU.add)
                    last.then_inc(read, 1)
    return total


class Pipeline:

    def __init__(self, sem, name, stages):
        self.stages = stages
        self.made = [sem(f"{name}_made{k}") for k in range(stages)]
        self.brought = [sem(f"{name}_brought{k}") for k in range(stages)]

    def tensor(self, pe, work):
        for step in range(NT + self.stages - 1):
            for k in reversed(range(self.stages)):
                i = step - k
                if not 0 <= i < NT:
                    continue
                if k:
                    pe.wait_ge(self.brought[k - 1], i + 1)
                if i >= 2:
                    pe.wait_ge(self.brought[k], i - 1)
                work[k](i).then_inc(self.made[k], 1)

    def scalar(self, act, work):
        last = self.stages - 1
        for step in range(NT + last - 1):
            for k in reversed(range(last)):
                i = step - k
                if not 0 <= i < NT:
                    continue
                act.wait_ge(self.made[k], i + 1)
                if i >= 2:
                    act.wait_ge(self.made[k + 1], i - 1)
                work[k](i).then_inc(self.brought[k], 1)

    def vector(self, v, work):
        for i in range(NT):
            v.wait_ge(self.made[-1], i + 1)
            work(i).then_inc(self.brought[-1], 1)


def layer2(nc, a, sem, g):
    x = g["x"]
    ident = g["identity"]
    with ExitStack() as outer:
        s0 = Space(nc, outer)
        tail = s0.sb("l2_tail", [P, H * F2 + H])
        head = s0.sb("l2_head", [P, B2])
        with ExitStack() as stack:
            s = Space(nc, stack)
            hidden = s.sb("l2_hidden", [P, NT, C])
            work, stat = s.sb("l2_work", [P, NT, C]), s.sb("l2_stat", [P, 3, NT])
            gain, shift = s.sb("l2_gain", [P, C]), s.sb("l2_shift", [P, C])
            wq, bq, keys = s.sb("l2_wq", [C, H * C]), s.sb("l2_bq", [H * C, 1]), s.sb("l2_keys", [H * C, H * F2])
            bq8 = s.sb("l2_bq8", [H * C, 1])
            rows = s.sb("l2_node_rows", [P, NT, B2])
            hid_t, query_t = s.sb("l2_hid_t", [C, 2, P]), s.sb("l2_query_t", [H * C, 2, P])
            ps_a, ps_b, ps_c = s.ps("l2_psa", [P, 2, 512]), s.ps("l2_psb", [P, 2, 512]), s.ps("l2_psc", [P, 2, 512])
            loaded, ready, saved, spread, fetched, scaled, tabled = (sem(f"l2a_{n}") for n in (
                "loaded", "ready", "saved", "spread", "fetched", "scaled", "tabled"))
            sems = sem("l2a_centred"), sem("l2a_rooted")
            pipe = Pipeline(sem, "l2a", 3)
            inv = float(C) ** -0.5
            with nc.Block() as block:
                @block.sync
                def _(sp):
                    sp.dma_start(gain[:], a["ln1_g"].to_broadcast([P, C])).then_inc(loaded, 16)
                    sp.dma_start(shift[:], a["ln1_b"].to_broadcast([P, C])).then_inc(loaded, 16)
                    sp.dma_start(wq[:], a["wq"]).then_inc(loaded, 16)
                    sp.dma_start(bq[:], a["bq"]).then_inc(loaded, 16)
                    sp.dma_start(keys[:], a["keys2"]).then_inc(loaded, 16)
                    sp.wait_ge(ready, 1)
                    sp.dma_start(g["h2_d"].rearrange("(t p) w -> p t w", p=P), hidden[:]).then_inc(saved, 16)
                    sp.wait_ge(tabled, 1)
                    sp.dma_start(g["table2_d"].rearrange("(t p) w -> p t w", p=P), rows[:]).then_inc(saved, 16)
                    sp.wait_ge(saved, 32)

                @block.vector
                def _(v):
                    v.wait_ge(loaded, 80)
                    v.memset(rows[:, :, H * F2:B2], 1.0)
                    v.tensor_scalar(bq8[:], bq[:], inv, None, ALU.mult)
                    v.tensor_copy(work[:], x[:])
                    v.drain().then_inc(scaled, 1)
                    normalise(nc, v, None, work[:], hidden[:], hidden[:], stat, sems, 1, gain, shift)
                    v.drain().then_inc(ready, 1)
                    pipe.vector(v, lambda i: v.tensor_copy(rows[:, i, 0:H * F2], ps_c[:, i % 2, 0:H * F2]))
                    v.drain().then_inc(tabled, 1)

                @block.scalar
                def _(act):
                    normalise(nc, None, act, None, None, None, stat, sems, 1)
                    act.wait_ge(scaled, 1)
                    pipe.scalar(act, [
                        lambda i: nc.scalar.copy(hid_t[:, i % 2], ps_a[0:C, i % 2, 0:P]),
                        lambda i: nc.scalar.activation(query_t[:, i % 2], ps_b[:, i % 2, 0:P], ACT.Identity, bias=bq8[:, 0:1], scale=inv)])

                @block.tensor
                def _(pe):
                    pe.wait_ge(ready, 1)
                    pipe.tensor(pe, [
                        lambda i: nc.tensor.transpose(ps_a[0:C, i % 2, 0:P], hidden[:, i], ident[:]),
                        lambda i: nc.tensor.matmul(ps_b[:, i % 2, 0:P], wq[:], hid_t[:, i % 2], start=True, stop=True),
                        lambda i: nc.tensor.matmul(ps_c[:, i % 2, 0:H * F2], query_t[:, i % 2], keys[:], start=True, stop=True)])

                @block.gpsimd
                def _(pool):
                    for i in range(NT):
                        pool.wait_ge(pipe.brought[-1], i + 1)
                        pool.indirect_dma_start(g["spread2_d"], bass.IndirectOffsetOnAxis(ap=g["start_idx"]["dst"][:, i:i + 1], axis=0),
                                                rows[:, i], None, bounds_check=EP - 1, oob_is_err=False).then_inc(spread, 16)
                    pool.wait_ge(saved, 32)
                    pool.indirect_dma_start(head[:], None, g["table2_d"],
                                            bass.IndirectOffsetOnAxis(ap=g["head_key"]["dst"][:], axis=0)).then_inc(fetched, 16)
                    pool.wait_ge(spread, 16 * NT)
                    pool.wait_ge(fetched, 16)

        T, NC, W = T2, L // T2, H * F2
        with ExitStack() as stack:
            s = Space(nc, stack)
            spread = s.sb("l2_spread", [P, 2, T, B2])
            rows = s.sb("l2_rows", [P, UNROLL, T, F2])
            idx = s.sb("l2_idx", [P, UNROLL, T], I32)
            hold_keep = s.sb("l2_hold_keep", [P, 2, W, T + 1])
            hold = s.sb("l2_hold", [P, 2, H, F2, T + 1])
            prod = s.sb("l2_prod", [P, H, F2, T])
            score = s.sb("l2_score", [P, H, T + 1])
            soft = Softmax(s, "l2s", T, F2)
            outb = s.sb("l2_out", [P, 2, T, W + H])
            two = lambda n: [sem(f"l2_{n}{b}") for b in range(2)]
            four = lambda n: [sem(f"l2_{n}{b}") for b in range(UNROLL)]
            spread_in, spread_used, keep_ready = two("spread_in"), two("spread_used"), two("keep_ready")
            loaded, idx_in, got, used = four("loaded"), four("idx_in"), four("got"), four("used")
            soft.semaphores(two)
            set_up = sem("l2_set_up")
            with nc.Block() as block:
                @block.sync
                def _(sp):
                    spread_v, attr_v, src_v = g["run_of"](g["spread2_d"], B2), g["e"]["attr32"].rearrange("(p l) w -> p l w", p=P), g["run_of"](g["e"]["src"], 1)
                    for c in chunks(sp, NC):
                        wait(sp, used[c.r], c.g + 1)
                        sp.dma_start(idx[:, c.r], src_v[:, bass.ds(c.at * T, T)]).then_inc(idx_in[c.r], 16)
                        sp.dma_start(rows[:, c.r, :, C:C + D32], attr_v[:, bass.ds(c.at * T, T)]).then_inc(loaded[c.r], 16)
                        wait(sp, spread_used[c.b], c.h + 1)
                        sp.dma_start(spread[:, c.b].rearrange("p t w -> p (t w)"), spread_v[:, bass.ds(c.at * (T * B2), T * B2)]).then_inc(spread_in[c.b], 16)

                @block.gpsimd
                def _(pool):
                    for c in chunks(pool, NC):
                        wait(pool, idx_in[c.r], (c.g + 1) * 16)
                        for t in range(T):
                            pool.indirect_dma_start(rows[:, c.r, t, 0:C], None, g["h2_d"],
                                                    bass.IndirectOffsetOnAxis(ap=idx[:, c.r, t:t + 1], axis=0)).then_inc(got[c.r], 16)

                @block.scalar
                def _(act):
                    act.wait_ge(set_up, 1)

                    def keep(c):
                        wait(act, spread_in[c.b], (c.h + 1) * 16)
                        nc.scalar.copy(hold[:, c.b].rearrange("p h f t -> p (h f) t")[:, :, 1:], spread[:, c.b, :, 0:W].rearrange("p t w -> p w t"))
                        nc.scalar.activation(hold_keep[:, c.b, :, 1:], spread[:, c.b, :, W].unsqueeze(1).to_broadcast([P, W, T]),
                                             ACT.Copy, bias=1.0, scale=-1.0).then_inc(keep_ready[c.b], 1)
                    soft.scalar_program(nc, act, NC, outb, g["run_of"](g["sums2_d"], W + H), keep)

                @block.vector
                def _(v):
                    v.memset(hold_keep[:], 0.0)
                    v.memset(rows[:, :, :, F2 - 1:F2], 1.0)
                    v.tensor_copy(hold[:, 1].rearrange("p h f t -> p (h f) t")[:, :, T], head[:, 0:W])
                    soft.start(v)
                    for b in range(2):
                        v.sem_inc(spread_used[b], 1)
                    for r in range(UNROLL):
                        v.sem_inc(used[r], 1)
                    v.drain().then_inc(set_up, 1)

                    def scores(c):
                        b = c.b
                        start = spread[:, b, :, W].unsqueeze(1).to_broadcast([P, H, T])
                        wait(v, spread_in[b], (c.h + 1) * 16)
                        v.tensor_copy(hold[:, b, :, :, 0:1], hold[:, 1 - b, :, :, T:T + 1])
                        wait(v, keep_ready[b], c.h + 1)
                        v.drain()
                        held = hold[:, b].rearrange("p h f t -> p (h f t)")
                        v.tensor_tensor_scan(held, hold_keep[:, b].rearrange("p w t -> p (w t)"), held, 0.0, ALU.mult, ALU.add)
                        wait(v, loaded[c.r], (c.g + 1) * 16)
                        wait(v, got[c.r], (c.g + 1) * (16 * T))
                        v.drain()
                        for h in range(H):
                            v.tensor_tensor(prod[:, h], hold[:, b, h, :, 1:], rows[:, c.r].rearrange("p t f -> p f t"), ALU.mult)
                        v.drain()
                        v.tensor_reduce(score[:, :, 1:], prod[:].rearrange("p h f t -> p h t f"), AX, ALU.add)
                        soft.running_max(v, c, score, start)
                        v.drain().then_inc(spread_used[b], 1)

                    def sums(c):
                        soft.sums(v, c, rows[:, c.r].rearrange("p t f -> p f t")).then_inc(used[c.r], 1)
                        soft.scan(v, c)

                    soft.vector_program(v, NC, scores, sums)
                    soft.keep_tail(v, tail)

        summed = collect_softmax(nc, sem, g, outer, "l2", "dst", g["sums2_d"], tail, F2)
        with ExitStack() as stack:
            s = Space(nc, stack)
            vals, wp = s.sb("l2_vals", [F2, H, C]), s.sb("l2_wp", [C, H, C])
            w1, w2, b1 = s.sb("l2_w1", [C, C]), s.sb("l2_w2", [C, C]), s.sb("l2_b1", [C, 1])
            bp, b2 = s.sb("l2_bp", [P, C]), s.sb("l2_b2", [P, C])
            gain, shift = s.sb("l2_gain2", [P, C]), s.sb("l2_shift2", [P, C])
            recip = s.sb("l2_recip", [P, NT, H])
            res, acc, hidden = s.sb("l2_res", [P, NT, C]), s.sb("l2_acc", [P, NT, C]), s.sb("l2_hidden2", [P, NT, C])
            stat = s.sb("l2_stat2", [P, 3, NT])
            sum_t, mean_t = s.sb("l2_sum_t", [F2, 2, H, P]), s.sb("l2_mean_t", [C, 2, H, P])
            ps_a, ps_b, ps_c = s.ps("l2_psd", [P, 2, 512]), s.ps("l2_pse", [P, 2, 512]), s.ps("l2_psf", [P, 2, 512])
            loaded, scaled, ready = (sem(f"l2c_{n}") for n in ("loaded", "scaled", "ready"))
            sems = sem("l2c_centred"), sem("l2c_rooted")
            pipe, mlp = Pipeline(sem, "l2c", 3), Pipeline(sem, "l2m", 3)
            loads = [(vals, a["values2"]), (wp, a["wp"]), (w1, a["w1"]), (w2, a["w2"]), (b1, a["b1"])] + [
                (t, a[k].to_broadcast([P, C])) for t, k in ((bp, "bp"), (b2, "b2"), (gain, "ln2_g"), (shift, "ln2_b"))]
            with nc.Block() as block:
                @block.sync
                def _(sp):
                    for t, of in loads:
                        sp.dma_start(t[:], of).then_inc(loaded, 16)

                @block.vector
                def _(v):
                    den = summed[:, :, 0:H * F2].rearrange("p t (h f) -> p t h f", h=H)[:, :, :, F2 - 1]
                    v.tensor_scalar(recip[:], den, 1e-8, None, ALU.add)
                    v.drain()
                    v.reciprocal(recip[:], recip[:])
                    v.drain()
                    for h in range(H):
                        part = summed[:, :, h * F2:(h + 1) * F2]
                        v.tensor_tensor(part, part, recip[:, :, h].unsqueeze(2).to_broadcast([P, NT, F2]), ALU.mult)
                    v.drain().then_inc(scaled, 1)
                    v.wait_ge(loaded, 16 * len(loads))
                    v.tensor_tensor(res[:], x[:], bp[:].unsqueeze(1).to_broadcast([P, NT, C]), ALU.add)
                    v.drain()
                    pipe.vector(v, lambda i: v.tensor_tensor(res[:, i], res[:, i], ps_c[:, i % 2, 0:C], ALU.add))
                    v.drain()
                    v.tensor_copy(acc[:], res[:])
                    v.drain()
                    normalise(nc, v, None, acc[:], hidden[:], hidden[:], stat, sems, 1, gain, shift)
                    v.tensor_tensor(acc[:], x[:], res[:], ALU.add)
                    v.drain()
                    v.tensor_tensor(acc[:], acc[:], b2[:].unsqueeze(1).to_broadcast([P, NT, C]), ALU.add)
                    v.drain().then_inc(ready, 1)
                    mlp.vector(v, lambda i: v.tensor_tensor(acc[:, i], acc[:, i], ps_c[:, i % 2, C:2 * C], ALU.add))
                    v.drain()
                    normalise(nc, v, None, acc[:], x[:], res[:], stat, sems, 2)

                @block.scalar
                def _(act):
                    act.wait_ge(loaded, 16 * len(loads))
                    pipe.scalar(act, [
                        lambda i: nc.scalar.copy(sum_t[:, i % 2].rearrange("f h e -> f (h e)"), ps_a[0:F2, i % 2, 0:H * P]),
                        lambda i: nc.scalar.copy(mean_t[:, i % 2].rearrange("f h e -> f (h e)"), ps_b[0:C, i % 2, 0:H * P])])
                    normalise(nc, None, act, None, None, None, stat, sems, 1)
                    mlp.scalar(act, [
                        lambda i: nc.scalar.copy(mean_t[:, i % 2, 0], ps_a[0:C, i % 2, 256:256 + P]),
                        lambda i: nc.scalar.activation(mean_t[:, i % 2, 1], ps_b[0:C, i % 2, 256:256 + P], ACT.Gelu, bias=b1[:, 0:1])])
                    normalise(nc, None, act, None, None, None, stat, sems, 2)

                @block.tensor
                def _(pe):
                    def turn(i):
                        for h in range(H):
                            last = nc.tensor.transpose(ps_a[0:F2, i % 2, h * P:(h + 1) * P], summed[:, i, h * F2:(h + 1) * F2], ident[:])
                        return last

                    def means(i):
                        for h in range(H):
                            last = nc.tensor.matmul(ps_b[0:C, i % 2, h * P:(h + 1) * P], vals[:, h], sum_t[:, i % 2, h], start=True, stop=True)
                        return last

                    def project(i):
                        for h in range(H):
                            last = nc.tensor.matmul(ps_c[:, i % 2, 0:C], mean_t[:, i % 2, h], wp[:, h], start=(h == 0), stop=(h == H - 1))
                        return last
                    pe.wait_ge(loaded, 16 * len(loads))
                    pe.wait_ge(scaled, 1)
                    pipe.tensor(pe, [turn, means, project])
                    pe.wait_ge(ready, 1)
                    mlp.tensor(pe, [
                        lambda i: nc.tensor.transpose(ps_a[0:C, i % 2, 256:256 + P], hidden[:, i], ident[:]),
                        lambda i: nc.tensor.matmul(ps_b[0:C, i % 2, 256:256 + P], w1[:], mean_t[:, i % 2, 0], start=True, stop=True),
                        lambda i: nc.tensor.matmul(ps_c[:, i % 2, C:2 * C], mean_t[:, i % 2, 1], w2[:], start=True, stop=True)])


def layer3(nc, a, sem, g, out):
    x = g["x"]
    ident = g["identity"]
    T, NC = T2, L // T2
    with ExitStack() as outer:
        s0 = Space(nc, outer)
        tail = s0.sb("l3_tail", [P, C])
        rooted_x = s0.sb("l3_rooted_x", [P, NT, C])
        with ExitStack() as stack:
            s = Space(nc, stack)
            spline, root = s.sb("l3_spline", [C, S3 * C]), s.sb("l3_root", [C, C])
            x_t = s.sb("l3_x_t", [C, 2, P])
            row = s.sb("l3_row", [P, 2, S3 * C])
            ps_a, ps_b, ps_c = s.ps("l3_psa", [P, 2, 512]), s.ps("l3_psb", [P, 2, 512]), s.ps("l3_psc", [P, 2, 512])
            loaded, made, brought, tabled, copied, read, differenced = (sem(f"l3a_{n}") for n in (
                "loaded", "made", "brought", "tabled", "copied", "read", "differenced"))
            stored = [sem(f"l3a_stored{b}") for b in range(2)]
            with nc.Block() as block:
                @block.sync
                def _(sp):
                    sp.dma_start(spline[:], a["spline"]).then_inc(loaded, 16)
                    sp.dma_start(root[:], a["root"]).then_inc(loaded, 16)
                    for i in range(NT):
                        sp.wait_ge(copied, i + 1)
                        sp.dma_start(g["table3_d"][i * P:(i + 1) * P], row[:, i % 2]).then_inc(stored[i % 2], 16)
                    sp.wait_ge(stored[0], 16 * ((NT + 1) // 2))
                    sp.wait_ge(stored[1], 16 * (NT // 2))

                @block.tensor
                def _(pe):
                    pe.wait_ge(loaded, 32)
                    pe.wait_ge(differenced, 1)

                    def turn(i):
                        if i >= 2:
                            pe.wait_ge(brought, i - 1)
                        nc.tensor.transpose(ps_a[0:C, i % 2, 0:P], x[:, i], ident[:]).then_inc(made, 1)
                    turn(0)
                    for i in range(NT):
                        if i + 1 < NT:
                            turn(i + 1)
                        pe.wait_ge(brought, i + 1)
                        if i >= 2:
                            pe.wait_ge(copied, i - 1)
                            pe.wait_ge(read, i - 1)
                        nc.tensor.matmul(ps_b[:, i % 2], x_t[:, i % 2], spline[:], start=True, stop=True)
                        nc.tensor.matmul(ps_c[:, i % 2, 0:C], x_t[:, i % 2], root[:], start=True, stop=True).then_inc(tabled, 1)

                @block.scalar
                def _(act):
                    for i in range(NT):
                        act.wait_ge(made, i + 1)
                        if i >= 2:
                            act.wait_ge(tabled, i - 1)
                        nc.scalar.copy(x_t[:, i % 2], ps_a[0:C, i % 2, 0:P]).then_inc(brought, 1)
                        if i >= 1:
                            act.wait_ge(tabled, i)
                            nc.scalar.copy(rooted_x[:, i - 1], ps_c[:, (i - 1) % 2, 0:C]).then_inc(read, 1)
                    act.wait_ge(tabled, NT)
                    nc.scalar.copy(rooted_x[:, NT - 1], ps_c[:, (NT - 1) % 2, 0:C]).then_inc(read, 1)

                @block.vector
                def _(v):
                    v.wait_ge(loaded, 32)
                    for d in range(D3):
                        by_bit = spline[:].rearrange("c (low bit high f) -> c low bit (high f)", low=2 ** d, bit=2, f=C)
                        v.tensor_tensor(by_bit[:, :, 1], by_bit[:, :, 1], by_bit[:, :, 0], ALU.subtract)
                        v.drain()
                    v.sem_inc(differenced, 1)
                    for i in range(NT):
                        v.wait_ge(tabled, i + 1)
                        if i >= 2:
                            v.wait_ge(stored[i % 2], 16 * (i // 2))
                        v.tensor_copy(row[:, i % 2], ps_b[:, i % 2]).then_inc(copied, 1)

        with ExitStack() as stack:
            s = Space(nc, stack)
            idx = s.sb("l3_idx", [P, 2, T], I32)
            rows = s.sb("l3_rows", [P, 2, T, S3 * C])
            data = s.sb("l3_data", [P, C, T + 1])
            keep = s.sb("l3_keep", [P, 2, C, T + 1])
            run = s.sb("l3_run", [P, 2, C, T + 1])
            outb = s.sb("l3_out", [P, 2, T, C])
            frac = s.sb("l3_frac", [P, L * D3])
            half = s.sb("l3_half", [P, T, S3 // 2 * C])
            quarter = s.sb("l3_quarter", [P, T, S3 // 4 * C])
            keys, prev, same = s.sb("l3_keys", [P, L], I32), s.sb("l3_prev", [P, L], I32), s.sb("l3_same", [P, L])
            two = lambda n: [sem(f"l3_{n}{b}") for b in range(2)]
            idx_in, got, rows_used, keep_ready, scanned, copied, stored = (two(n) for n in (
                "idx_in", "got", "rows_used", "keep_ready", "scanned", "copied", "stored"))
            loaded, flags = sem("l3_loaded"), sem("l3_flags")
            with nc.Block() as block:
                @block.sync
                def _(sp):
                    sp.dma_start(frac[:], g["run_of"](g["e"]["attr3"], D3)).then_inc(loaded, 16)
                    sp.dma_start(keys[:], g["run_of"](g["e"]["dst"], 1)).then_inc(loaded, 16)
                    sp.dma_start(prev[:], g["run_of"](g["e"]["dst_before"], 1)).then_inc(loaded, 16)
                    src = g["run_of"](g["e"]["src"], 1)
                    with sp.Fori(0, NC // 2) as h:
                        for b in range(2):
                            wait(sp, rows_used[b], h + 1)
                            sp.dma_start(idx[:, b], src[:, bass.ds((h * 2 + b) * T, T)]).then_inc(idx_in[b], 16)

                @block.gpsimd
                def _(pool):
                    with pool.Fori(0, NC // 2) as h:
                        for b in range(2):
                            wait(pool, idx_in[b], (h + 1) * 16)
                            for t in range(T):
                                pool.indirect_dma_start(rows[:, b, t], None, g["table3_d"],
                                                        bass.IndirectOffsetOnAxis(ap=idx[:, b, t:t + 1], axis=0)) \
                                    .then_inc(got[b], 16)

                @block.vector
                def _(v):
                    v.memset(run[:], 0.0)
                    v.memset(keep[:], 0.0)
                    v.sem_inc(rows_used[0], 1)
                    v.sem_inc(rows_used[1], 1)
                    v.wait_ge(loaded, 48)
                    v.tensor_tensor(same[:], keys[:], prev[:], ALU.is_equal)
                    v.tensor_scalar(frac[:], frac[:], 0.0, 1.0, ALU.max, ALU.min)
                    v.drain().then_inc(flags, 1)
                    with v.Fori(0, NC // 2) as h:
                        for b in range(2):
                            c = h * 2 + b
                            up = frac[:, bass.ds(c * (T * D3), T * D3)].rearrange("p (t d) -> p t d", d=D3)
                            wait(v, got[b], (h + 1) * (16 * T))
                            for n, (low, high) in enumerate(((rows[:, b], half), (half, quarter))):
                                w = high.shape[-1]
                                for k in range(T):
                                    v.scalar_tensor_tensor(out=high[:, k], in0=low[:, k, w:2 * w], scalar=up[:, k, n:n + 1],
                                                           in1=low[:, k, 0:w], op0=ALU.mult, op1=ALU.add)
                                if n == 0:
                                    v.drain().then_inc(rows_used[b], 1)
                                else:
                                    v.drain()
                            v.tensor_tensor(quarter[:, :, C:], quarter[:, :, C:], up[:, :, 2].unsqueeze(2).to_broadcast([P, T, C]), ALU.mult)
                            v.drain()
                            v.tensor_tensor(data[:, :, 1:], quarter[:, :, 0:C].rearrange("p t f -> p f t"),
                                            quarter[:, :, C:].rearrange("p t f -> p f t"), ALU.add)
                            v.tensor_copy(data[:, :, 0:1], run[:, 1 - b, :, T:T + 1])
                            wait(v, keep_ready[b], h + 1)
                            wait(v, copied[b], h + 1)
                            v.drain()
                            v.tensor_tensor_scan(run[:, b].rearrange("p f t -> p (f t)"),
                                                 keep[:, b].rearrange("p f t -> p (f t)"),
                                                 data[:].rearrange("p f t -> p (f t)"), 0.0, ALU.mult, ALU.add) \
                             .then_inc(scanned[b], 1)
                            v.drain()
                    v.tensor_copy(tail[:], run[:, 1, :, T])

                @block.scalar
                def _(act):
                    act.wait_ge(flags, 1)
                    for b in range(2):
                        act.sem_inc(copied[b], 1)
                        act.sem_inc(stored[b], 16)
                        act.sem_inc(scanned[b], 1)
                    with act.Fori(0, NC // 2) as h:
                        for b in range(2):
                            wait(act, scanned[b], h + 1)
                            at = bass.ds((h * 2 + b) * T, T)
                            nc.scalar.copy(keep[:, b, :, 1:], same[:, at].unsqueeze(1).to_broadcast([P, C, T])) \
                              .then_inc(keep_ready[b], 1)
                            wait(act, scanned[b], h + 2)
                            wait(act, stored[b], (h + 1) * 16)
                            nc.scalar.copy(outb[:, b], run[:, b, :, 1:].rearrange("p f t -> p t f")).then_inc(copied[b], 1)
                            wait(act, copied[b], h + 2)
                            act.dma_start(g["run_of"](g["sums3_d"], C)[:, bass.ds((h * 2 + b) * (T * C), T * C)],
                                          outb[:, b].rearrange("p t f -> p (t f)")).then_inc(stored[b], 16)
                    for b in range(2):
                        act.wait_ge(stored[b], 16 * (NC // 2 + 1))

        total = collect_sums(nc, sem, g, outer, "l3", g["sums3_d"], tail)
        with ExitStack() as stack:
            s = Space(nc, stack)
            valid = s.sb("l3_valid", [P, NT])
            part = s.sb("l3_part", [P, C])
            moment = s.sb("l3_moment", [P, 2, C])
            deviation = s.sb("l3_deviation", [P, C])
            gamma, beta = s.sb("l3_gamma", [P, C]), s.sb("l3_beta", [P, C])
            ones = s.sb("l3_ones", [P, P])
            recip = s.sb("l3_recip", [P, NT])
            work, work2, stat = s.sb("l3_work", [P, NT, C]), s.sb("l3_work2", [P, NT, C]), s.sb("l3_stat", [P, 3, NT])
            summed = s.ps("l3_summed", [P, 2, 512])
            loaded, parted, added, ready, rooted_, low, high, done, finished = (sem(f"l3c_{n}") for n in (
                "loaded", "parted", "added", "ready", "rooted", "low", "high", "done", "finished"))
            sems = sem("l3c_centred"), sem("l3c_rooted_")
            with nc.Block() as block:
                @block.sync
                def _(sp):
                    sp.dma_start(gamma[:], a["gamma"].to_broadcast([P, C])).then_inc(loaded, 16)
                    sp.dma_start(beta[:], a["beta"].to_broadcast([P, C])).then_inc(loaded, 16)
                    sp.wait_ge(finished, 1)
                    sp.dma_start(out[0:NP - P].rearrange("(t p) c -> p t c", p=P), x[:, 0:NT - 1]).then_inc(done, 16)
                    sp.dma_start(out[NP - P:N], x[0:N - (NP - P), NT - 1]).then_inc(done, 16)
                    sp.wait_ge(done, 32)

                @block.tensor
                def _(pe):
                    for n in range(2):
                        pe.wait_ge(parted, n + 1)
                        nc.tensor.matmul(summed[:, n, 0:C], ones[:], part[:], start=True, stop=True).then_inc(added, 1)

                @block.vector
                def _(v):
                    over_tiles = lambda t: t[:].unsqueeze(1).to_broadcast([P, NT, C])
                    over_features = lambda t: t.unsqueeze(2).to_broadcast([P, NT, C])
                    v.memset(ones[:], 1.0)
                    v.memset(valid[:], 1.0)
                    v.tensor_scalar(recip[:], g["degree"][:], 1.0, None, ALU.max)
                    v.drain()
                    v.tensor_scalar(valid[:, NT - 1:NT], g["run_end"][:], float((N - (NP - P)) * L), None, ALU.is_le)
                    v.reciprocal(recip[:], recip[:])
                    v.drain()
                    v.tensor_tensor(total[:], total[:], over_features(recip[:]), ALU.mult)
                    v.drain()
                    v.tensor_tensor(total[:], total[:], rooted_x[:], ALU.add)
                    v.drain()
                    for n in range(2):
                        if n:
                            v.tensor_tensor(work[:], total[:], total[:], ALU.mult)
                            v.drain()
                        v.tensor_tensor(work[:], work[:] if n else total[:], over_features(valid[:]), ALU.mult)
                        v.drain()
                        v.tensor_reduce(part[:], work[:].rearrange("p t c -> p c t"), AX, ALU.add)
                        v.drain().then_inc(parted, 1)
                        v.wait_ge(added, n + 1)
                        v.tensor_scalar(moment[:, n], summed[:, n, 0:C], 1.0 / N, LN_EPS * n, ALU.mult, ALU.add)
                        v.drain()
                        if n == 0:
                            v.tensor_tensor(total[:], total[:], moment[:, 0].unsqueeze(1).to_broadcast([P, NT, C]), ALU.subtract)
                            v.drain()
                    v.drain().then_inc(ready, 1)
                    v.wait_ge(rooted_, 1)
                    v.reciprocal(deviation[:], deviation[:])
                    v.wait_ge(loaded, 32)
                    v.drain()
                    v.tensor_tensor(deviation[:], deviation[:], gamma[:], ALU.mult)
                    v.drain()
                    v.tensor_tensor(total[:], total[:], over_tiles(deviation), ALU.mult)
                    v.drain()
                    v.tensor_tensor(total[:], total[:], over_tiles(beta), ALU.add)
                    v.drain()
                    v.tensor_scalar(work[:], total[:], 0.0, None, ALU.min)
                    v.drain().then_inc(low, 1)
                    v.tensor_scalar(total[:], total[:], 0.0, -1.0, ALU.max, ALU.add)
                    v.drain()
                    v.tensor_tensor(total[:], total[:], x[:], ALU.add)
                    v.wait_ge(high, 1)
                    v.drain()
                    v.tensor_tensor(total[:], total[:], work2[:], ALU.add)
                    v.drain()
                    normalise(nc, v, None, total[:], x[:], work[:], stat, sems, 1)
                    v.drain().then_inc(finished, 1)

                @block.scalar
                def _(act):
                    act.wait_ge(ready, 1)
                    nc.scalar.activation(deviation[:], moment[:, 1], ACT.Sqrt).then_inc(rooted_, 1)
                    act.wait_ge(low, 1)
                    nc.scalar.activation(work2[:], work[:], ACT.Exp).then_inc(high, 1)
                    normalise(nc, None, act, None, None, None, stat, sems, 1)


def laid_out(inputs):
    n = {k: np.asarray(v) for k, v in inputs.items()}

    def padded(t, rows, fill=0):
        t = np.asarray(t)
        more = np.full((rows - t.shape[0],) + t.shape[1:], fill, t.dtype)
        return np.ascontiguousarray(np.concatenate([t, more]))

    arrays = {"x": padded(n["x"], NP), "edge_weight": padded(n["edge_weight"], EP).reshape(EP, 1)}
    for k in ("src", "dst"):
        arrays[k] = padded(n[k], EP, N).reshape(EP, 1)
    arrays["dst_before"] = np.concatenate([np.full((1, 1), -1, n["dst"].dtype), arrays["dst"][:-1]])
    arrays["attr3"] = padded(n["edge_attr_3"], EP)
    arrays["attr5"] = padded(n["edge_attr_5"], EP)
    arrays["attr32"] = padded(n["edge_attr_32"], EP)
    lin, edge = n["L1_gnn_W_lin"].reshape(C, H, C), n["L1_gnn_W_edge"].reshape(D5, H, C)
    b_lin, b_edge = n["L1_gnn_b_lin"].reshape(1, H, C), n["L1_gnn_b_edge"].reshape(1, H, C)
    arrays["att1"] = n["L1_gnn_att"].reshape(H, 2, C).transpose(2, 1, 0).reshape(C, 2 * H)
    arrays["proj1"] = np.concatenate([lin, b_lin, edge, b_edge]).transpose(2, 1, 0)
    arrays["out1"] = np.concatenate([lin, edge, b_lin])
    arrays["out1_bias"] = b_edge
    arrays["bias1"] = n["L1_gnn_bias"].reshape(1, C)
    wk, wv, we = (n[f"L2_gnn_{k}"].reshape(-1, H, C) for k in ("Wk", "Wv", "We"))
    bk, bv = n["L2_gnn_bk"].reshape(1, H, C), n["L2_gnn_bv"].reshape(1, H, C)
    arrays["wq"] = n["L2_gnn_Wq"]
    arrays["bq"] = n["L2_gnn_bq"].reshape(H * C, 1)
    keys = np.zeros((H, C, H, F2), n["L2_gnn_Wk"].dtype)
    for h in range(H):
        keys[h, :, h] = np.concatenate([wk, we, bk])[:, h].T
    arrays["keys2"] = keys.reshape(H * C, H * F2)
    arrays["values2"] = np.concatenate([wv, we, bv])
    arrays["wp"] = n["L2_gnn_Wp"].reshape(H, C, C).transpose(1, 0, 2)
    for k in ("ln1_g", "ln1_b", "ln2_g", "ln2_b", "bp", "b2"):
        arrays[k] = n[f"L2_gnn_{k}"].reshape(1, C)
    arrays["w1"], arrays["w2"] = n["L2_gnn_W1"], n["L2_gnn_W2"]
    arrays["b1"] = n["L2_gnn_b1"].reshape(C, 1)
    arrays["spline"] = n["L3_gnn_W"].reshape(2, 2, 2, C, C).transpose(3, 2, 1, 0, 4).reshape(C, S3 * C)
    arrays["root"] = n["L3_gnn_root"]
    arrays["gamma"], arrays["beta"] = n["L3_gnn_gamma"].reshape(1, C), n["L3_gnn_beta"].reshape(1, C)
    return {f"in_{k}": np.ascontiguousarray(v) for k, v in arrays.items()}


def kernel(**inputs):
    import concourse.bacc as bacc
    from concourse.bass_utils import run_bass_kernel_spmd

    arrays = laid_out(inputs)
    nc = bacc.Bacc("TRN2", target_bir_lowering=False, num_devices=1)
    a = {k[3:]: nc.dram_tensor(k, v.shape, mybir.dt.from_np(v.dtype), kind="ExternalInput").ap()
         for k, v in arrays.items()}
    out = nc.dram_tensor("out_0_dram", (N, C), F32, kind="ExternalOutput").ap()
    build(nc, a, out)
    r = run_bass_kernel_spmd(nc, [arrays], core_ids=[0])
    return r.results[0]["out_0_dram"]
```
